# Optimizing a Trainium2 kernel written in Bass

```python
import numpy as np
import jax
import jax.numpy as jnp

def _softmax(x, axis=-1):
    return jax.nn.softmax(x, axis=axis)

def _gelu(x):
    return jax.nn.gelu(x, approximate=True)

def _silu(x):
    return jax.nn.silu(x)

def _sigmoid(x):
    return jax.nn.sigmoid(x)

def _layernorm(x, axis=-1, eps=1e-05):
    m = jnp.mean(x, axis=axis, keepdims=True)
    v = jnp.var(x, axis=axis, keepdims=True)
    return (x - m) / jnp.sqrt(v + eps)

def _scatter_add(tgt, idx, src, axis=0):
    return tgt.at[idx].add(src)

def _segment_sum(src, seg, n):
    return jax.ops.segment_sum(src, seg, n)
kernel_name = 'mk_seq_preln_d2_jaxref_r8_b8ec2c'

def setup_inputs(seed: int=0):
    np.random.seed(seed)
    _w = jnp.asarray

    def _L0_attn_setup():
        import jax, jax.numpy as jnp
        import numpy as np
        import math
        D_MODEL, N_HEADS, D_K, D_C, D_HR = (128, 8, 128, 32, 32)
        B, S = (4, 256)
        key = jax.random.key(seed)
        ks = jax.random.split(key, 17)

        def lin(k, fan_in, fan_out):
            lim = 1.0 / math.sqrt(fan_in)
            kw, kb = jax.random.split(k)
            W = jax.random.uniform(kw, (fan_in, fan_out), jnp.float32, -lim, lim)
            b = jax.random.uniform(kb, (fan_out,), jnp.float32, -lim, lim)
            return (W, b)
        W_DQ, b_DQ = lin(ks[0], D_MODEL, D_C)
        W_UQ, b_UQ = lin(ks[1], D_C, N_HEADS * D_K)
        W_DKV, b_DKV = lin(ks[2], D_MODEL, D_C)
        W_UK, b_UK = lin(ks[3], D_C, N_HEADS * D_K)
        W_UV, b_UV = lin(ks[4], D_C, N_HEADS * D_K)
        W_QR, b_QR = lin(ks[5], D_C, N_HEADS * D_HR)
        W_KR, b_KR = lin(ks[6], D_MODEL, D_HR)
        W_O, b_O = lin(ks[7], N_HEADS * D_K, D_MODEL)
        h_t = jax.random.normal(ks[8], (B, S, D_MODEL), jnp.float32)
        return {'h_t': h_t, 'W_DQ': W_DQ, 'b_DQ': b_DQ, 'W_UQ': W_UQ, 'b_UQ': b_UQ, 'W_DKV': W_DKV, 'b_DKV': b_DKV, 'W_UK': W_UK, 'b_UK': b_UK, 'W_UV': W_UV, 'b_UV': b_UV, 'W_QR': W_QR, 'b_QR': b_QR, 'W_KR': W_KR, 'b_KR': b_KR, 'W_O': W_O, 'b_O': b_O}
    _L0_attn_in = _L0_attn_setup()

    def _L0_ffn_setup():
        import jax, jax.numpy as jnp
        import numpy as np
        E, D, F = (8, 128, 512)
        B, S = (4, 256)

        def _layernorm(x, g, b, eps=1e-05):
            mu = jnp.mean(x, axis=-1, keepdims=True)
            var = jnp.var(x, axis=-1, keepdims=True)
            return (x - mu) * jax.lax.rsqrt(var + eps) * g + b
        key = jax.random.key(seed)
        ks = jax.random.split(key, 5)
        return {'input_features': jax.random.normal(ks[0], (B, S, D), jnp.float32), 'centroids': jax.random.normal(ks[1], (E, D), jnp.float32) * 0.1, 'ln_g': jnp.ones((E, D), jnp.float32), 'ln_b': jnp.zeros((E, D), jnp.float32), 'w1': jax.random.normal(ks[2], (E, F, D), jnp.float32) * (1.0 / np.sqrt(D).astype(np.float32)), 'b1': jnp.zeros((E, F), jnp.float32), 'w2': jax.random.normal(ks[3], (E, D, F), jnp.float32) * (1.0 / np.sqrt(F).astype(np.float32)), 'b2': jnp.zeros((E, D), jnp.float32)}
    _L0_ffn_in = _L0_ffn_setup()

    def _L1_attn_setup():
        import jax, jax.numpy as jnp
        import numpy as np
        B, T, C, H = (2, 128, 128, 16)
        D = C // H
        EPS = 1e-06
        key = jax.random.key(seed)
        k1, k2, k3, k4, k5 = jax.random.split(key, 5)
        s = 0.02
        return {'x': jax.random.normal(k1, (B, T, C), dtype=jnp.float32), 'w_qkv': jax.random.normal(k2, (3 * C, C), dtype=jnp.float32) * s, 'b_qkv': jax.random.normal(k3, (3 * C,), dtype=jnp.float32) * s, 'w_out': jax.random.normal(k4, (C, C), dtype=jnp.float32) * s, 'b_out': jax.random.normal(k5, (C,), dtype=jnp.float32) * s}
    _L1_attn_in = _L1_attn_setup()

    def _L1_ffn_setup():
        import jax, jax.numpy as jnp
        import numpy as np
        D_MODEL, D_FF, N_EXPERTS, TOP_K = (128, 512, 8, 2)
        key = jax.random.key(seed)
        k1, k2, k3, k4 = jax.random.split(key, 4)
        x = jax.random.normal(k1, (2, 256, D_MODEL), dtype=jnp.float32)
        Wg = jax.random.normal(k2, (D_MODEL, N_EXPERTS), dtype=jnp.float32) * 0.02
        W1 = jax.random.normal(k3, (N_EXPERTS, D_MODEL, D_FF), dtype=jnp.float32) * 0.02
        b1 = jnp.zeros((N_EXPERTS, D_FF), dtype=jnp.float32)
        W2 = jax.random.normal(k4, (N_EXPERTS, D_FF, D_MODEL), dtype=jnp.float32) * 0.02
        b2 = jnp.zeros((N_EXPERTS, D_MODEL), dtype=jnp.float32)
        return {'x': x, 'Wg': Wg, 'W1': W1, 'b1': b1, 'W2': W2, 'b2': b2}
    _L1_ffn_in = _L1_ffn_setup()
    _d = {'L0_attn_h_t': _L0_attn_in['h_t'], 'L0_attn_W_DQ': _L0_attn_in['W_DQ'], 'L0_attn_b_DQ': _L0_attn_in['b_DQ'], 'L0_attn_W_UQ': _L0_attn_in['W_UQ'], 'L0_attn_b_UQ': _L0_attn_in['b_UQ'], 'L0_attn_W_DKV': _L0_attn_in['W_DKV'], 'L0_attn_b_DKV': _L0_attn_in['b_DKV'], 'L0_attn_W_UK': _L0_attn_in['W_UK'], 'L0_attn_b_UK': _L0_attn_in['b_UK'], 'L0_attn_W_UV': _L0_attn_in['W_UV'], 'L0_attn_b_UV': _L0_attn_in['b_UV'], 'L0_attn_W_QR': _L0_attn_in['W_QR'], 'L0_attn_b_QR': _L0_attn_in['b_QR'], 'L0_attn_W_KR': _L0_attn_in['W_KR'], 'L0_attn_b_KR': _L0_attn_in['b_KR'], 'L0_attn_W_O': _L0_attn_in['W_O'], 'L0_attn_b_O': _L0_attn_in['b_O'], 'L0_ffn_centroids': _L0_ffn_in['centroids'], 'L0_ffn_ln_g': _L0_ffn_in['ln_g'], 'L0_ffn_ln_b': _L0_ffn_in['ln_b'], 'L0_ffn_w1': _L0_ffn_in['w1'], 'L0_ffn_b1': _L0_ffn_in['b1'], 'L0_ffn_w2': _L0_ffn_in['w2'], 'L0_ffn_b2': _L0_ffn_in['b2'], 'L1_attn_w_qkv': _L1_attn_in['w_qkv'], 'L1_attn_b_qkv': _L1_attn_in['b_qkv'], 'L1_attn_w_out': _L1_attn_in['w_out'], 'L1_attn_b_out': _L1_attn_in['b_out'], 'L1_ffn_Wg': _L1_ffn_in['Wg'], 'L1_ffn_W1': _L1_ffn_in['W1'], 'L1_ffn_b1': _L1_ffn_in['b1'], 'L1_ffn_W2': _L1_ffn_in['W2'], 'L1_ffn_b2': _L1_ffn_in['b2']}
    _x0 = _d['L0_attn_h_t']
    _d['L0_attn_h_t'] = jax.random.normal(jax.random.fold_in(jax.random.key(seed), 1), (4, 512, 128), dtype=_x0.dtype)
    del _x0
    return _d

def reference(L0_attn_h_t, L0_attn_W_DQ, L0_attn_b_DQ, L0_attn_W_UQ, L0_attn_b_UQ, L0_attn_W_DKV, L0_attn_b_DKV, L0_attn_W_UK, L0_attn_b_UK, L0_attn_W_UV, L0_attn_b_UV, L0_attn_W_QR, L0_attn_b_QR, L0_attn_W_KR, L0_attn_b_KR, L0_attn_W_O, L0_attn_b_O, L0_ffn_centroids, L0_ffn_ln_g, L0_ffn_ln_b, L0_ffn_w1, L0_ffn_b1, L0_ffn_w2, L0_ffn_b2, L1_attn_w_qkv, L1_attn_b_qkv, L1_attn_w_out, L1_attn_b_out, L1_ffn_Wg, L1_ffn_W1, L1_ffn_b1, L1_ffn_W2, L1_ffn_b2):

    def _L0_attn_ref(h_t, W_DQ, b_DQ, W_UQ, b_UQ, W_DKV, b_DKV, W_UK, b_UK, W_UV, b_UV, W_QR, b_QR, W_KR, b_KR, W_O, b_O):
        import jax, jax.numpy as jnp
        import numpy as np
        import math
        D_MODEL, N_HEADS, D_K, D_C, D_HR = (128, 8, 128, 32, 32)
        B, S = (4, 256)
        b, s, _ = h_t.shape
        c_q = h_t @ W_DQ + b_DQ
        c_kv = h_t @ W_DKV + b_DKV
        q_c = (c_q @ W_UQ + b_UQ).reshape(b, s, N_HEADS, D_K).transpose(0, 2, 1, 3)
        k_c = (c_kv @ W_UK + b_UK).reshape(b, s, N_HEADS, D_K).transpose(0, 2, 1, 3)
        v_c = (c_kv @ W_UV + b_UV).reshape(b, s, N_HEADS, D_K).transpose(0, 2, 1, 3)
        q_r = (c_q @ W_QR + b_QR).reshape(b, s, N_HEADS, D_HR).transpose(0, 2, 1, 3)
        k_r = (h_t @ W_KR + b_KR)[:, None, :, :]
        k_r = jnp.broadcast_to(k_r, (b, N_HEADS, s, D_HR))
        q = jnp.concatenate([q_c, q_r], axis=-1)
        k = jnp.concatenate([k_c, k_r], axis=-1)
        scale = 1.0 / math.sqrt(D_K + D_HR)
        scores = jnp.einsum('bhsd,bhtd->bhst', q, k) * scale
        attn = jax.nn.softmax(scores, axis=-1)
        o = jnp.einsum('bhst,bhtd->bhsd', attn, v_c)
        o = o.transpose(0, 2, 1, 3).reshape(b, s, N_HEADS * D_K)
        return o @ W_O + b_O

    def _L0_ffn_ref(input_features, centroids, ln_g, ln_b, w1, b1, w2, b2):
        import jax, jax.numpy as jnp
        import numpy as np
        E, D, F = (8, 128, 512)
        B, S = (4, 256)

        def _layernorm(x, g, b, eps=1e-05):
            mu = jnp.mean(x, axis=-1, keepdims=True)
            var = jnp.var(x, axis=-1, keepdims=True)
            return (x - mu) * jax.lax.rsqrt(var + eps) * g + b
        Bf, Sf, Df = input_features.shape
        x = input_features.reshape(-1, Df)
        aff = x @ centroids.T
        assign = jnp.argmax(aff, axis=1)
        order = jnp.argsort(assign)
        xs = x[order]
        es = assign[order]
        alpha = jax.nn.sigmoid(jnp.take_along_axis(aff[order], es[:, None], axis=1))
        nE = centroids.shape[0]
        y = jnp.zeros_like(xs)
        for e in range(nE):
            h = _layernorm(xs, ln_g[e], ln_b[e])
            h = jax.nn.relu(h @ w1[e].T + b1[e])
            ye = xs + h @ w2[e].T + b2[e]
            y = y + jnp.where((es == e)[:, None], ye, 0.0)
        out_sorted = alpha * y + (1.0 - alpha) * xs
        inv = jnp.argsort(order)
        return out_sorted[inv].reshape(Bf, Sf, Df)

    def _L1_attn_ref(x, w_qkv, b_qkv, w_out, b_out):
        import jax, jax.numpy as jnp
        import numpy as np
        B, T, C, H = (2, 128, 128, 16)
        D = C // H
        EPS = 1e-06
        b, t, c = x.shape
        qkv = x @ w_qkv.T + b_qkv
        q, k, v = jnp.split(qkv, 3, axis=-1)

        def to_heads(u):
            return u.reshape(b, t, H, D).transpose(0, 2, 1, 3).astype(jnp.float32)
        q, k, v = (to_heads(q), to_heads(k), to_heads(v))
        q_prime = jax.nn.elu(q) + 1.0
        k_prime = jax.nn.elu(k) + 1.0
        kv_cumsum = jnp.cumsum(jnp.einsum('bhtd,bhte->bhtde', k_prime, v), axis=2)
        context = jnp.einsum('bhtd,bhtde->bhte', q_prime, kv_cumsum)
        norm = jnp.einsum('bhtd,bhtd->bht', q_prime, jnp.cumsum(k_prime, axis=2))
        out = context / (norm[..., None] + EPS)
        out = out.astype(x.dtype).transpose(0, 2, 1, 3).reshape(b, t, c)
        return out @ w_out.T + b_out

    def _L1_ffn_ref(x, Wg, W1, b1, W2, b2):
        import jax, jax.numpy as jnp
        import numpy as np
        D_MODEL, D_FF, N_EXPERTS, TOP_K = (128, 512, 8, 2)
        B, S, D = x.shape
        T = B * S
        flat_x = x.reshape(T, D)
        logits = flat_x @ Wg
        probs = jax.nn.softmax(logits, axis=-1)
        _, top_idx = jax.lax.top_k(probs, TOP_K)
        mask = jax.nn.one_hot(top_idx, N_EXPERTS, dtype=probs.dtype).sum(axis=1)
        weights = probs * mask
        h = jax.nn.gelu(jnp.einsum('td,edh->eth', flat_x, W1) + b1[:, None, :])
        y = jnp.einsum('eth,ehd->etd', h, W2) + b2[:, None, :]
        out = jnp.einsum('etd,te->td', y, weights)
        return out.reshape(B, S, D)
    x = L0_attn_h_t
    x = x + _L0_attn_ref(_layernorm(x, axis=-1), L0_attn_W_DQ, L0_attn_b_DQ, L0_attn_W_UQ, L0_attn_b_UQ, L0_attn_W_DKV, L0_attn_b_DKV, L0_attn_W_UK, L0_attn_b_UK, L0_attn_W_UV, L0_attn_b_UV, L0_attn_W_QR, L0_attn_b_QR, L0_attn_W_KR, L0_attn_b_KR, L0_attn_W_O, L0_attn_b_O)
    x = x + _L0_ffn_ref(_layernorm(x, axis=-1), L0_ffn_centroids, L0_ffn_ln_g, L0_ffn_ln_b, L0_ffn_w1, L0_ffn_b1, L0_ffn_w2, L0_ffn_b2)
    x = x + _L1_attn_ref(_layernorm(x, axis=-1), L1_attn_w_qkv, L1_attn_b_qkv, L1_attn_w_out, L1_attn_b_out)
    x = x + _L1_ffn_ref(_layernorm(x, axis=-1), L1_ffn_Wg, L1_ffn_W1, L1_ffn_b1, L1_ffn_W2, L1_ffn_b2)
    return x

_drawn_inputs = setup_inputs


def setup_inputs(seed=0):
    import zlib

    import numpy as np

    out = dict(_drawn_inputs(seed))
    spreads = {'L0_ffn_ln_g': (1.0, 0.2),
     'L0_ffn_ln_b': (0.0, 0.275),
     'L0_ffn_b1': (0.0, 0.284),
     'L0_ffn_b2': (0.0, 0.1),
     'L1_ffn_b1': (0.0, 0.8),
     'L1_ffn_b2': (0.0, 0.713)}
    factors = {'L0_attn_W_DQ': 3.568,
     'L0_attn_b_DQ': 8.0,
     'L0_attn_W_UQ': 3.989,
     'L0_attn_b_UQ': 3.707,
     'L0_attn_W_UK': 4.484,
     'L0_attn_b_UK': 8.0,
     'L0_attn_W_QR': 3.966,
     'L0_attn_b_QR': 4.452,
     'L0_attn_W_KR': 4.782,
     'L0_attn_b_KR': 8.0,
     'L1_attn_w_qkv': 8.0,
     'L1_attn_b_qkv': 8.0,
     'L1_attn_w_out': 8.0,
     'L1_attn_b_out': 5.757,
     'L1_ffn_Wg': 4.949,
     'L1_ffn_W1': 8.0,
     'L1_ffn_W2': 8.0}
    for name, (base, spread) in spreads.items():
        noise = np.random.default_rng([zlib.crc32(name.encode()), seed]).standard_normal(out[name].shape)
        drawn = base * np.exp(spread * noise) if base else spread * noise
        out[name] = jnp.asarray(drawn.astype(out[name].dtype))
    for name, factor in factors.items():
        out[name] = (out[name] * factor).astype(out[name].dtype)
    return out
```

```python
from contextlib import ExitStack
import math

import numpy as np
import concourse.bass as bass
from concourse import mybir

F32 = mybir.dt.float32
F32R = mybir.dt.float32r
BF16 = mybir.dt.bfloat16
I32 = mybir.dt.int32
U32 = mybir.dt.uint32
ALU = mybir.AluOpType
ACT = mybir.ActivationFunctionType
AX = mybir.AxisListType

P = 128
BATCH, SEQ, D = 4, 512, 128
TOK = BATCH * SEQ
NT = TOK // P
TPB = SEQ // P
HEADS, DK, DC, DR = 8, 128, 32, 32
SCORE_SCALE = 1.0 / math.sqrt(DK + DR)
EPS = 1e-5

ROW_ONE = 3 * DC
ROW_MHI = ROW_ONE + 2
ROW_MLO = ROW_MHI + HEADS
SCORE_K = ROW_MHI
SHIFT_K = ROW_MLO + HEADS
KSIDE = DC + DR + 1
QUAD = 4

LH, LD = 16, 8
LE = LD + 1
LEPS = 1e-6
GRP = 4
GW = GRP * LE * LD

NE, FF = 8, 512
FC = FF // P
REC = D + 2
REGION = TOK + P
PAD_ROW = NE * REGION
SKIP = 1 << 20


def n_blocks(k):
    return (k * TOK) // P + NE - 1


def flat(x):
    if x is None:
        return []
    if isinstance(x, dict):
        return [x]
    return [t for y in x for t in flat(y)]


class Queues:

    def __init__(self, nc, ctx):
        self.nc, self.ctx = nc, ctx
        self.items = {e: [] for e in ("sync", "scalar", "vector", "gpsimd", "tensor")}
        self.done = {e: ctx.enter_context(nc.semaphore(f"done_{e}")) for e in self.items if e != "sync"}
        self.slots = {}

    def put(self, engine, fn, after, token):
        after = flat(after)
        for t in after:
            t["needed"] = True
        self.items[engine].append((fn, after, token))
        return token

    def add(self, engine, fn, after=()):
        return self.put(engine, fn, after, {"dma": False, "needed": False, "sem": None, "value": None})

    def dma(self, engine, slot, fn, after=()):
        if slot not in self.slots:
            self.slots[slot] = [self.ctx.enter_context(self.nc.semaphore(f"dma_{slot}")), 0]
        self.slots[slot][1] += 16
        token = {"dma": True, "needed": True, "sem": self.slots[slot][0], "value": self.slots[slot][1]}
        return self.put(engine, fn, after, token)

    def emit(self, block):
        for engine, items in self.items.items():
            count = 0
            for _, _, t in items:
                if t["needed"] and not t["dma"]:
                    count += 1
                    t["sem"], t["value"] = self.done[engine], count

        def play(engine, items):
            def body(eng):
                seen = {}
                for fn, after, token in items:
                    need = {}
                    for t in after:
                        if t["value"] > seen.get(t["sem"].name, 0):
                            seen[t["sem"].name] = t["value"]
                            need[t["sem"].name] = (t["sem"], t["value"])
                    for sem, value in need.values():
                        eng.wait_ge(sem, value)
                    ins = fn(eng)
                    if token["needed"]:
                        ins.then_inc(token["sem"], 16 if token["dma"] else 1)
                if engine == "sync":
                    for sem, value in self.slots.values():
                        eng.wait_ge(sem, value)
            return body

        block.sync(play("sync", self.items["sync"]))
        block.scalar(play("scalar", self.items["scalar"]))
        block.vector(play("vector", self.items["vector"]))
        block.gpsimd(play("gpsimd", self.items["gpsimd"]))
        block.tensor(play("tensor", self.items["tensor"]))


class Buffer:

    def __init__(self, ap):
        self.ap, self.free = ap, []


def build(nc, a, out):
    ctx = ExitStack()
    with ctx:
        q = Queues(nc, ctx)

        def sb(name, shape, dt=F32):
            return ctx.enter_context(nc.sbuf_tensor(name, shape, dt))[:]

        def V(fn, *after):
            return q.add("vector", fn, after)

        def S(fn, *after):
            return q.add("scalar", fn, after)

        def G(fn, *after):
            return q.add("gpsimd", fn, after)

        def T(fn, *after):
            return q.add("tensor", fn, after)

        psum = ctx.enter_context(nc.psum_tensor("psum", [P, 8, 512], F32))[:]

        loaded = {}

        def load(name, shape, dt=F32, place=None, after=()):
            t = sb(name, shape, dt) if place is None else place
            loaded[name] = q.dma("sync", name, lambda e: e.dma_start(t, a[name]), after)
            return t

        def spread(name, n, place=None, after=()):
            t = sb(name, [P, n]) if place is None else place
            loaded[name] = q.dma("sync", name, lambda e: e.dma_start(t, a[name].to_broadcast([P, n])), after)
            return t

        early = sb("early", [P, 5 * 1024])
        probs_mem = sb("probs_mem", [P, HEADS * TPB * SEQ])

        def carve(region, sizes):
            at, pieces = 0, []
            for n in sizes:
                pieces.append(region[:, at:at + n])
                at += n
            assert at <= region.shape[1]
            return pieces

        x_sb = sb("x", [P, NT, D])
        x_rows = a["x"].rearrange("(t p) d -> p t d", p=P)
        x_in = []
        for b in range(BATCH):
            sl = slice(b * TPB, (b + 1) * TPB)
            x_in.append(q.dma("sync", f"x{b}", lambda e, sl=sl: e.dma_start(x_sb[:, sl, :], x_rows[:, sl, :])))
            if b == 0:
                ident = load("ident", [P, P])
                wq = load("wq", [P, P])
                bq = load("bq", [P, 1])
                wk = load("wk", [P, KSIDE])
                bk = load("bk", [KSIDE, 1])
                bkv = spread("bkv", DC)
                lo_rows = load("lo_rows", [P, 2])
                mk_m, mq_m, rq_m, buv_m, wo_m = carve(early, [HEADS * KSIDE] + 4 * [HEADS * P])
                heads = lambda m: m.rearrange("p (h c) -> p h c", h=HEADS)
                mk = load("mk", None, place=heads(mk_m))
                mq = load("mq", None, place=heads(mq_m))
                rk = load("rk", [DR + 1, KSIDE])
                rq = load("rq", None, place=heads(rq_m)[0:DR + 1])
        wuv = load("wuv", [P, HEADS, DC])
        buv = load("buv", [P, HEADS])
        wo = load("wo", None, place=heads(wo_m))
        bo = load("bo", [1, D])
        upto = load("upto", [P, P])
        before = sb("before", [P, P], BF16)
        before_set = V(lambda e: e.tensor_tensor(before, upto, ident, ALU.subtract), loaded["upto"], loaded["ident"])
        ones_bf = sb("ones_bf", [P, P], BF16)
        ones_bf_set = V(lambda e: e.memset(ones_bf, 1.0))
        choice = load("choice", [P, 2 * NE])
        token_id = load("token_id", [P, 2, NT], I32)
        pad_rec = load("pad_rec", [P, REC])
        wqkv, bqkv = load("wqkv", [D, 3 * D]), spread("bqkv", 3 * D)
        wout, bout = load("wout", [D, D]), spread("bout", D)
        head_mask = load("head_mask", [P, LH * LE])
        wg = load("wg", [D, NE])

        half = sb("half", [P, TPB])
        half_set = G(lambda e: e.memset(half, -0.5))
        ones_row = sb("ones_row", [1, P])
        ones_row_set = G(lambda e: e.memset(ones_row, 1.0))

        score_banks = [Buffer(psum[:, i, :]) for i in range(3)]
        shift_banks = [Buffer(psum[:, 3 + i, :]) for i in range(2)]
        num_bank, den_bank = Buffer(psum[:, 5, :]), Buffer(psum[:, 6, :])
        misc = Buffer(psum[:, 7, :])

        ln_stats = [sb(f"ln_stats{i}", [P, TPB, 6]) for i in range(2)]
        ln_mv = [Buffer(sb(f"ln_mv{i}", [P, TPB, 2])) for i in range(2)]
        ln_scale = [sb(f"ln_scale{i}", [P, TPB, 4]) for i in range(2)]
        ln_count = [0]

        def norm_stats(src, ready, twice=False):
            i = ln_count[0] % 2
            ln_count[0] += 1
            mv, stats, sc = ln_mv[i], ln_stats[i], ln_scale[i]
            st = [V(lambda e, j=j: e.bn_stats(stats[:, j, :], src(j)), ready, mv.free) for j in range(TPB)]
            ag = [V(lambda e, j=j: e.bn_aggr(mv.ap[:, j, :], stats[:, j, :]), st[j]) for j in range(TPB)]
            var, tmp = mv.ap[:, :, 1], sc[:, :, 2]
            t = G(lambda e: e.tensor_scalar(tmp, var, EPS, None, ALU.add), ag, mv.free)
            rs = [G(lambda e: e.tensor_tensor(sc[:, :, 0], tmp, half, ALU.pow), t, half_set)]
            if twice:
                t = G(lambda e: e.tensor_tensor(tmp, var, sc[:, :, 0], ALU.mult), rs)
                t = G(lambda e: e.tensor_tensor(tmp, tmp, sc[:, :, 0], ALU.mult), t)
                t = G(lambda e: e.tensor_scalar(tmp, tmp, EPS, None, ALU.add), t)
                t = G(lambda e: e.tensor_tensor(tmp, tmp, half, ALU.pow), t)
                rs.append(G(lambda e: e.tensor_tensor(sc[:, :, 1], tmp, sc[:, :, 0], ALU.mult), t))
            mv.free = []
            return mv, sc, rs

        def norm_apply(stats, which, dst, src, dst_free=(), engine=V):
            mv, sc, rs = stats
            w = [engine(lambda e, j=j: e.tensor_scalar(dst(j), src(j), mv.ap[:, j, 0:1], sc[:, j, which:which + 1],
                                                       ALU.subtract, ALU.mult), rs, dst_free) for j in range(TPB)]
            mv.free += w
            return w

        m_sb = sb("m_absorbed", [KSIDE, HEADS, P])
        m_ready = []

        def absorb(h0):
            mm = None
            for h in range(h0, h0 + 4):
                o = misc.ap[0:KSIDE, (h - h0) * P:(h - h0 + 1) * P]
                T(lambda e, h=h, o=o: e.matmul(o, mk[:, h, :], mq[:, h, :], start=True, stop=False),
                  misc.free, loaded["mk"], loaded["mq"])
                mm = T(lambda e, h=h, o=o: e.matmul(o, rk, rq[:, h, :], start=False, stop=True),
                       loaded["rk"], loaded["rq"])
            w = S(lambda e: e.copy(m_sb[:, h0:h0 + 4, :], misc.ap[0:KSIDE, :].rearrange("p (h c) -> p h c", h=4)), mm)
            misc.free = [w]
            m_ready.append(w)

        wvo = sb("wvo", [P, 2, D])
        bvo = sb("bvo", [P, D])
        buv_wide = heads(buv_m)

        def absorb_values():
            wide = [G(lambda e, h=h: e.tensor_copy(buv_wide[:, h, :], buv[:, h:h + 1].to_broadcast([P, P])),
                      loaded["buv"]) for h in range(HEADS)]
            mm = None
            for h in range(HEADS):
                g, r = divmod(h, 4)
                mm = T(lambda e, h=h, g=g, r=r: e.matmul(misc.ap[r * DC:(r + 1) * DC, g * D:(g + 1) * D], wuv[:, h, :],
                                                         wo[:, h, :], start=True, stop=True),
                       misc.free, loaded["wuv"], loaded["wo"])
            for h in range(HEADS):
                T(lambda e, h=h: e.matmul(misc.ap[:, 2 * D:3 * D], buv_wide[:, h, :], wo[:, h, :],
                                          start=(h == 0), stop=False), wide)
            mm = T(lambda e: e.matmul(misc.ap[:, 2 * D:3 * D], ones_row, bo, start=False, stop=True),
                   ones_row_set, loaded["bo"])
            w1 = V(lambda e: e.tensor_copy(wvo, misc.ap[:, 0:2 * D].rearrange("p (g d) -> p g d", g=2)), mm)
            w2 = V(lambda e: e.tensor_copy(bvo, misc.ap[:, 2 * D:3 * D]), mm)
            misc.free = [w1, w2]
            return [w1, w2]

        z = [Buffer(sb(f"z{i}", [P, TPB, D])) for i in range(2)]
        zT = [Buffer(sb(f"zT{i}", [P, SEQ])) for i in range(2)]
        q_full = sb("q_full", [P, SEQ])
        q_hi = sb("q_hi", [P, SEQ], F32R)
        q_free = [[]]
        q_stack = [Buffer(sb(f"q_stack{i}", [P, SEQ], F32R)) for i in range(3)]
        k_side = [Buffer(sb(f"k_side{i}", [KSIDE, SEQ])) for i in range(2)]
        ckv = [Buffer(sb(f"ckv{i}", [P, TPB, DC])) for i in range(3)]
        ones_dc = sb("ones_dc", [P, DC])
        ones_dc_set = G(lambda e: e.memset(ones_dc, 1.0))
        u_hi = [Buffer(sb(f"u_hi{i}", [P, SEQ], F32R)) for i in range(2)]
        u_ring = [Buffer(sb(f"u_stack{i}", [P, SEQ], F32R)) for i in range(HEADS + 2)]
        u_stack = lambda b, h: u_ring[(b * HEADS + h) % len(u_ring)]
        q_ready, k_ready, c_ready, u_ready, zT_ready = {}, {}, {}, {}, {}
        z_ready = {}

        z_stats = {}

        def step_stats(b):
            z_stats[b] = norm_stats(lambda j: x_sb[:, b * TPB + j, :], x_in[b])

        def step_norm(b):
            zb = z[b % 2]
            z_ready[b] = norm_apply(z_stats[b], 0, lambda j: zb.ap[:, j, :], lambda j: x_sb[:, b * TPB + j, :], zb.free)

        def transposes(dst, src, ready, dst_free, bank=None):
            bank = bank or misc
            mm = [T(lambda e, j=j: e.transpose(bank.ap[:, j * P:(j + 1) * P], src(j), ident),
                    ready, bank.free, loaded["ident"]) for j in range(TPB)]
            w = S(lambda e: e.copy(dst, bank.ap), mm[-1], dst_free)
            bank.free = [w]
            return mm[-1], w

        def step_zT(b):
            zb, zt = z[b % 2], zT[b % 2]
            t, w = transposes(zt.ap, lambda j: zb.ap[:, j, :], z_ready[b], zt.free)
            zb.free = [t]
            zT_ready[b] = w

        def step_q(b):
            zt, qs = zT[b % 2], q_stack[b % 3]
            mm = T(lambda e: e.matmul(misc.ap, wq, zt.ap, start=True, stop=True), zT_ready[b], misc.free, loaded["wq"])
            full = S(lambda e: e.activation(q_full, misc.ap, ACT.Identity, bias=bq), mm, loaded["bq"], q_free[0])
            misc.free = [full]
            hi = V(lambda e: e.tensor_copy(q_hi, q_full), full, q_free[0])
            w = V(lambda e: e.scalar_tensor_tensor(qs.ap, q_hi.bitcast(F32), lo_rows[:, 0:1], q_full, ALU.mult, ALU.add),
                  hi, loaded["lo_rows"], qs.free)
            q_free[0] = [w]
            q_ready[b] = w

        def step_k(b):
            zt, ks = zT[b % 2], k_side[b % 2]
            mm = T(lambda e: e.matmul(misc.ap[0:KSIDE, :], wk, zt.ap, start=True, stop=True),
                   zT_ready[b], misc.free, loaded["wk"])
            w = S(lambda e: e.activation(ks.ap, misc.ap[0:KSIDE, :], ACT.Identity, bias=bk), mm, loaded["bk"], ks.free)
            misc.free = [w]
            k_ready[b] = w

        def step_ckv(b):
            zt, c = zT[b % 2], ckv[b % 3]
            mm = [T(lambda e, j=j: e.matmul(misc.ap[:, j * DC:(j + 1) * DC], zt.ap[:, j * P:(j + 1) * P], wk[:, 0:DC],
                                            start=True, stop=True), zT_ready[b], misc.free) for j in range(TPB)]
            w = V(lambda e: e.tensor_tensor(c.ap, misc.ap[:, 0:TPB * DC].rearrange("p (t c) -> p t c", t=TPB),
                                            bkv.unsqueeze(1).to_broadcast([P, TPB, DC]), ALU.add),
                  mm[-1], loaded["bkv"], c.free)
            misc.free = [w]
            zt.free = [mm[-1]]
            c_ready[b] = w

        def step_u(b, h):
            ks, us, uh = k_side[b % 2], u_stack(b, h), u_hi[h % 2]
            mm = T(lambda e: e.matmul(misc.ap, m_sb[:, h, :], ks.ap, start=True, stop=True),
                   k_ready[b], m_ready[h // 4], misc.free)
            hi = S(lambda e: e.copy(uh.ap, misc.ap), mm, uh.free)
            w = V(lambda e: e.scalar_tensor_tensor(us.ap, uh.ap.bitcast(F32), lo_rows[:, 1:2], misc.ap,
                                                   ALU.mult, ALU.add), hi, us.free)
            misc.free = [w]
            uh.free = [w]
            ks.free = [mm]
            u_ready[b, h] = w

        neg_max = [Buffer(sb(f"neg_max{i}", [P, TPB, HEADS])) for i in range(2)]
        max_ready = {}

        score_turn = [0]

        def step_scores(b, h, tiles):
            qs, us, nm = q_stack[b % 3], u_stack(b, h), neg_max[b % 2]
            for j in tiles:
                bank = score_banks[score_turn[0] % len(score_banks)]
                score_turn[0] += 1
                mm = T(lambda e, j=j, bank=bank: e.matmul(bank.ap, qs.ap[0:SCORE_K, j * P:(j + 1) * P],
                                                          us.ap[0:SCORE_K, :], start=True, stop=True),
                       q_ready[b], u_ready[b, h], bank.free)
                w = V(lambda e, j=j, bank=bank: e.tensor_reduce(nm.ap[:, j, h:h + 1], bank.ap, AX.X, ALU.max, negate=True),
                      mm, nm.free)
                bank.free = [w]
                max_ready.setdefault(b, []).append(w)

        max_hi = sb("max_hi", [P, TPB, HEADS], F32R)
        max_tile = sb("max_tile", [P, TPB, P])
        mt_zero = G(lambda e: e.memset(max_tile, 0.0))
        mt_ones = G(lambda e: e.memset(max_tile[:, :, ROW_ONE:ROW_MHI], 1.0), mt_zero)
        mt_free = [[mt_ones]]
        shift_ready = {}

        def step_shift(b):
            nm, qs = neg_max[b % 2], q_stack[b % 3]
            hi = V(lambda e: e.tensor_copy(max_hi, nm.ap), max_ready[b], mt_free[0])
            w1 = V(lambda e: e.tensor_copy(max_tile[:, :, ROW_MHI:ROW_MLO], max_hi.bitcast(F32)), hi, mt_free[0])
            w2 = V(lambda e: e.tensor_tensor(max_tile[:, :, ROW_MLO:SHIFT_K], nm.ap, max_hi.bitcast(F32), ALU.subtract), hi)
            nm.free = [w2]
            mm = [T(lambda e, j=j: e.transpose(misc.ap[:, j * P:(j + 1) * P], max_tile[:, j, :], ident),
                    w1, w2, misc.free) for j in range(TPB)]
            w = V(lambda e: e.tensor_copy(qs.ap[ROW_ONE:P, :], misc.ap[ROW_ONE:P, :]), mm[-1], max_ready[b])
            misc.free = [w]
            mt_free[0] = [w2, mm[-1]]
            shift_ready[b] = w

        prob = [Buffer(m.rearrange("p (t s) -> p t s", t=TPB)) for m in carve(probs_mem, HEADS * [TPB * SEQ])]
        oT = [Buffer(sb(f"oT{g}", [P, SEQ])) for g in range(2)]
        den_t, inv_col, inv_den = sb("den_t", [P, SEQ]), sb("inv_col", [P, SEQ // DC]), sb("inv_den", [P, SEQ])
        prob_ready, oT_ready = {}, {}

        def step_exp(b, h, tiles):
            qs, us, pr = q_stack[b % 3], u_stack(b, h), prob[h]
            for j in tiles:
                bank = shift_banks[j % 2]
                mm = T(lambda e, j=j, bank=bank: e.matmul(bank.ap, us.ap[0:SHIFT_K, j * P:(j + 1) * P],
                                                          qs.ap[0:SHIFT_K, :], start=True, stop=True),
                       shift_ready[b], u_ready[b, h], bank.free)
                x = S(lambda e, j=j, bank=bank: e.activation(pr.ap[:, j, :], bank.ap, ACT.Exp, scale=SCORE_SCALE),
                      mm, pr.free)
                bank.free = [x]
                prob_ready.setdefault((b, h), []).append(x)
            us.free = [mm]
            qs.free = [mm]

        def step_values(b, g, j, part):
            c = ckv[b % 3]
            bank = (num_bank, den_bank)[part]
            for r in range(QUAD):
                pr = prob[g * QUAD + r]
                lhs = c.ap[:, j, :] if part == 0 else ones_dc
                mm = T(lambda e, r=r, pr=pr, lhs=lhs: e.matmul(bank.ap[r * DC:(r + 1) * DC, :], lhs, pr.ap[:, j, :],
                                                               start=(j == 0), stop=(j == TPB - 1)),
                       [prob_ready[b, g * QUAD + x] for x in range(QUAD)], c_ready[b], ones_dc_set, bank.free)
            if (j, part) == (TPB - 1, 1):
                for r in range(QUAD):
                    prob[g * QUAD + r].free = [mm]
                c.free = [mm]
                t = V(lambda e: e.transpose(den_t, den_bank.ap), mm)
                den_bank.free = [t]
                r = V(lambda e: e.reciprocal(inv_col, den_t.rearrange("p (b c) -> p b c", c=DC)[:, :, 0]), t)
                t = V(lambda e: e.transpose(inv_den.rearrange("p (b c) -> p b c", c=DC),
                                            inv_col.unsqueeze(2).to_broadcast([P, SEQ // DC, DC])), r)
                w = V(lambda e: e.tensor_tensor(oT[g].ap, num_bank.ap, inv_den, ALU.mult), t, oT[g].free)
                num_bank.free = [w]
                oT_ready[b, g] = w

        res_ready = {}
        xb_ready = {}

        def step_residual_bias(b, bias_ready):
            for j in range(TPB):
                t = b * TPB + j
                w = G(lambda e, t=t: e.tensor_tensor(x_sb[:, t, :], x_sb[:, t, :], bvo, ALU.add),
                      bias_ready, z_ready[b])
                xb_ready.setdefault(b, []).append(w)

        def step_out(b):
            for j in range(TPB):
                for g in range(2):
                    mm = T(lambda e, j=j, g=g: e.matmul(misc.ap[:, j * P:(j + 1) * P], oT[g].ap[:, j * P:(j + 1) * P],
                                                        wvo[:, g, :], start=(g == 0), stop=(g == 1)),
                           oT_ready[b, 0], oT_ready[b, 1], misc.free, wvo_ready)
            oT[0].free = oT[1].free = [mm]
            xs = x_sb[:, b * TPB:(b + 1) * TPB, :]
            w = V(lambda e: e.tensor_tensor(xs, misc.ap.rearrange("p (t d) -> p t d", t=TPB), xs, ALU.add),
                  mm, xb_ready[b])
            misc.free = [w]
            res_ready[b] = w

        wide_free = [[]]

        class Experts:
            def __init__(self, n, k, w1, w2, b1, b2, weights_ready, func, gate, gate_ready, work, work_free):
                self.n, self.k, self.nb = n, k, n_blocks(k)
                self.w1, self.w2, self.b1, self.b2 = w1, w2, b1, b2
                self.weights_ready, self.func, self.gate, self.gate_ready = weights_ready, func, gate, gate_ready
                self.work, self.work_free = work, work_free
                self.records = nc.dram_tensor(f"records{n}", [PAD_ROW + P, REC], F32, kind="Internal").ap()
                self.outs = nc.dram_tensor(f"outs{n}", [k * TOK, D], F32, kind="Internal").ap()
                self.pad = q.dma("sync", f"pad{n}", lambda e: e.dma_start(self.records[PAD_ROW:PAD_ROW + P, :], pad_rec),
                                 loaded["pad_rec"])
                self.rec = [[Buffer(sb(f"rec{n}_{i}_{c}", [P, TPB, REC])) for c in range(k)] for i in range(2)]
                self.logits = sb(f"logits{n}", [P, TPB, NE])
                self.top = sb(f"top{n}", [P, TPB, NE])
                self.top_at = sb(f"top_at{n}", [P, TPB, NE], U32)
                self.pick = [sb(f"pick{n}_{c}", [P, TPB, NE]) for c in range(k)]
                self.pick_bf = sb(f"pick_bf{n}", [P, TPB, NE], BF16)
                self.seen = [sb(f"seen{n}_{i}", [P, NE], BF16) for i in range(2)]
                self.seen_f = sb(f"seen_f{n}", [P, NE])
                self.seen_set = [V(lambda e: e.memset(self.seen[0], 0.0))]
                self.rank = sb(f"rank{n}", [P, TPB, NE])
                self.rank_k = sb(f"rank_k{n}", [P, TPB, NE])
                self.row_f = sb(f"row_f{n}", [P, TPB])
                self.row = [sb(f"row{n}_{c}", [P, NT], I32) for c in range(k)]
                self.scattered = []
                self.chain = []

            def choose_top(self, b):
                mx = [V(lambda e, j=j: e.max(self.top[:, j, :], self.logits[:, j, :]), self.logits_ready, self.chain)
                      for j in range(TPB)]
                at = [V(lambda e, j=j: e.max_index(self.top_at[:, j, :], self.top[:, j, :], self.logits[:, j, :]), mx[j])
                      for j in range(TPB)]
                self.top_ready = mx
                self.pick_ready = [V(lambda e, c=c: e.tensor_tensor(
                    self.pick[c], choice[:, 0:NE].unsqueeze(1).to_broadcast([P, TPB, NE]),
                    self.top_at[:, :, c:c + 1].to_broadcast([P, TPB, NE]), ALU.is_equal),
                    at, loaded["choice"]) for c in range(self.k)]

            def send(self, b, bank, rec_ready):
                if self.k == 1:
                    bf = V(lambda e: e.tensor_copy(self.pick_bf, self.pick[0]), self.pick_ready, self.chain)
                else:
                    bf = V(lambda e: e.tensor_tensor(self.pick_bf, self.pick[0], self.pick[1], ALU.add),
                           self.pick_ready, self.chain)
                old, new = self.seen[b % 2], self.seen[(b + 1) % 2]
                for j in range(TPB):
                    o = bank.ap[:, j * NE:(j + 1) * NE]
                    mm = T(lambda e, o=o: e.matmul(o, ones_bf, old, start=True, stop=False),
                           bank.free, self.seen_set, ones_bf_set)
                    for i in range(j):
                        mm = T(lambda e, o=o, i=i: e.matmul(o, ones_bf, self.pick_bf[:, i, :], start=False, stop=False), bf)
                    mm = T(lambda e, o=o, j=j: e.matmul(o, before, self.pick_bf[:, j, :], start=False, stop=True),
                           bf, before_set)
                s1 = V(lambda e: e.tensor_reduce(self.seen_f, self.pick_bf.rearrange("p t n -> p n t"), AX.X, ALU.add), bf)
                self.seen_set = [V(lambda e: e.tensor_tensor(new, old, self.seen_f, ALU.add), s1, self.seen_set)]
                r = V(lambda e: e.tensor_tensor(self.rank, bank.ap[:, 0:TPB * NE].rearrange("p (t n) -> p t n", t=TPB),
                                                choice[:, NE:2 * NE].unsqueeze(1).to_broadcast([P, TPB, NE]), ALU.add), mm)
                bank.free = [r]
                done = [mm, s1]
                for c in range(self.k):
                    m = V(lambda e, c=c: e.tensor_tensor(self.rank_k, self.rank, self.pick[c], ALU.mult), r, done)
                    f = V(lambda e: e.tensor_reduce(self.row_f, self.rank_k, AX.X, ALU.add), m)
                    w = V(lambda e, c=c: e.tensor_copy(self.row[c][:, b * TPB:(b + 1) * TPB], self.row_f), f)
                    done = [mm, s1, w]
                    rec = self.rec[b % 2][c]
                    rec.free = []
                    for j in range(TPB):
                        t = b * TPB + j
                        d = q.dma("gpsimd", f"scatter{self.n}_{b % 2}{c}{j}", lambda e, c=c, j=j, t=t, rec=rec: e.indirect_dma_start(
                            self.records, bass.IndirectOffsetOnAxis(self.row[c][:, t:t + 1], 0), rec.ap[:, j, :], None),
                            [w, rec_ready])
                        rec.free.append(d)
                        self.scattered.append(d)
                self.chain = done

            def plan(self, bank):
                n, nb = self.n, self.nb
                one = lambda name, shape, dt=F32: sb(f"{name}{n}", shape, dt)
                block_no, is_from, is_upto, val = (m[0:1, 0:nb * NE].rearrange("p (b n) -> p b n", n=NE)
                                                   for m in (max_tile.rearrange("p t c -> p (t c)"), den_t, inv_den, q_full))
                load(f"block_no{n}", None, place=block_no, after=[mt_free[0], wide_free[0]])
                mm = T(lambda e: e.matmul(bank.ap[:, 0:NE], ones_bf, self.seen[BATCH % 2], start=True, stop=True),
                       self.seen_set, bank.free)
                count = one("count", [1, NE], I32)
                fill = one("fill", [1, NE], I32)
                blocks_i, blocks_f = one("blocks_i", [1, NE], I32), one("blocks_f", [1, NE])
                upto_e, from_e, base = one("upto_e", [1, NE]), one("from_e", [1, NE]), one("base", [1, NE])
                first = one("first", [1, nb])
                table = one("table", [1, 3, nb], I32)
                wide = lambda x: x.unsqueeze(1).to_broadcast([1, nb, NE])
                c1 = V(lambda e: e.tensor_scalar(count, bank.ap[0:1, 0:NE], float(P - 1), None, ALU.add), mm)
                c2 = V(lambda e: e.tensor_tensor(fill, bank.ap[0:1, 0:NE], choice[0:1, NE:2 * NE], ALU.add), mm)
                bank.free = [c1, c2]
                c3 = V(lambda e: e.tensor_scalar(blocks_i, count, P.bit_length() - 1, None, ALU.logical_shift_right), c1)
                c4 = V(lambda e: e.tensor_copy(blocks_f, blocks_i), c3)
                c5 = V(lambda e: e.tensor_tensor_scan(upto_e, ones_row[:, 0:NE], blocks_f, 0.0, ALU.mult, ALU.add),
                       c4, ones_row_set)
                c6 = V(lambda e: e.tensor_tensor(from_e, upto_e, blocks_f, ALU.subtract), c5)
                c7 = V(lambda e: e.scalar_tensor_tensor(base, from_e, -float(P), choice[0:1, NE:2 * NE], ALU.mult, ALU.add), c6)
                c8 = V(lambda e: e.tensor_tensor(is_upto, wide(upto_e), block_no, ALU.is_le), c5, loaded[f"block_no{n}"])
                c9 = V(lambda e: e.tensor_tensor(is_from, wide(from_e), block_no, ALU.is_le), c6)
                ca = V(lambda e: e.tensor_tensor(is_from, is_from, is_upto, ALU.subtract), c8, c9)
                cb = V(lambda e: e.scalar_tensor_tensor(val, block_no, float(P), wide(base), ALU.mult, ALU.add), c7)
                cc = V(lambda e: e.scalar_tensor_tensor(val, val, -float(PAD_ROW), is_from, ALU.add, ALU.mult), ca, cb)
                cd = V(lambda e: e.tensor_reduce(first, val, AX.X, ALU.add), cc)
                ce = V(lambda e: e.tensor_scalar(table[:, 0, :], first, float(PAD_ROW), None, ALU.add), cd)
                cf = V(lambda e: e.tensor_tensor(val, is_from, wide(choice[0:1, 0:NE]), ALU.mult), cd)
                cg = V(lambda e: e.tensor_reduce(first, val, AX.X, ALU.add), cf, ce)
                ch = V(lambda e: e.tensor_scalar(table[:, 1, :], first, float(FF), None, ALU.mult), cg)
                ci = V(lambda e: e.tensor_scalar(table[:, 2, :], first, float(D), None, ALU.mult), cg)
                self.table, self.table_ready = table, [ce, ch, ci]
                wide_free[0] = self.table_ready

                def pad(e, i):
                    at = e.value_load(fill[0:1, i:i + 1], min_val=0, max_val=PAD_ROW)
                    return e.dma_start(self.records[bass.ds(at, P), :], pad_rec)

                self.padded = [q.dma("sync", f"fill{n}_{i}", lambda e, i=i: pad(e, i), c2) for i in range(NE)]

            def blocks(self, banks):
                n, k, nb = self.n, self.k, self.nb
                IN = 6
                sizes = IN * [REC] + 2 * [P] + 2 * [FF] + 2 * [FF] + 2 * [D] + 4 * [D]
                m = [Buffer(x) for x in carve(self.work, sizes)]
                for x in m:
                    x.free = list(self.work_free)
                rec_in, xT, h_sb, hT, y_sb, out_sb = m[0:IN], m[IN:IN + 2], m[IN + 2:IN + 4], m[IN + 4:IN + 6], \
                    m[IN + 6:IN + 8], m[IN + 8:IN + 12]
                x_bank, h_banks, hT_banks, y_banks = banks[0], banks[1:3], banks[3:5], banks[5:7]
                w1, w2 = self.w1, self.w2
                got, xt, h_ok, hT_ok = {}, {}, {}, {}
                self.sent = []

                def fetch(i):
                    r = rec_in[i % IN]

                    def go(e):
                        at = e.value_load(self.table[0:1, 0, i:i + 1], min_val=0, max_val=PAD_ROW)
                        return e.dma_start(r.ap, self.records[bass.ds(at, P), :])

                    got[i] = q.dma("sync", f"fetch{n}_{i % IN}", go, [self.table_ready, self.padded, self.scattered, self.pad, r.free])

                def turn(i):
                    r, x = rec_in[i % IN], xT[i % 2]
                    mm = T(lambda e: e.transpose(x_bank.ap[:, 0:P], r.ap[:, 0:D], ident), got[i], x_bank.free)
                    w = S(lambda e: e.copy(x.ap, x_bank.ap[:, 0:P]), mm, x.free)
                    x_bank.free = [w]
                    xt[i] = [w, mm]

                def first(i):
                    x, h, bank = xT[i % 2], h_sb[i % 2], h_banks[i % 2]

                    def go(e):
                        at = e.value_load(self.table[0:1, 1, i:i + 1], min_val=0, max_val=(NE - 1) * FF)
                        return e.matmul(bank.ap, x.ap, w1[:, bass.ds(at, FF)], start=True, stop=True)

                    mm = T(go, xt[i], bank.free, self.table_ready, self.weights_ready)

                    def bias(e):
                        at = e.value_load(self.table[0:1, 1, i:i + 1], min_val=0, max_val=(NE - 1) * FF)
                        return e.tensor_tensor(h.ap, bank.ap, self.b1[:, bass.ds(at, FF)], ALU.add)

                    w = V(bias, mm, h.free, self.table_ready, self.weights_ready)
                    x.free = [mm]
                    bank.free = [w]
                    h_ok[i] = w

                def middle(i):
                    h, ht, bank = h_sb[i % 2], hT[i % 2], hT_banks[i % 2]
                    mm = [T(lambda e, c=c: e.transpose(bank.ap[:, c * P:(c + 1) * P], h.ap[:, c * P:(c + 1) * P], ident),
                            h_ok[i], bank.free) for c in range(FC)]
                    w = S(lambda e: e.activation(ht.ap, bank.ap, self.func), mm[-1], ht.free)
                    h.free = [mm[-1]]
                    bank.free = [w]
                    hT_ok[i] = w

                def second(i):
                    ht, y, o, r, bank = hT[i % 2], y_sb[i % 2], out_sb[i % 4], rec_in[i % IN], y_banks[i % 2]

                    def go(e, c, at=[None]):
                        if c == 0:
                            at[0] = e.value_load(self.table[0:1, 1, i:i + 1], min_val=0, max_val=(NE - 1) * FF)
                        return e.matmul(bank.ap[:, 0:D], ht.ap[:, c * P:(c + 1) * P], w2[:, bass.ds(at[0] + c * P, D)],
                                        start=(c == 0), stop=(c == FC - 1))

                    for c in range(FC):
                        mm = T(lambda e, c=c: go(e, c), hT_ok[i], bank.free)

                    def bias(e):
                        at = e.value_load(self.table[0:1, 2, i:i + 1], min_val=0, max_val=(NE - 1) * D)
                        return e.tensor_tensor(y.ap, bank.ap[:, 0:D], self.b2[:, bass.ds(at, D)], ALU.add)

                    w = V(bias, mm, y.free)
                    ht.free = [mm]
                    bank.free = [w]
                    g = G(lambda e: e.tensor_scalar(o.ap, y.ap, r.ap[:, D:D + 1], None, ALU.mult), w, o.free)
                    y.free = [g]
                    d = q.dma("gpsimd", f"send{n}_{i % 4}", lambda e: e.indirect_dma_start(
                        self.outs, bass.IndirectOffsetOnAxis(r.ap[:, D + 1:D + 2].bitcast(I32), 0), o.ap, None,
                        bounds_check=k * TOK - 1, oob_is_err=False), g)
                    o.free = [d]
                    r.free = [d]
                    self.sent.append(d)
                    self.ended = [mm, w, g]

                for i in range(IN):
                    fetch(i)
                turn(0)
                for i in range(nb + 2):
                    if i < nb:
                        first(i)
                    if 1 <= i <= nb:
                        middle(i - 1)
                    if i >= 2:
                        second(i - 2)
                    if i + 1 < nb:
                        turn(i + 1)
                    if 2 <= i and i - 2 + IN < nb:
                        fetch(i - 2 + IN)

        w2_mem, b2_mem0, b2_mem1, w1_mem1, moe_work, late = carve(
            probs_mem, [NE * FF, NE * D, NE * D, NE * FF, NE * FF, NE * FF // 2])
        b1_0 = spread("b1_0", NE * FF)
        ln_g, ln_b = load("ln_g", [P, NE]), load("ln_b", [P, NE])
        centroids = load("centroids", [P, NE])
        z1 = [Buffer(sb(f"ffn_z{i}", [P, TPB, D])) for i in range(2)]
        z1T = Buffer(sb("ffn_zT", [P, SEQ]))

        class Experts0(Experts):
            def steps(self, b):
                tiles = slice(b * TPB, (b + 1) * TPB)

                def norms():
                    self.stats = norm_stats(lambda j: x_sb[:, b * TPB + j, :], res_ready[b], twice=True)

                def apply():
                    src = lambda j: x_sb[:, b * TPB + j, :]
                    self.z_ok = norm_apply(self.stats, 0, lambda j: z1[b % 2].ap[:, j, :], src, z1[b % 2].free, engine=G)
                    rec = self.rec[b % 2][0]
                    self.rec_ok = norm_apply(self.stats, 1, lambda j: rec.ap[:, j, 0:D], src, rec.free)
                    self.rec_ok.append(V(lambda e: e.tensor_copy(rec.ap[:, :, D + 1].bitcast(I32), token_id[:, 0, tiles]),
                                         loaded["token_id"], rec.free))

                def choose():
                    t, w = transposes(z1T.ap, lambda j: z1[b % 2].ap[:, j, :], self.z_ok, z1T.free)
                    mm = [T(lambda e, j=j: e.matmul(misc.ap[:, j * NE:(j + 1) * NE], z1T.ap[:, j * P:(j + 1) * P],
                                                    centroids, start=True, stop=True), w, misc.free, loaded["centroids"])
                          for j in range(TPB)]
                    z1T.free = [mm[-1]]
                    lg = V(lambda e: e.tensor_copy(self.logits, misc.ap[:, 0:TPB * NE].rearrange("p (t n) -> p t n", t=TPB)),
                           mm[-1], self.chain)
                    misc.free = [lg]
                    self.logits_ready = lg
                    self.choose_top(b)
                    ex = S(lambda e: e.activation(self.gate, self.top[:, :, 0], ACT.Exp, scale=-1.0), self.top_ready, self.gate_ready)
                    p1 = V(lambda e: e.tensor_scalar(self.gate, self.gate, 1.0, None, ALU.add), ex)
                    rec = self.rec[b % 2][0]
                    self.gate_ready = [V(lambda e: e.reciprocal(rec.ap[:, :, D], self.gate), p1, rec.free)]
                    self.rec_ok += self.gate_ready

                def send():
                    self.send(b, misc, self.rec_ok)
                    zb, xs = z1[b % 2], x_sb[:, tiles, :]
                    w = G(lambda e: e.tensor_tensor(xs, xs, zb.ap, ALU.add), self.rec_ok, self.z_ok)
                    zb.free = [w]
                    self.residual.append(w)

                return [norms, apply, choose, send]

            def setup(self, e0):
                lnb_wide = self.lnb_wide
                for x in e0:
                    w = G(lambda e, x=x: e.tensor_copy(lnb_wide, ln_b[:, x:x + 1].to_broadcast([P, P])),
                          loaded["ln_b"], self.wide_free)
                    mm = T(lambda e, x=x: e.matmul(misc.ap, lnb_wide, self.w1[:, x * FF:(x + 1) * FF], start=True, stop=True),
                           w, misc.free, loaded["w1_0"])
                    self.wide_free = [mm]
                    sl = self.b1[:, x * FF:(x + 1) * FF]
                    v = V(lambda e, sl=sl: e.tensor_tensor(sl, misc.ap, sl, ALU.add), mm, loaded["b1_0"])
                    misc.free = [v]
                    g = G(lambda e, x=x: e.tensor_scalar(self.w1[:, x * FF:(x + 1) * FF], self.w1[:, x * FF:(x + 1) * FF],
                                                         ln_g[:, x:x + 1], None, ALU.mult), mm, loaded["ln_g"])
                    self.weights_ready += [v, g]

            def finish(self):
                self.work_free = [p.free for p in prob]
                self.plan(misc)
                banks = [Buffer(psum[:, i, :]) for i in range(8)]
                for bank, old in zip(banks, score_banks + shift_banks + [num_bank, den_bank, misc]):
                    bank.free = list(old.free)
                self.blocks(banks)
                self.banks = banks

        experts0 = Experts0(0, 1, None, None, b1_0, None, [], ACT.Relu,
                            sb("gate0", [P, TPB]), [], moe_work, ())
        experts0.residual, experts0.wide_free, experts0.lnb_wide = [], [], sb("lnb_wide", [P, P])

        step_stats(0)
        step_norm(0)
        absorb(0)
        step_zT(0)
        step_k(0)
        step_q(0)
        absorb(4)
        step_ckv(0)
        wvo_ready = absorb_values()
        experts0.w1 = load("w1_0", None, place=early[:, 0:NE * FF], after=[wvo_ready, m_ready])
        step_u(0, 0)
        ahead = {0: [lambda: step_stats(1)], 1: [lambda: step_norm(1)], 3: [lambda: step_zT(1)], 4: [lambda: step_k(1)],
                 5: [lambda: step_q(1)], 6: [lambda: step_ckv(1)]}
        for h in range(HEADS):
            step_scores(0, h, range(0, 2))
            if h + 1 < HEADS:
                step_u(0, h + 1)
            step_scores(0, h, range(2, 4))
            for step in ahead.get(h, []):
                step()
        step_u(1, 0)
        step_shift(0)

        def group_steps(b, g):
            return [(b, g, j, part) for j in range(TPB) for part in range(2)]

        values = []
        later = []
        for b in range(BATCH):
            step_residual_bias(b, wvo_ready)
            nxt, nxt2 = b + 1 < BATCH, b + 2 < BATCH
            scores = [(b + 1, h, (2 * k, 2 * k + 1)) for h in range(HEADS) for k in range(2)] if nxt else []
            for h in range(HEADS):
                if nxt and h + 1 < HEADS:
                    step_u(b + 1, h + 1)
                step_exp(b, h, (0, 1))
                for _ in range(1 if h < 6 else 2):
                    if scores and scores[0][1] <= h + 1:
                        step_scores(*scores.pop(0))
                if values:
                    step_values(*values.pop(0))
                step_exp(b, h, (2, 3))
                for _ in range(1 if h < 6 else 2):
                    if scores and scores[0][1] <= h + 1:
                        step_scores(*scores.pop(0))
                if nxt2 and h == 1:
                    step_stats(b + 2)
                if nxt2 and h == 2:
                    step_norm(b + 2)
                if nxt2 and h == 4:
                    step_zT(b + 2)
                if nxt2 and h == 5:
                    step_k(b + 2)
                if nxt2 and h == 6:
                    step_q(b + 2)
                if nxt2 and h == 7:
                    step_ckv(b + 2)
                if b == BATCH - 1:
                    experts0.setup([h])
                if b > 0 and h == QUAD:
                    later += [lambda b=b: step_out(b - 1)] + experts0.steps(b - 1)
                if later:
                    later.pop(0)()
                if values:
                    step_values(*values.pop(0))
                if h == QUAD - 1:
                    values += group_steps(b, 0)
            if nxt2:
                step_u(b + 2, 0)
            if nxt:
                step_shift(b + 1)
            values += group_steps(b, 1)
        for v in values:
            step_values(*v)
        for step in later:
            step()
        step_out(BATCH - 1)
        experts0.w2 = load("w2_0", None, place=w2_mem, after=[p.free for p in prob[0:2]])
        experts0.b2 = spread("b2_0", NE * D, place=b2_mem0, after=prob[2].free)
        experts0.weights_ready += [loaded["w2_0"], loaded["b2_0"]]
        for step in experts0.steps(BATCH - 1):
            step()
        experts0.finish()
        collect_bufs = [Buffer(m.rearrange("p (t d) -> p t d", t=TPB)) for m in carve(late, 4 * [TPB * D])]
        for m in collect_bufs:
            m.free = [p.free for p in prob]
        collect_turn = [0]

        def collect(ex, b, ready):
            xs = x_sb[:, b * TPB:(b + 1) * TPB, :]
            for c in range(ex.k):
                y = collect_bufs[collect_turn[0] % 4]
                collect_turn[0] += 1
                rows = ex.outs[(c * NT + b * TPB) * P:(c * NT + (b + 1) * TPB) * P, :]
                d = q.dma("sync", f"collect{collect_turn[0] % 4}", lambda e, y=y, rows=rows: e.dma_start(
                    y.ap, rows.rearrange("(t p) d -> p t d", p=P)), [ex.sent, y.free])
                ready = [V(lambda e, y=y: e.tensor_tensor(xs, xs, y.ap, ALU.add), d, ready)]
                y.free = ready
            return ready

        freed = [experts0.ended, experts0.sent]

        def reuse(m):
            x = Buffer(m)
            x.free = list(freed)
            return x

        e_ = carve(early, [LH * LE * LD] * 3 + [3 * D] * 2 + [2 * D] * 3 + [D])
        kv_buf, prod_buf = [reuse(m) for m in e_[0:2]], reuse(e_[2])
        qkv_buf, qk_buf, low_buf, o_buf = [reuse(m) for m in e_[3:5]], [reuse(m) for m in e_[5:7]], reuse(e_[7]), reuse(e_[8])
        w_ = carve(moe_work, [2 * D] + 2 * [LH * LE] + 2 * [P] + 2 * [LH * LE] + [P] + 2 * [LH * LE] + [LH * LE] + [LH] * 2)
        exp_buf, v_buf, qT_buf = reuse(w_[0]), [reuse(m) for m in w_[1:3]], [reuse(m) for m in w_[3:5]]
        sum_buf, oT_buf, state_buf = [reuse(m) for m in w_[5:7]], reuse(w_[7]), [reuse(m) for m in w_[8:10]]
        new_buf, norm_buf, inv_buf = reuse(w_[10]), reuse(w_[11]), reuse(w_[12])
        heads_of = lambda m, n: m.rearrange("p (h c) -> p h c", c=n)
        v_one = [V(lambda e, v=v: e.memset(heads_of(v.ap, LE)[:, :, LD:LE], 1.0), v.free) for v in v_buf]
        banks = experts0.banks
        spare, qkv_bank, q_bank, inter_bank, out_bank = banks[0], banks[1], banks[2], banks[3], banks[4]
        half_banks = [Buffer(psum[:, 5, :]), Buffer(psum[:, 6, :]), Buffer(psum[:, 7, :])]
        for hb, old in zip(half_banks, banks[5:8]):
            hb.free = old.free
        l1_ready, l1z, l1zT, part = {}, {}, {}, {}

        def l1_tokens(b):
            l1_ready[b] = collect(experts0, b, experts0.residual)
            xs = x_sb[:, b * TPB:(b + 1) * TPB, :]
            st = norm_stats(lambda j: x_sb[:, b * TPB + j, :], l1_ready[b])
            zb = z[b % 2]
            zw = norm_apply(st, 0, lambda j: zb.ap[:, j, :], lambda j: x_sb[:, b * TPB + j, :], zb.free)
            l1_ready[b] = [G(lambda e: e.tensor_tensor(xs, xs, bout.unsqueeze(1).to_broadcast([P, TPB, D]), ALU.add),
                             zw, loaded["bout"])]
            zt = zT[b % 2]
            t, l1zT[b] = transposes(zt.ap, lambda j: zb.ap[:, j, :], zw, zt.free, bank=spare)
            zb.free = [t]

        def l1_features(t):
            b, c = divmod(t, TPB)
            zt, qkv, qk, v, kv = zT[b % 2], qkv_buf[t % 2], qk_buf[t % 2], v_buf[t % 2], kv_buf[t % 2]
            mm = T(lambda e: e.matmul(qkv_bank.ap[:, 0:3 * D], zt.ap[:, c * P:(c + 1) * P], wqkv, start=True, stop=True),
                   l1zT[b], qkv_bank.free, loaded["wqkv"])
            zt.free = [mm]
            w = V(lambda e: e.tensor_tensor(qkv.ap, qkv_bank.ap[:, 0:3 * D], bqkv, ALU.add), mm, qkv.free, loaded["bqkv"])
            qkv_bank.free = [w]
            lo = G(lambda e: e.tensor_scalar(low_buf.ap, qkv.ap[:, 0:2 * D], 0.0, None, ALU.min), w, low_buf.free)
            ex = S(lambda e: e.activation(exp_buf.ap, low_buf.ap, ACT.Exp), lo, exp_buf.free)
            low_buf.free = [ex]
            vc = S(lambda e: e.copy(heads_of(v.ap, LE)[:, :, 0:LD], heads_of(qkv.ap[:, 2 * D:3 * D], LD)), w, v.free)
            f = V(lambda e: e.scalar_tensor_tensor(qk.ap, qkv.ap[:, 0:2 * D], 0.0, exp_buf.ap, ALU.max, ALU.add), ex, qk.free)
            exp_buf.free = [f]
            qkv.free = [f, vc]
            kh, vh = heads_of(qk.ap[:, D:2 * D], LD), heads_of(v.ap, LE)
            o = G(lambda e: e.tensor_tensor(kv.ap.rearrange("p (h c d) -> p h c d", h=LH, c=LE),
                                            kh.unsqueeze(2).to_broadcast([P, LH, LE, LD]),
                                            vh.unsqueeze(3).to_broadcast([P, LH, LE, LD]), ALU.mult), f, vc, v_one, kv.free)
            part[t] = [f, vc, o]

        def l1_sums(t):
            b, c = divmod(t, TPB)
            f, vc, o = part[t]
            qk, v, kv, qT, total = qk_buf[t % 2], v_buf[t % 2], kv_buf[t % 2], qT_buf[t % 2], sum_buf[t % 2]
            old, new = state_buf[t % 2], state_buf[(t + 1) % 2]
            if c > 0:
                mq_ = T(lambda e: e.transpose(q_bank.ap[:, 0:P], qk.ap[:, 0:D], ident), f, q_bank.free)
                qt = S(lambda e: e.copy(qT.ap, q_bank.ap[:, 0:P]), mq_, qT.free)
                q_bank.free = [qt]
            ps, last = [], None
            for g in range(LH // GRP):
                bank = half_banks[(t * (LH // GRP) + g) % len(half_banks)]
                mm = T(lambda e, g=g, bank=bank: e.matmul(bank.ap[:, 0:GW], upto, kv.ap[:, g * GW:(g + 1) * GW],
                                                          start=True, stop=True), o, bank.free, loaded["upto"])
                qh = heads_of(qk.ap[:, g * GRP * LD:(g + 1) * GRP * LD], LD)
                last = V(lambda e, g=g, bank=bank, qh=qh: e.tensor_tensor(
                    prod_buf.ap[:, g * GW:(g + 1) * GW].rearrange("p (h c d) -> p h c d", h=GRP, c=LE),
                    bank.ap[:, 0:GW].rearrange("p (h c d) -> p h c d", h=GRP, c=LE),
                    qh.unsqueeze(2).to_broadcast([P, GRP, LE, LD]), ALU.mult), mm, prod_buf.free)
                bank.free = [last]
                ps.append(last)
            kv.free = [mm]
            red = V(lambda e: e.tensor_reduce(total.ap, prod_buf.ap.rearrange("p (c d) -> p c d", d=LD), AX.X, ALU.add),
                    ps, total.free)
            prod_buf.free = [red]
            users = [mm, last]
            if c > 0:
                mi = T(lambda e: e.matmul(inter_bank.ap[:, 0:LH * LE], qT.ap, old.ap, start=True, stop=True),
                       qt, state_ready[t], inter_bank.free)
                qT.free = [mi]
                red = V(lambda e: e.tensor_tensor(total.ap, total.ap, inter_bank.ap[:, 0:LH * LE], ALU.add), mi, red)
                inter_bank.free = [red]
                old.free = [mi]
                users.append(mq_)
            if c < TPB - 1:
                ms = T(lambda e: e.matmul(inter_bank.ap[:, 0:LH * LE], qk.ap[:, D:2 * D], v.ap, start=True, stop=True),
                       f, vc, v_one, inter_bank.free)
                users.append(ms)
                dst = new_buf if c > 0 else new
                m = V(lambda e: e.tensor_tensor(dst.ap, inter_bank.ap[:, 0:LH * LE], head_mask, ALU.mult), ms, dst.free,
                      loaded["head_mask"])
                inter_bank.free = [m]
                if c > 0:
                    m = G(lambda e: e.tensor_tensor(new.ap, old.ap, new_buf.ap, ALU.add), m, new.free)
                    new_buf.free = [m]
                    old.free = [mi, m]
                state_ready[t + 1] = m
            qk.free = list(users)
            v.free = [o] + users
            part[t] = red

        def l1_output(t):
            b, c = divmod(t, TPB)
            total = sum_buf[t % 2]
            th = heads_of(total.ap, LE)
            n = V(lambda e: e.tensor_scalar(norm_buf.ap, th[:, :, LD], LEPS, None, ALU.add), part[t], norm_buf.free)
            r = V(lambda e: e.reciprocal(inv_buf.ap, norm_buf.ap), n, inv_buf.free)
            norm_buf.free = [r]
            o = V(lambda e: e.tensor_tensor(heads_of(o_buf.ap, LD), th[:, :, 0:LD],
                                            inv_buf.ap.unsqueeze(2).to_broadcast([P, LH, LD]), ALU.mult), r, o_buf.free)
            inv_buf.free = total.free = [o]
            mt = T(lambda e: e.transpose(out_bank.ap[:, 0:P], o_buf.ap, ident), o, out_bank.free)
            o_buf.free = [mt]
            w = S(lambda e: e.copy(oT_buf.ap, out_bank.ap[:, 0:P]), mt, oT_buf.free)
            mm = T(lambda e: e.matmul(out_bank.ap[:, P:2 * P], oT_buf.ap, wout, start=True, stop=True), w, loaded["wout"])
            oT_buf.free = [mm]
            xt = x_sb[:, t, :]
            x = V(lambda e: e.tensor_tensor(xt, xt, out_bank.ap[:, P:2 * P], ALU.add), mm, l1_ready[b])
            out_bank.free = [x]
            l1_done.setdefault(b, []).append(x)

        state_ready, l1_done = {}, {}

        class Experts1(Experts):
            def steps(self, b):
                tiles = slice(b * TPB, (b + 1) * TPB)
                r0, r1 = self.rec[b % 2]

                def norms():
                    self.stats = norm_stats(lambda j: x_sb[:, b * TPB + j, :], l1_done[b])

                def apply():
                    rows = norm_apply(self.stats, 0, lambda j: r0.ap[:, j, 0:D], lambda j: x_sb[:, b * TPB + j, :], r0.free)
                    self.rec_ok = [rows, G(lambda e: e.tensor_copy(r1.ap[:, :, 0:D], r0.ap[:, :, 0:D]), rows, r1.free)]
                    self.rec_ok += [G(lambda e, c=c, r=r: e.tensor_copy(r.ap[:, :, D + 1].bitcast(I32), token_id[:, c, tiles]),
                                      loaded["token_id"], r.free) for c, r in ((0, r0), (1, r1))]

                def choose():
                    t, w = transposes(z1T.ap, lambda j: r0.ap[:, j, 0:D], self.rec_ok[0], z1T.free, bank=out_bank)
                    bank = out_bank
                    mm = [T(lambda e, j=j: e.matmul(bank.ap[:, j * NE:(j + 1) * NE], z1T.ap[:, j * P:(j + 1) * P],
                                                    wg, start=True, stop=True), w, bank.free, loaded["wg"])
                          for j in range(TPB)]
                    z1T.free = [mm[-1]]
                    lg3 = bank.ap[:, 0:TPB * NE].rearrange("p (t n) -> p t n", t=TPB)
                    row = lambda m: m.unsqueeze(2).to_broadcast([P, TPB, NE])
                    m = V(lambda e: e.tensor_reduce(self.gate, lg3, AX.X, ALU.max), mm[-1], self.gate_ready)
                    d = V(lambda e: e.tensor_tensor(self.logits, lg3, row(self.gate), ALU.subtract), m, self.chain)
                    bank.free = [d]
                    x = S(lambda e: e.activation(self.logits, self.logits, ACT.Exp), d)
                    u = V(lambda e: e.tensor_reduce(self.gate, self.logits, AX.X, ALU.add), x, d)
                    i_ = V(lambda e: e.reciprocal(self.gate, self.gate), u)
                    self.logits_ready = V(lambda e: e.tensor_tensor(self.logits, self.logits, row(self.gate), ALU.mult), i_)
                    self.gate_ready = [self.logits_ready]
                    self.choose_top(b)
                    self.rec_ok += [V(lambda e, c=c, r=r: e.tensor_copy(r.ap[:, :, D], self.top[:, :, c]), self.top_ready, r.free)
                                    for c, r in ((0, r0), (1, r1))]

                def send():
                    self.send(b, out_bank, self.rec_ok)
                    self.chain += self.rec_ok[-2:]

                return [norms, apply, choose, send]

        experts1 = Experts1(1, 2, w1_mem1, w2_mem, b1_0, b2_mem1, [], ACT.Gelu_apprx_tanh,
                            sb("gate1", [P, TPB]), [], moe_work, ())
        experts1.residual = []
        load("w1_1", None, place=w1_mem1, after=[p.free for p in prob])
        load("w2_1", None, place=w2_mem, after=experts0.ended)
        spread("b1_1", NE * FF, place=b1_0, after=experts0.ended)
        spread("b2_1", NE * D, place=b2_mem1, after=[p.free for p in prob])
        experts1.weights_ready = [loaded[n] for n in ("w1_1", "w2_1", "b1_1", "b2_1")]

        later = []
        l1_tokens(0)
        for t in range(NT + 2):
            if t < NT:
                l1_features(t)
            if t % TPB == 1 and t // TPB + 1 < BATCH:
                l1_tokens(t // TPB + 1)
            if 1 <= t <= NT:
                l1_sums(t - 1)
            if t >= 2:
                l1_output(t - 2)
                if (t - 2) % TPB == TPB - 1:
                    later += experts1.steps((t - 2) // TPB)
            if later:
                later.pop(0)()
        for step in later:
            step()

        experts1.work_free = [l1_done[b] for b in l1_done] + [half_banks[i].free for i in range(3)]
        experts1.plan(out_bank)
        banks = [spare, qkv_bank, q_bank, inter_bank, out_bank] + half_banks
        experts1.blocks(banks)

        out_rows = out.rearrange("b (t p) d -> p (b t) d", p=P)
        for b in range(BATCH):
            sl = slice(b * TPB, (b + 1) * TPB)
            w = collect(experts1, b, l1_done[b])
            q.dma("sync", f"out{b}", lambda e, sl=sl: e.dma_start(out_rows[:, sl, :], x_sb[:, sl, :]), w)
        q.emit(ctx.enter_context(nc.Block()))


def lay_out(i):
    r = {k: np.asarray(v) for k, v in i.items()}
    f = lambda name: r[name]
    z = lambda *s: np.zeros(s, np.float32)
    o = {"x": f("L0_attn_h_t").reshape(TOK, D)}
    o["ident"] = np.eye(P, dtype=np.float32)
    wdq, bdq = f("L0_attn_W_DQ"), f("L0_attn_b_DQ")
    o["wq"] = np.concatenate([wdq, wdq, wdq, z(D, P - 3 * DC)], 1)
    o["bq"] = np.concatenate([bdq, bdq, bdq, np.ones(2, np.float32), z(P - 3 * DC - 2)])[:, None]
    o["wk"] = np.concatenate([f("L0_attn_W_DKV"), f("L0_attn_W_KR"), z(D, 1)], 1)
    o["bk"] = np.concatenate([f("L0_attn_b_DKV"), f("L0_attn_b_KR"), np.ones(1, np.float32)])[:, None]
    o["bkv"] = f("L0_attn_b_DKV")[None]
    lo = z(P, 2)
    lo[2 * DC:3 * DC, 0] = -1.0
    lo[DC:2 * DC, 1] = -1.0
    lo[ROW_ONE + 1, 1] = -1.0
    o["lo_rows"] = lo
    per_head = lambda w: w.reshape(w.shape[0], HEADS, -1)
    uk, uq, uv = (per_head(f(f"L0_attn_W_{n}")) for n in ("UK", "UQ", "UV"))
    qr = per_head(f("L0_attn_W_QR"))
    buk, buq, buv, bqr = (f(f"L0_attn_b_{n}").reshape(HEADS, -1) for n in ("UK", "UQ", "UV", "QR"))
    o["mk"] = np.concatenate([uk.transpose(2, 1, 0), z(DK, HEADS, DR), buk.T[:, :, None]], 2)
    t = uq.transpose(2, 1, 0)
    o["mq"] = np.concatenate([t, t, t, buq.T[:, :, None], buq.T[:, :, None], z(DK, HEADS, P - ROW_MHI)], 2)
    rk = z(DR + 1, KSIDE)
    rk[0:DR, DC:DC + DR] = np.eye(DR)
    rk[DR, KSIDE - 1] = 1.0
    o["rk"] = rk
    t = qr.transpose(2, 1, 0)
    sel = z(1, HEADS, P)
    for h in range(HEADS):
        sel[0, h, ROW_MHI + h] = sel[0, h, ROW_MLO + h] = 1.0
    o["rq"] = np.concatenate([np.concatenate([t, t, t, bqr.T[:, :, None], bqr.T[:, :, None],
                                              z(DR, HEADS, P - ROW_MHI)], 2), sel], 0)
    o["wuv"] = uv.transpose(2, 1, 0)
    o["buv"] = buv.T
    o["wo"] = f("L0_attn_W_O").reshape(HEADS, DK, D).transpose(1, 0, 2)
    o["bo"] = f("L0_attn_b_O")[None]
    i = np.arange(P)
    o["upto"] = (i[:, None] <= i[None, :]).astype(np.float32)
    o["choice"] = np.tile(np.concatenate([np.arange(NE), np.arange(NE) * REGION]).astype(np.float32), (P, 1))
    o["token_id"] = (np.arange(2)[None, :, None] * TOK + np.arange(NT)[None, None, :] * P + i[:, None, None]).astype(np.int32)
    pad = z(P, REC)
    pad[:, D + 1:D + 2] = np.full((P, 1), SKIP, np.int32).view(np.float32)
    o["pad_rec"] = pad
    for n, k in ((0, 1), (1, 2)):
        o[f"block_no{n}"] = np.tile(np.arange(n_blocks(k), dtype=np.float32)[:, None], (1, NE))[None]
    o["centroids"] = f("L0_ffn_centroids").T
    o["ln_g"], o["ln_b"] = f("L0_ffn_ln_g").T, f("L0_ffn_ln_b").T
    o["w1_0"] = f("L0_ffn_w1").transpose(2, 0, 1).reshape(D, NE * FF)
    o["w2_0"] = f("L0_ffn_w2").transpose(2, 0, 1).reshape(FC, P, NE, D).transpose(1, 2, 0, 3).reshape(P, NE * FF)
    o["b1_0"], o["b2_0"] = f("L0_ffn_b1").reshape(1, -1), f("L0_ffn_b2").reshape(1, -1)
    o["wqkv"], o["bqkv"] = f("L1_attn_w_qkv").T, f("L1_attn_b_qkv")[None]
    o["wout"], o["bout"] = f("L1_attn_w_out").T, f("L1_attn_b_out")[None]
    o["head_mask"] = (i[:, None] // LD == np.arange(LH * LE)[None, :] // LE).astype(np.float32)
    o["wg"] = f("L1_ffn_Wg")
    o["w1_1"] = f("L1_ffn_W1").transpose(1, 0, 2).reshape(D, NE * FF)
    o["w2_1"] = f("L1_ffn_W2").reshape(NE, FC, P, D).transpose(2, 0, 1, 3).reshape(P, NE * FF)
    o["b1_1"], o["b2_1"] = f("L1_ffn_b1").reshape(1, -1), f("L1_ffn_b2").reshape(1, -1)
    return {k: np.ascontiguousarray(v) for k, v in o.items()}


def kernel(**inputs):
    import concourse.bacc as bacc
    from concourse.bass_utils import run_bass_kernel_spmd

    nc = bacc.Bacc("TRN2", target_bir_lowering=False, num_devices=1)
    arrays = lay_out(inputs)
    aps = {k: nc.dram_tensor(f"in_{k}", v.shape, mybir.dt.from_np(v.dtype), kind="ExternalInput").ap()
           for k, v in arrays.items()}
    out = nc.dram_tensor("out_0", (BATCH, SEQ, D), F32, kind="ExternalOutput").ap()
    build(nc, aps, out)
    r = run_bass_kernel_spmd(nc, [{f"in_{k}": v for k, v in arrays.items()}], core_ids=[0])
    return r.results[0]["out_0"]
```

```python
from contextlib import ExitStack
import math

import numpy as np
import concourse.bass as bass
from concourse import mybir

F32 = mybir.dt.float32
F32R = mybir.dt.float32r
BF16 = mybir.dt.bfloat16
I32 = mybir.dt.int32
U32 = mybir.dt.uint32
ALU = mybir.AluOpType
ACT = mybir.ActivationFunctionType
AX = mybir.AxisListType

P = 128
BATCH, SEQ, D = 4, 512, 128
TOK = BATCH * SEQ
NT = TOK // P
TPB = SEQ // P
HEADS, DK, DC, DR = 8, 128, 32, 32
SCORE_SCALE = 1.0 / math.sqrt(DK + DR)
EPS = 1e-5

ROW_ONE = 3 * DC
ROW_MHI = ROW_ONE + 2
ROW_MLO = ROW_MHI + HEADS
SCORE_K = ROW_MHI
SHIFT_K = ROW_MLO + HEADS
KSIDE = DC + DR + 1
QUAD = 4

LH, LD = 16, 8
LE = LD + 1
LEPS = 1e-6
GRP = 4
GW = GRP * LE * LD

NE, FF = 8, 512
FC = FF // P
REC = D + 2
REGION = TOK + P
PAD_ROW = NE * REGION
SKIP = 1 << 20


def n_blocks(k):
    return (k * TOK) // P + NE - 1


def flat(x):
    if x is None:
        return []
    if isinstance(x, dict):
        return [x]
    return [t for y in x for t in flat(y)]


class Queues:

    def __init__(self, nc, ctx):
        self.nc, self.ctx = nc, ctx
        self.items = {e: [] for e in ("sync", "scalar", "vector", "gpsimd", "tensor")}
        self.done = {e: ctx.enter_context(nc.semaphore(f"done_{e}")) for e in self.items if e != "sync"}
        self.slots = {}

    def put(self, engine, fn, after, token):
        after = flat(after)
        for t in after:
            t["needed"] = True
        self.items[engine].append((fn, after, token))
        return token

    def add(self, engine, fn, after=()):
        return self.put(engine, fn, after, {"dma": False, "needed": False, "sem": None, "value": None})

    def dma(self, engine, slot, fn, after=()):
        if slot not in self.slots:
            self.slots[slot] = [self.ctx.enter_context(self.nc.semaphore(f"dma_{slot}")), 0]
        self.slots[slot][1] += 16
        token = {"dma": True, "needed": True, "sem": self.slots[slot][0], "value": self.slots[slot][1]}
        return self.put(engine, fn, after, token)

    def emit(self, block):
        for engine, items in self.items.items():
            count = 0
            for _, _, t in items:
                if t["needed"] and not t["dma"]:
                    count += 1
                    t["sem"], t["value"] = self.done[engine], count

        def play(engine, items):
            def body(eng):
                seen = {}
                for fn, after, token in items:
                    need = {}
                    for t in after:
                        if t["value"] > seen.get(t["sem"].name, 0):
                            seen[t["sem"].name] = t["value"]
                            need[t["sem"].name] = (t["sem"], t["value"])
                    for sem, value in need.values():
                        eng.wait_ge(sem, value)
                    ins = fn(eng)
                    if token["needed"]:
                        ins.then_inc(token["sem"], 16 if token["dma"] else 1)
                if engine == "sync":
                    for sem, value in self.slots.values():
                        eng.wait_ge(sem, value)
            return body

        block.sync(play("sync", self.items["sync"]))
        block.scalar(play("scalar", self.items["scalar"]))
        block.vector(play("vector", self.items["vector"]))
        block.gpsimd(play("gpsimd", self.items["gpsimd"]))
        block.tensor(play("tensor", self.items["tensor"]))


class Buffer:

    def __init__(self, ap):
        self.ap, self.free = ap, []


def build(nc, a, out):
    ctx = ExitStack()
    with ctx:
        q = Queues(nc, ctx)

        def sb(name, shape, dt=F32):
            return ctx.enter_context(nc.sbuf_tensor(name, shape, dt))[:]

        def V(fn, *after):
            return q.add("vector", fn, after)

        def S(fn, *after):
            return q.add("scalar", fn, after)

        def G(fn, *after):
            return q.add("gpsimd", fn, after)

        def T(fn, *after):
            return q.add("tensor", fn, after)

        psum = ctx.enter_context(nc.psum_tensor("psum", [P, 8, 512], F32))[:]

        loaded = {}

        def load(name, shape, dt=F32, place=None, after=()):
            t = sb(name, shape, dt) if place is None else place
            loaded[name] = q.dma("sync", name, lambda e: e.dma_start(t, a[name]), after)
            return t

        def spread(name, n, place=None, after=()):
            t = sb(name, [P, n]) if place is None else place
            loaded[name] = q.dma("sync", name, lambda e: e.dma_start(t, a[name].to_broadcast([P, n])), after)
            return t

        early = sb("early", [P, 5 * 1024])
        probs_mem = sb("probs_mem", [P, HEADS * TPB * SEQ])

        def carve(region, sizes):
            at, pieces = 0, []
            for n in sizes:
                pieces.append(region[:, at:at + n])
                at += n
            assert at <= region.shape[1]
            return pieces

        x_sb = sb("x", [P, NT, D])
        x_rows = a["x"].rearrange("(t p) d -> p t d", p=P)
        x_in = []
        for b in range(BATCH):
            sl = slice(b * TPB, (b + 1) * TPB)
            x_in.append(q.dma("sync", f"x{b}", lambda e, sl=sl: e.dma_start(x_sb[:, sl, :], x_rows[:, sl, :])))
            if b == 0:
                ident = load("ident", [P, P])
                wq = load("wq", [P, P])
                bq = load("bq", [P, 1])
                wk = load("wk", [P, KSIDE])
                bk = load("bk", [KSIDE, 1])
                bkv = spread("bkv", DC)
                lo_rows = load("lo_rows", [P, 2])
                mk_m, mq_m, rq_m, buv_m, wo_m = carve(early, [HEADS * KSIDE] + 4 * [HEADS * P])
                heads = lambda m: m.rearrange("p (h c) -> p h c", h=HEADS)
                mk = load("mk", None, place=heads(mk_m))
                mq = load("mq", None, place=heads(mq_m))
                rk = load("rk", [DR + 1, KSIDE])
                rq = load("rq", None, place=heads(rq_m)[0:DR + 1])
        wuv = load("wuv", [P, HEADS, DC])
        buv = load("buv", [P, HEADS])
        wo = load("wo", None, place=heads(wo_m))
        bo = load("bo", [1, D])
        upto = load("upto", [P, P])
        before = sb("before", [P, P], BF16)
        before_set = V(lambda e: e.tensor_tensor(before, upto, ident, ALU.subtract), loaded["upto"], loaded["ident"])
        ones_bf = sb("ones_bf", [P, P], BF16)
        ones_bf_set = V(lambda e: e.memset(ones_bf, 1.0))
        choice = load("choice", [P, 2 * NE])
        token_id = load("token_id", [P, 2, NT], I32)
        pad_rec = load("pad_rec", [P, REC])
        wqkv, bqkv = load("wqkv", [D, 3 * D]), load("bqkv", [1, 3 * D])
        wout, bout = load("wout", [D, D]), load("bout", [1, D])
        head_mask = load("head_mask", [P, LH * LE])
        wg = load("wg", [D, NE])

        half = sb("half", [P, TPB])
        half_set = G(lambda e: e.memset(half, -0.5))
        ones_row = sb("ones_row", [1, P])
        ones_row_set = G(lambda e: e.memset(ones_row, 1.0))

        score_banks = [Buffer(psum[:, i, :]) for i in range(3)]
        shift_banks = [Buffer(psum[:, 3 + i, :]) for i in range(2)]
        num_bank, den_bank = Buffer(psum[:, 5, :]), Buffer(psum[:, 6, :])
        misc = Buffer(psum[:, 7, :])

        ln_stats = [sb(f"ln_stats{i}", [P, TPB, 6]) for i in range(2)]
        ln_mv = [Buffer(sb(f"ln_mv{i}", [P, TPB, 2])) for i in range(2)]
        ln_scale = [sb(f"ln_scale{i}", [P, TPB, 4]) for i in range(2)]
        ln_count = [0]

        def norm_stats(src, ready, twice=False):
            i = ln_count[0] % 2
            ln_count[0] += 1
            mv, stats, sc = ln_mv[i], ln_stats[i], ln_scale[i]
            st = [V(lambda e, j=j: e.bn_stats(stats[:, j, :], src(j)), ready, mv.free) for j in range(TPB)]
            ag = [V(lambda e, j=j: e.bn_aggr(mv.ap[:, j, :], stats[:, j, :]), st[j]) for j in range(TPB)]
            var, tmp = mv.ap[:, :, 1], sc[:, :, 2]
            t = G(lambda e: e.tensor_scalar(tmp, var, EPS, None, ALU.add), ag, mv.free)
            rs = [G(lambda e: e.tensor_tensor(sc[:, :, 0], tmp, half, ALU.pow), t, half_set)]
            if twice:
                t = G(lambda e: e.tensor_tensor(tmp, var, sc[:, :, 0], ALU.mult), rs)
                t = G(lambda e: e.tensor_tensor(tmp, tmp, sc[:, :, 0], ALU.mult), t)
                t = G(lambda e: e.tensor_scalar(tmp, tmp, EPS, None, ALU.add), t)
                t = G(lambda e: e.tensor_tensor(tmp, tmp, half, ALU.pow), t)
                rs.append(G(lambda e: e.tensor_tensor(sc[:, :, 1], tmp, sc[:, :, 0], ALU.mult), t))
            mv.free = []
            return mv, sc, rs

        def norm_apply_scalar(stats, dst, src, dst_free=()):
            mv, sc, rs = stats
            m = V(lambda e: e.scalar_tensor_tensor(sc[:, :, 3], mv.ap[:, :, 0], -1.0, sc[:, :, 0], ALU.mult, ALU.mult), rs)
            w = [S(lambda e, j=j: e.activation(dst(j), src(j), ACT.Identity, bias=sc[:, j, 3:4], scale=sc[:, j, 0:1]),
                   m, dst_free) for j in range(TPB)]
            mv.free += w
            return w

        def norm_apply(stats, which, dst, src, dst_free=(), engine=V):
            mv, sc, rs = stats
            w = [engine(lambda e, j=j: e.tensor_scalar(dst(j), src(j), mv.ap[:, j, 0:1], sc[:, j, which:which + 1],
                                                       ALU.subtract, ALU.mult), rs, dst_free) for j in range(TPB)]
            mv.free += w
            return w

        m_sb = sb("m_absorbed", [KSIDE, HEADS, P])
        m_ready = []

        def absorb(h0):
            mm = None
            for h in range(h0, h0 + 4):
                o = misc.ap[0:KSIDE, (h - h0) * P:(h - h0 + 1) * P]
                T(lambda e, h=h, o=o: e.matmul(o, mk[:, h, :], mq[:, h, :], start=True, stop=False),
                  misc.free, loaded["mk"], loaded["mq"])
                mm = T(lambda e, h=h, o=o: e.matmul(o, rk, rq[:, h, :], start=False, stop=True),
                       loaded["rk"], loaded["rq"])
            w = S(lambda e: e.copy(m_sb[:, h0:h0 + 4, :], misc.ap[0:KSIDE, :].rearrange("p (h c) -> p h c", h=4)), mm)
            misc.free = [w]
            m_ready.append(w)

        wvo = sb("wvo", [P, 2, D])
        bvo = sb("bvo", [P, D])
        buv_wide = heads(buv_m)

        def absorb_values():
            wide = [G(lambda e, h=h: e.tensor_copy(buv_wide[:, h, :], buv[:, h:h + 1].to_broadcast([P, P])),
                      loaded["buv"]) for h in range(HEADS)]
            mm = None
            for h in range(HEADS):
                g, r = divmod(h, 4)
                mm = T(lambda e, h=h, g=g, r=r: e.matmul(misc.ap[r * DC:(r + 1) * DC, g * D:(g + 1) * D], wuv[:, h, :],
                                                         wo[:, h, :], start=True, stop=True),
                       misc.free, loaded["wuv"], loaded["wo"])
            for h in range(HEADS):
                T(lambda e, h=h: e.matmul(misc.ap[:, 2 * D:3 * D], buv_wide[:, h, :], wo[:, h, :],
                                          start=(h == 0), stop=False), wide)
            mm = T(lambda e: e.matmul(misc.ap[:, 2 * D:3 * D], ones_row, bo, start=False, stop=True),
                   ones_row_set, loaded["bo"])
            w1 = V(lambda e: e.tensor_copy(wvo, misc.ap[:, 0:2 * D].rearrange("p (g d) -> p g d", g=2)), mm)
            w2 = V(lambda e: e.tensor_copy(bvo, misc.ap[:, 2 * D:3 * D]), mm)
            misc.free = [w1, w2]
            return [w1, w2]

        z = [Buffer(sb(f"z{i}", [P, TPB, D])) for i in range(2)]
        zT = [Buffer(sb(f"zT{i}", [P, SEQ])) for i in range(2)]
        q_full = sb("q_full", [P, SEQ])
        q_hi = sb("q_hi", [P, SEQ], F32R)
        q_free = [[]]
        q_stack = [Buffer(sb(f"q_stack{i}", [P, SEQ], F32R)) for i in range(3)]
        k_side = [Buffer(sb(f"k_side{i}", [KSIDE, SEQ])) for i in range(2)]
        ckv = [Buffer(sb(f"ckv{i}", [P, TPB, DC])) for i in range(3)]
        ones_dc = sb("ones_dc", [P, DC])
        ones_dc_set = G(lambda e: e.memset(ones_dc, 1.0))
        u_hi = [Buffer(sb(f"u_hi{i}", [P, SEQ], F32R)) for i in range(2)]
        u_ring = [Buffer(sb(f"u_stack{i}", [P, SEQ], F32R)) for i in range(HEADS + 2)]
        u_stack = lambda b, h: u_ring[(b * HEADS + h) % len(u_ring)]
        q_ready, k_ready, c_ready, u_ready, zT_ready = {}, {}, {}, {}, {}
        z_ready = {}

        z_stats = {}

        def step_stats(b):
            z_stats[b] = norm_stats(lambda j: x_sb[:, b * TPB + j, :], x_in[b])

        def step_norm(b):
            zb = z[b % 2]
            z_ready[b] = norm_apply(z_stats[b], 0, lambda j: zb.ap[:, j, :], lambda j: x_sb[:, b * TPB + j, :], zb.free)

        def transposes(dst, src, ready, dst_free, bank=None):
            bank = bank or misc
            mm = [T(lambda e, j=j: e.transpose(bank.ap[:, j * P:(j + 1) * P], src(j), ident),
                    ready, bank.free, loaded["ident"]) for j in range(TPB)]
            w = S(lambda e: e.copy(dst, bank.ap), mm[-1], dst_free)
            bank.free = [w]
            return mm[-1], w

        def step_zT(b):
            zb, zt = z[b % 2], zT[b % 2]
            t, w = transposes(zt.ap, lambda j: zb.ap[:, j, :], z_ready[b], zt.free)
            zb.free = [t]
            zT_ready[b] = w

        def step_q(b):
            zt, qs = zT[b % 2], q_stack[b % 3]
            mm = T(lambda e: e.matmul(misc.ap, wq, zt.ap, start=True, stop=True), zT_ready[b], misc.free, loaded["wq"])
            full = S(lambda e: e.activation(q_full, misc.ap, ACT.Identity, bias=bq), mm, loaded["bq"], q_free[0])
            misc.free = [full]
            hi = V(lambda e: e.tensor_copy(q_hi, q_full), full, q_free[0])
            w = V(lambda e: e.scalar_tensor_tensor(qs.ap, q_hi.bitcast(F32), lo_rows[:, 0:1], q_full, ALU.mult, ALU.add),
                  hi, loaded["lo_rows"], qs.free)
            q_free[0] = [w]
            q_ready[b] = w

        def step_k(b):
            zt, ks = zT[b % 2], k_side[b % 2]
            mm = T(lambda e: e.matmul(misc.ap[0:KSIDE, :], wk, zt.ap, start=True, stop=True),
                   zT_ready[b], misc.free, loaded["wk"])
            w = S(lambda e: e.activation(ks.ap, misc.ap[0:KSIDE, :], ACT.Identity, bias=bk), mm, loaded["bk"], ks.free)
            misc.free = [w]
            k_ready[b] = w

        def step_ckv(b):
            zt, c = zT[b % 2], ckv[b % 3]
            mm = [T(lambda e, j=j: e.matmul(misc.ap[:, j * DC:(j + 1) * DC], zt.ap[:, j * P:(j + 1) * P], wk[:, 0:DC],
                                            start=True, stop=True), zT_ready[b], misc.free) for j in range(TPB)]
            w = V(lambda e: e.tensor_tensor(c.ap, misc.ap[:, 0:TPB * DC].rearrange("p (t c) -> p t c", t=TPB),
                                            bkv.unsqueeze(1).to_broadcast([P, TPB, DC]), ALU.add),
                  mm[-1], loaded["bkv"], c.free)
            misc.free = [w]
            zt.free = [mm[-1]]
            c_ready[b] = w

        def step_u(b, h):
            ks, us, uh = k_side[b % 2], u_stack(b, h), u_hi[h % 2]
            mm = T(lambda e: e.matmul(misc.ap, m_sb[:, h, :], ks.ap, start=True, stop=True),
                   k_ready[b], m_ready[h // 4], misc.free)
            hi = S(lambda e: e.copy(uh.ap, misc.ap), mm, uh.free)
            w = V(lambda e: e.scalar_tensor_tensor(us.ap, uh.ap.bitcast(F32), lo_rows[:, 1:2], misc.ap,
                                                   ALU.mult, ALU.add), hi, us.free)
            misc.free = [w]
            uh.free = [w]
            ks.free = [mm]
            u_ready[b, h] = w

        neg_max = [Buffer(sb(f"neg_max{i}", [P, TPB, HEADS])) for i in range(2)]
        max_ready = {}

        score_turn = [0]

        def step_scores(b, h, tiles):
            qs, us, nm = q_stack[b % 3], u_stack(b, h), neg_max[b % 2]
            for j in tiles:
                bank = score_banks[score_turn[0] % len(score_banks)]
                score_turn[0] += 1
                mm = T(lambda e, j=j, bank=bank: e.matmul(bank.ap, qs.ap[0:SCORE_K, j * P:(j + 1) * P],
                                                          us.ap[0:SCORE_K, :], start=True, stop=True),
                       q_ready[b], u_ready[b, h], bank.free)
                w = V(lambda e, j=j, bank=bank: e.tensor_reduce(nm.ap[:, j, h:h + 1], bank.ap, AX.X, ALU.max, negate=True),
                      mm, nm.free)
                bank.free = [w]
                max_ready.setdefault(b, []).append(w)

        max_hi = sb("max_hi", [P, TPB, HEADS], F32R)
        max_tile = sb("max_tile", [P, TPB, P])
        mt_zero = G(lambda e: e.memset(max_tile, 0.0))
        mt_ones = G(lambda e: e.memset(max_tile[:, :, ROW_ONE:ROW_MHI], 1.0), mt_zero)
        mt_free = [[mt_ones]]
        shift_ready = {}

        def step_shift(b):
            nm, qs = neg_max[b % 2], q_stack[b % 3]
            hi = V(lambda e: e.tensor_copy(max_hi, nm.ap), max_ready[b], mt_free[0])
            w1 = V(lambda e: e.tensor_copy(max_tile[:, :, ROW_MHI:ROW_MLO], max_hi.bitcast(F32)), hi, mt_free[0])
            w2 = V(lambda e: e.tensor_tensor(max_tile[:, :, ROW_MLO:SHIFT_K], nm.ap, max_hi.bitcast(F32), ALU.subtract), hi)
            nm.free = [w2]
            mm = [T(lambda e, j=j: e.transpose(misc.ap[:, j * P:(j + 1) * P], max_tile[:, j, :], ident),
                    w1, w2, misc.free) for j in range(TPB)]
            w = V(lambda e: e.tensor_copy(qs.ap[ROW_ONE:P, :], misc.ap[ROW_ONE:P, :]), mm[-1], max_ready[b])
            misc.free = [w]
            mt_free[0] = [w2, mm[-1]]
            shift_ready[b] = w

        prob = [Buffer(m.rearrange("p (t s) -> p t s", t=TPB)) for m in carve(probs_mem, HEADS * [TPB * SEQ])]
        oT = [Buffer(sb(f"oT{g}", [P, SEQ])) for g in range(2)]
        den_t, inv_col, inv_den = sb("den_t", [P, SEQ]), sb("inv_col", [P, SEQ // DC]), sb("inv_den", [P, SEQ])
        prob_ready, oT_ready = {}, {}

        def step_exp(b, h, tiles):
            qs, us, pr = q_stack[b % 3], u_stack(b, h), prob[h]
            for j in tiles:
                bank = shift_banks[j % 2]
                mm = T(lambda e, j=j, bank=bank: e.matmul(bank.ap, us.ap[0:SHIFT_K, j * P:(j + 1) * P],
                                                          qs.ap[0:SHIFT_K, :], start=True, stop=True),
                       shift_ready[b], u_ready[b, h], bank.free)
                x = S(lambda e, j=j, bank=bank: e.activation(pr.ap[:, j, :], bank.ap, ACT.Exp, scale=SCORE_SCALE),
                      mm, pr.free)
                bank.free = [x]
                prob_ready.setdefault((b, h), []).append(x)
            us.free = [mm]
            qs.free = [mm]

        def step_values(b, g, j, part):
            c = ckv[b % 3]
            bank = (num_bank, den_bank)[part]
            for r in range(QUAD):
                pr = prob[g * QUAD + r]
                lhs = c.ap[:, j, :] if part == 0 else ones_dc
                mm = T(lambda e, r=r, pr=pr, lhs=lhs: e.matmul(bank.ap[r * DC:(r + 1) * DC, :], lhs, pr.ap[:, j, :],
                                                               start=(j == 0), stop=(j == TPB - 1)),
                       [prob_ready[b, g * QUAD + x] for x in range(QUAD)], c_ready[b], ones_dc_set, bank.free)
            if (j, part) == (TPB - 1, 1):
                for r in range(QUAD):
                    prob[g * QUAD + r].free = [mm]
                c.free = [mm]
                t = V(lambda e: e.transpose(den_t, den_bank.ap), mm)
                den_bank.free = [t]
                r = V(lambda e: e.reciprocal(inv_col, den_t.rearrange("p (b c) -> p b c", c=DC)[:, :, 0]), t)
                t = V(lambda e: e.transpose(inv_den.rearrange("p (b c) -> p b c", c=DC),
                                            inv_col.unsqueeze(2).to_broadcast([P, SEQ // DC, DC])), r)
                w = V(lambda e: e.tensor_tensor(oT[g].ap, num_bank.ap, inv_den, ALU.mult), t, oT[g].free)
                num_bank.free = [w]
                oT_ready[b, g] = w

        res_ready = {}
        xb_ready = {}

        def step_residual_bias(b, bias_ready):
            for j in range(TPB):
                t = b * TPB + j
                w = G(lambda e, t=t: e.tensor_tensor(x_sb[:, t, :], x_sb[:, t, :], bvo, ALU.add),
                      bias_ready, z_ready[b])
                xb_ready.setdefault(b, []).append(w)

        def step_out(b):
            for j in range(TPB):
                for g in range(2):
                    mm = T(lambda e, j=j, g=g: e.matmul(misc.ap[:, j * P:(j + 1) * P], oT[g].ap[:, j * P:(j + 1) * P],
                                                        wvo[:, g, :], start=(g == 0), stop=(g == 1)),
                           oT_ready[b, 0], oT_ready[b, 1], misc.free, wvo_ready)
            oT[0].free = oT[1].free = [mm]
            xs = x_sb[:, b * TPB:(b + 1) * TPB, :]
            w = V(lambda e: e.tensor_tensor(xs, misc.ap.rearrange("p (t d) -> p t d", t=TPB), xs, ALU.add),
                  mm, xb_ready[b])
            misc.free = [w]
            res_ready[b] = w

        wide_free = [[]]

        class Experts:
            def __init__(self, n, k, w1, w2, b1, b2, weights_ready, func, gate, gate_ready, work, work_free):
                self.n, self.k, self.nb = n, k, n_blocks(k)
                self.w1, self.w2, self.b1, self.b2 = w1, w2, b1, b2
                self.weights_ready, self.func, self.gate, self.gate_ready = weights_ready, func, gate, gate_ready
                self.work, self.work_free = work, work_free
                self.records = nc.dram_tensor(f"records{n}", [PAD_ROW + P, REC], F32, kind="Internal").ap()
                self.outs = nc.dram_tensor(f"outs{n}", [k * TOK, D], F32, kind="Internal").ap()
                self.pad = q.dma("sync", f"pad{n}", lambda e: e.dma_start(self.records[PAD_ROW:PAD_ROW + P, :], pad_rec),
                                 loaded["pad_rec"])
                self.rec = [[Buffer(sb(f"rec{n}_{i}_{c}", [P, TPB, REC])) for c in range(k)] for i in range(2)]
                self.logits = sb(f"logits{n}", [P, TPB, NE])
                self.top = sb(f"top{n}", [P, TPB, NE])
                self.top_at = sb(f"top_at{n}", [P, TPB, NE], U32)
                self.pick = [sb(f"pick{n}_{c}", [P, TPB, NE]) for c in range(k)]
                self.pick_bf = sb(f"pick_bf{n}", [P, TPB, NE], BF16)
                self.seen = [sb(f"seen{n}_{i}", [P, NE], BF16) for i in range(2)]
                self.seen_f = sb(f"seen_f{n}", [P, NE])
                self.seen_set = [V(lambda e: e.memset(self.seen[0], 0.0))]
                self.rank = sb(f"rank{n}", [P, TPB, NE])
                self.rank_k = sb(f"rank_k{n}", [P, TPB, NE])
                self.row_f = sb(f"row_f{n}", [P, TPB])
                self.row = [sb(f"row{n}_{c}", [P, NT], I32) for c in range(k)]
                self.scattered = []
                self.chain = []

            def choose_top(self, b):
                mx = [V(lambda e, j=j: e.max(self.top[:, j, :], self.logits[:, j, :]), self.logits_ready, self.chain)
                      for j in range(TPB)]
                at = [V(lambda e, j=j: e.max_index(self.top_at[:, j, :], self.top[:, j, :], self.logits[:, j, :]), mx[j])
                      for j in range(TPB)]
                self.top_ready = mx
                self.pick_ready = [V(lambda e, c=c: e.tensor_tensor(
                    self.pick[c], choice[:, 0:NE].unsqueeze(1).to_broadcast([P, TPB, NE]),
                    self.top_at[:, :, c:c + 1].to_broadcast([P, TPB, NE]), ALU.is_equal),
                    at, loaded["choice"]) for c in range(self.k)]

            def send(self, b, bank, rec_ready):
                if self.k == 1:
                    bf = V(lambda e: e.tensor_copy(self.pick_bf, self.pick[0]), self.pick_ready, self.chain)
                else:
                    bf = V(lambda e: e.tensor_tensor(self.pick_bf, self.pick[0], self.pick[1], ALU.add),
                           self.pick_ready, self.chain)
                old, new = self.seen[b % 2], self.seen[(b + 1) % 2]
                for j in range(TPB):
                    o = bank.ap[:, j * NE:(j + 1) * NE]
                    mm = T(lambda e, o=o: e.matmul(o, ones_bf, old, start=True, stop=False),
                           bank.free, self.seen_set, ones_bf_set)
                    for i in range(j):
                        mm = T(lambda e, o=o, i=i: e.matmul(o, ones_bf, self.pick_bf[:, i, :], start=False, stop=False), bf)
                    mm = T(lambda e, o=o, j=j: e.matmul(o, before, self.pick_bf[:, j, :], start=False, stop=True),
                           bf, before_set)
                s1 = V(lambda e: e.tensor_reduce(self.seen_f, self.pick_bf.rearrange("p t n -> p n t"), AX.X, ALU.add), bf)
                self.seen_set = [V(lambda e: e.tensor_tensor(new, old, self.seen_f, ALU.add), s1, self.seen_set)]
                r = V(lambda e: e.tensor_tensor(self.rank, bank.ap[:, 0:TPB * NE].rearrange("p (t n) -> p t n", t=TPB),
                                                choice[:, NE:2 * NE].unsqueeze(1).to_broadcast([P, TPB, NE]), ALU.add), mm)
                bank.free = [r]
                done = [mm, s1]
                for c in range(self.k):
                    m = V(lambda e, c=c: e.tensor_tensor(self.rank_k, self.rank, self.pick[c], ALU.mult), r, done)
                    f = V(lambda e: e.tensor_reduce(self.row_f, self.rank_k, AX.X, ALU.add), m)
                    w = V(lambda e, c=c: e.tensor_copy(self.row[c][:, b * TPB:(b + 1) * TPB], self.row_f), f)
                    done = [mm, s1, w]
                    rec = self.rec[b % 2][c]
                    rec.free = []
                    for j in range(TPB):
                        t = b * TPB + j
                        d = q.dma("gpsimd", f"scatter{self.n}_{b % 2}{c}{j}", lambda e, c=c, j=j, t=t, rec=rec: e.indirect_dma_start(
                            self.records, bass.IndirectOffsetOnAxis(self.row[c][:, t:t + 1], 0), rec.ap[:, j, :], None),
                            [w, rec_ready])
                        rec.free.append(d)
                        self.scattered.append(d)
                self.chain = done

            def plan(self, bank):
                n, nb = self.n, self.nb
                one = lambda name, shape, dt=F32: sb(f"{name}{n}", shape, dt)
                block_no, is_from, is_upto, val = (m[0:1, 0:nb * NE].rearrange("p (b n) -> p b n", n=NE)
                                                   for m in (max_tile.rearrange("p t c -> p (t c)"), den_t, inv_den, q_full))
                load(f"block_no{n}", None, place=block_no, after=[mt_free[0], wide_free[0]])
                mm = T(lambda e: e.matmul(bank.ap[:, 0:NE], ones_bf, self.seen[BATCH % 2], start=True, stop=True),
                       self.seen_set, bank.free)
                count = one("count", [1, NE], I32)
                fill = one("fill", [1, NE], I32)
                blocks_i, blocks_f = one("blocks_i", [1, NE], I32), one("blocks_f", [1, NE])
                upto_e, from_e, base = one("upto_e", [1, NE]), one("from_e", [1, NE]), one("base", [1, NE])
                first = one("first", [1, nb])
                table = one("table", [1, 3, nb], I32)
                wide = lambda x: x.unsqueeze(1).to_broadcast([1, nb, NE])
                c1 = V(lambda e: e.tensor_scalar(count, bank.ap[0:1, 0:NE], float(P - 1), None, ALU.add), mm)
                c2 = V(lambda e: e.tensor_tensor(fill, bank.ap[0:1, 0:NE], choice[0:1, NE:2 * NE], ALU.add), mm)
                bank.free = [c1, c2]
                c3 = V(lambda e: e.tensor_scalar(blocks_i, count, P.bit_length() - 1, None, ALU.logical_shift_right), c1)
                c4 = V(lambda e: e.tensor_copy(blocks_f, blocks_i), c3)
                c5 = V(lambda e: e.tensor_tensor_scan(upto_e, ones_row[:, 0:NE], blocks_f, 0.0, ALU.mult, ALU.add),
                       c4, ones_row_set)
                c6 = V(lambda e: e.tensor_tensor(from_e, upto_e, blocks_f, ALU.subtract), c5)
                c7 = V(lambda e: e.scalar_tensor_tensor(base, from_e, -float(P), choice[0:1, NE:2 * NE], ALU.mult, ALU.add), c6)
                c8 = V(lambda e: e.tensor_tensor(is_upto, wide(upto_e), block_no, ALU.is_le), c5, loaded[f"block_no{n}"])
                c9 = V(lambda e: e.tensor_tensor(is_from, wide(from_e), block_no, ALU.is_le), c6)
                ca = V(lambda e: e.tensor_tensor(is_from, is_from, is_upto, ALU.subtract), c8, c9)
                cb = V(lambda e: e.scalar_tensor_tensor(val, block_no, float(P), wide(base), ALU.mult, ALU.add), c7)
                cc = V(lambda e: e.scalar_tensor_tensor(val, val, -float(PAD_ROW), is_from, ALU.add, ALU.mult), ca, cb)
                cd = V(lambda e: e.tensor_reduce(first, val, AX.X, ALU.add), cc)
                ce = V(lambda e: e.tensor_scalar(table[:, 0, :], first, float(PAD_ROW), None, ALU.add), cd)
                cf = V(lambda e: e.tensor_tensor(val, is_from, wide(choice[0:1, 0:NE]), ALU.mult), cd)
                cg = V(lambda e: e.tensor_reduce(first, val, AX.X, ALU.add), cf, ce)
                ch = V(lambda e: e.tensor_scalar(table[:, 1, :], first, float(FF), None, ALU.mult), cg)
                ci = V(lambda e: e.tensor_scalar(table[:, 2, :], first, float(D), None, ALU.mult), cg)
                self.table, self.table_ready = table, [ce, ch, ci]
                wide_free[0] = self.table_ready

                def pad(e, i):
                    at = e.value_load(fill[0:1, i:i + 1], min_val=0, max_val=PAD_ROW)
                    return e.dma_start(self.records[bass.ds(at, P), :], pad_rec)

                self.padded = [q.dma("sync", f"fill{n}_{i}", lambda e, i=i: pad(e, i), c2) for i in range(NE)]

            def blocks(self, banks):
                n, k, nb = self.n, self.k, self.nb
                IN = 12
                sizes = IN * [REC] + 2 * [P] + 2 * [FF] + 2 * [FF] + 2 * [D] + 4 * [D]
                m = [Buffer(x) for x in carve(self.work, sizes)]
                for x in m:
                    x.free = list(self.work_free)
                rec_in, xT, h_sb, hT, y_sb, out_sb = m[0:IN], m[IN:IN + 2], m[IN + 2:IN + 4], m[IN + 4:IN + 6], \
                    m[IN + 6:IN + 8], m[IN + 8:IN + 12]
                x_bank, h_banks, hT_banks, y_banks = banks[0], banks[1:3], banks[3:5], banks[5:7]
                w1, w2 = self.w1, self.w2
                got, xt, h_ok, hT_ok = {}, {}, {}, {}
                self.sent = []

                def fetch(i):
                    r = rec_in[i % IN]

                    def go(e):
                        at = e.value_load(self.table[0:1, 0, i:i + 1], min_val=0, max_val=PAD_ROW)
                        return e.dma_start(r.ap, self.records[bass.ds(at, P), :])

                    got[i] = q.dma("sync", f"fetch{n}_{i % IN}", go, [self.table_ready, self.padded, self.scattered, self.pad, r.free])

                def turn(i):
                    r, x = rec_in[i % IN], xT[i % 2]
                    mm = T(lambda e: e.transpose(x_bank.ap[:, 0:P], r.ap[:, 0:D], ident), got[i], x_bank.free)
                    w = S(lambda e: e.copy(x.ap, x_bank.ap[:, 0:P]), mm, x.free)
                    x_bank.free = [w]
                    xt[i] = [w, mm]

                at_tensor, at_vector = {}, {}

                def look(i):
                    if i >= nb:
                        return

                    def entries(e, rows, at):
                        at[i] = [e.snap(e.value_load(self.table[0:1, r, i:i + 1], min_val=0, max_val=(NE - 1) * w))
                                 for r, w in rows]

                    T(lambda e: entries(e, [(1, FF)], at_tensor), self.table_ready)
                    V(lambda e: entries(e, [(1, FF), (2, D)], at_vector), self.table_ready)

                def first(i):
                    x, h, bank = xT[i % 2], h_sb[i % 2], h_banks[i % 2]
                    mm = T(lambda e: e.matmul(bank.ap, x.ap, w1[:, bass.ds(at_tensor[i][0], FF)], start=True, stop=True),
                           xt[i], bank.free, self.weights_ready)
                    w = V(lambda e: e.tensor_tensor(h.ap, bank.ap, self.b1[:, bass.ds(at_vector[i][0], FF)], ALU.add),
                          mm, h.free, self.weights_ready)
                    x.free = [mm]
                    bank.free = [w]
                    h_ok[i] = w

                def middle(i):
                    h, ht, bank = h_sb[i % 2], hT[i % 2], hT_banks[i % 2]
                    mm = [T(lambda e, c=c: e.transpose(bank.ap[:, c * P:(c + 1) * P], h.ap[:, c * P:(c + 1) * P], ident),
                            h_ok[i], bank.free) for c in range(FC)]
                    w = S(lambda e: e.activation(ht.ap, bank.ap, self.func), mm[-1], ht.free)
                    h.free = [mm[-1]]
                    bank.free = [w]
                    hT_ok[i] = w

                def second(i):
                    ht, y, o, r, bank = hT[i % 2], y_sb[i % 2], out_sb[i % 4], rec_in[i % IN], y_banks[i % 2]

                    for c in range(FC):
                        mm = T(lambda e, c=c: e.matmul(bank.ap[:, 0:D], ht.ap[:, c * P:(c + 1) * P],
                                                       w2[:, bass.ds(at_tensor[i][0] + c * P, D)],
                                                       start=(c == 0), stop=(c == FC - 1)), hT_ok[i], bank.free)
                    w = V(lambda e: e.tensor_tensor(y.ap, bank.ap[:, 0:D], self.b2[:, bass.ds(at_vector[i][1], D)], ALU.add),
                          mm, y.free)
                    ht.free = [mm]
                    bank.free = [w]
                    g = S(lambda e: e.activation(o.ap, y.ap, ACT.Copy, scale=r.ap[:, D:D + 1]), w, o.free)
                    y.free = [g]
                    d = q.dma("gpsimd", f"send{n}_{i % 4}", lambda e: e.indirect_dma_start(
                        self.outs, bass.IndirectOffsetOnAxis(r.ap[:, D + 1:D + 2].bitcast(I32), 0), o.ap, None,
                        bounds_check=k * TOK - 1, oob_is_err=False), g)
                    o.free = [d]
                    r.free = [d]
                    self.sent.append(d)
                    self.ended = [mm, w, g]

                for i in range(IN):
                    fetch(i)
                turn(0)
                look(0)
                for i in range(nb + 2):
                    if i < nb:
                        first(i)
                    if i + 1 < nb:
                        turn(i + 1)
                    look(i + 1)
                    if 1 <= i <= nb:
                        middle(i - 1)
                    if i >= 2:
                        second(i - 2)
                    if 2 <= i and i - 2 + IN < nb:
                        fetch(i - 2 + IN)

        w2_mem, b2_mem0, b2_mem1, w1_mem1, moe_work = carve(
            probs_mem, [NE * FF, NE * D, NE * D, NE * FF, 6 * 1024])
        b1_0 = spread("b1_0", NE * FF)
        ln_g, ln_b = load("ln_g", [P, NE]), load("ln_b", [P, NE])
        centroids = load("centroids", [P, NE])
        z1 = [Buffer(sb(f"ffn_z{i}", [P, TPB, D])) for i in range(2)]
        z1T = Buffer(sb("ffn_zT", [P, SEQ]))

        class Experts0(Experts):
            def steps(self, b):
                tiles = slice(b * TPB, (b + 1) * TPB)

                def norms():
                    self.stats = norm_stats(lambda j: x_sb[:, b * TPB + j, :], res_ready[b], twice=True)

                def apply():
                    src = lambda j: x_sb[:, b * TPB + j, :]
                    self.z_ok = norm_apply(self.stats, 0, lambda j: z1[b % 2].ap[:, j, :], src, z1[b % 2].free, engine=G)
                    rec = self.rec[b % 2][0]
                    self.rec_ok = norm_apply(self.stats, 1, lambda j: rec.ap[:, j, 0:D], src, rec.free)
                    self.rec_ok.append(V(lambda e: e.tensor_copy(rec.ap[:, :, D + 1].bitcast(I32), token_id[:, 0, tiles]),
                                         loaded["token_id"], rec.free))

                def choose():
                    t, w = transposes(z1T.ap, lambda j: z1[b % 2].ap[:, j, :], self.z_ok, z1T.free)
                    mm = [T(lambda e, j=j: e.matmul(misc.ap[:, j * NE:(j + 1) * NE], z1T.ap[:, j * P:(j + 1) * P],
                                                    centroids, start=True, stop=True), w, misc.free, loaded["centroids"])
                          for j in range(TPB)]
                    z1T.free = [mm[-1]]
                    lg = V(lambda e: e.tensor_copy(self.logits, misc.ap[:, 0:TPB * NE].rearrange("p (t n) -> p t n", t=TPB)),
                           mm[-1], self.chain)
                    misc.free = [lg]
                    self.logits_ready = lg
                    self.choose_top(b)
                    ex = S(lambda e: e.activation(self.gate, self.top[:, :, 0], ACT.Exp, scale=-1.0), self.top_ready, self.gate_ready)
                    p1 = V(lambda e: e.tensor_scalar(self.gate, self.gate, 1.0, None, ALU.add), ex)
                    rec = self.rec[b % 2][0]
                    self.gate_ready = [V(lambda e: e.reciprocal(rec.ap[:, :, D], self.gate), p1, rec.free)]
                    self.rec_ok += self.gate_ready

                def send():
                    self.send(b, misc, self.rec_ok)
                    zb, xs = z1[b % 2], x_sb[:, tiles, :]
                    w = G(lambda e: e.tensor_tensor(xs, xs, zb.ap, ALU.add), self.rec_ok, self.z_ok)
                    zb.free = [w]
                    self.residual.append(w)

                return [norms, apply, choose, send]

            def setup(self, e0):
                lnb_wide = self.lnb_wide
                for x in e0:
                    w = G(lambda e, x=x: e.tensor_copy(lnb_wide, ln_b[:, x:x + 1].to_broadcast([P, P])),
                          loaded["ln_b"], self.wide_free)
                    mm = T(lambda e, x=x: e.matmul(misc.ap, lnb_wide, self.w1[:, x * FF:(x + 1) * FF], start=True, stop=True),
                           w, misc.free, loaded["w1_0"])
                    self.wide_free = [mm]
                    sl = self.b1[:, x * FF:(x + 1) * FF]
                    v = V(lambda e, sl=sl: e.tensor_tensor(sl, misc.ap, sl, ALU.add), mm, loaded["b1_0"])
                    misc.free = [v]
                    g = G(lambda e, x=x: e.tensor_scalar(self.w1[:, x * FF:(x + 1) * FF], self.w1[:, x * FF:(x + 1) * FF],
                                                         ln_g[:, x:x + 1], None, ALU.mult), mm, loaded["ln_g"])
                    self.weights_ready += [v, g]

            def finish(self):
                self.work_free = [p.free for p in prob]
                self.plan(misc)
                banks = [Buffer(psum[:, i, :]) for i in range(8)]
                for bank, old in zip(banks, score_banks + shift_banks + [num_bank, den_bank, misc]):
                    bank.free = list(old.free)
                self.blocks(banks)
                self.banks = banks

        experts0 = Experts0(0, 1, None, None, b1_0, None, [], ACT.Relu,
                            sb("gate0", [P, TPB]), [], moe_work, ())
        experts0.residual, experts0.wide_free, experts0.lnb_wide = [], [], sb("lnb_wide", [P, P])

        step_stats(0)
        step_norm(0)
        absorb(0)
        step_zT(0)
        step_k(0)
        step_q(0)
        absorb(4)
        step_ckv(0)
        wvo_ready = absorb_values()
        experts0.w1 = load("w1_0", None, place=early[:, 0:NE * FF], after=[wvo_ready, m_ready])
        step_u(0, 0)
        ahead = {0: [lambda: step_stats(1)], 1: [lambda: step_norm(1)], 3: [lambda: step_zT(1)], 4: [lambda: step_k(1)],
                 5: [lambda: step_q(1)], 6: [lambda: step_ckv(1)]}
        for h in range(HEADS):
            step_scores(0, h, range(0, 2))
            if h + 1 < HEADS:
                step_u(0, h + 1)
            step_scores(0, h, range(2, 4))
            for step in ahead.get(h, []):
                step()
        step_u(1, 0)
        step_shift(0)

        def group_steps(b, g):
            return [(b, g, j, part) for j in range(TPB) for part in range(2)]

        values = []
        later = []
        for b in range(BATCH):
            step_residual_bias(b, wvo_ready)
            nxt, nxt2 = b + 1 < BATCH, b + 2 < BATCH
            scores = [(b + 1, h, (2 * k, 2 * k + 1)) for h in range(HEADS) for k in range(2)] if nxt else []
            for h in range(HEADS):
                if nxt and h + 1 < HEADS:
                    step_u(b + 1, h + 1)
                step_exp(b, h, (0, 1))
                for _ in range(1 if h < 6 else 2):
                    if scores and scores[0][1] <= h + 1:
                        step_scores(*scores.pop(0))
                if values:
                    step_values(*values.pop(0))
                step_exp(b, h, (2, 3))
                for _ in range(1 if h < 6 else 2):
                    if scores and scores[0][1] <= h + 1:
                        step_scores(*scores.pop(0))
                if nxt2 and h == 1:
                    step_stats(b + 2)
                if nxt2 and h == 2:
                    step_norm(b + 2)
                if nxt2 and h == 4:
                    step_zT(b + 2)
                if nxt2 and h == 5:
                    step_k(b + 2)
                if nxt2 and h == 6:
                    step_q(b + 2)
                if nxt2 and h == 7:
                    step_ckv(b + 2)
                if b == BATCH - 1:
                    experts0.setup([h])
                if b > 0 and h == QUAD:
                    later += [lambda b=b: step_out(b - 1)] + experts0.steps(b - 1)
                if later:
                    later.pop(0)()
                if values:
                    step_values(*values.pop(0))
                if h == QUAD - 1:
                    values += group_steps(b, 0)
            if nxt2:
                step_u(b + 2, 0)
            if nxt:
                step_shift(b + 1)
            values += group_steps(b, 1)
        for v in values:
            step_values(*v)
        for step in later:
            step()
        step_out(BATCH - 1)
        experts0.w2 = load("w2_0", None, place=w2_mem, after=[p.free for p in prob[0:2]])
        experts0.b2 = spread("b2_0", NE * D, place=b2_mem0, after=prob[2].free)
        experts0.weights_ready += [loaded["w2_0"], loaded["b2_0"]]
        for step in experts0.steps(BATCH - 1):
            step()
        experts0.finish()
        collect_bufs = [Buffer(m.rearrange("p (t d) -> p t d", t=TPB)) for m in carve(moe_work[:, 4 * 1024:], 4 * [TPB * D])]
        collect_turn = [0]

        def collect(ex, b, ready):
            xs = x_sb[:, b * TPB:(b + 1) * TPB, :]
            for c in range(ex.k):
                y = collect_bufs[collect_turn[0] % 4]
                collect_turn[0] += 1
                rows = ex.outs[(c * NT + b * TPB) * P:(c * NT + (b + 1) * TPB) * P, :]
                d = q.dma("sync", f"collect{collect_turn[0] % 4}", lambda e, y=y, rows=rows: e.dma_start(
                    y.ap, rows.rearrange("(t p) d -> p t d", p=P)), [ex.sent, ex.ended, y.free])
                ready = [V(lambda e, y=y: e.tensor_tensor(xs, xs, y.ap, ALU.add), d, ready)]
                y.free = ready
            return ready

        freed = [experts0.ended, experts0.sent]

        def reuse(m):
            x = Buffer(m)
            x.free = list(freed)
            return x

        KVW = LH * LE * LD
        e_ = carve(early, [KVW] * 3 + [2 * D] * 5 + [D] * 2)
        kv_buf, prod_buf = [reuse(m) for m in e_[0:2]], reuse(e_[2])
        exp_buf, pos_buf, qk_buf = reuse(e_[3]), reuse(e_[4]), [reuse(m) for m in e_[5:8]]
        o_buf, oT_buf = reuse(e_[8]), reuse(e_[9])
        w_ = carve(moe_work, 3 * [LH * LE] + 2 * [P] + 2 * [LH * LE] + 6 * [LH * LE] + [LH] * 2)
        v_buf, qT_buf, sum_buf, state_buf = ([reuse(m) for m in w_[i:j]] for i, j in ((0, 3), (3, 5), (5, 7), (7, 13)))
        norm_buf, inv_buf = reuse(w_[13]), reuse(w_[14])
        heads_of = lambda m, n: m.rearrange("p (h c) -> p h c", c=n)
        v_one = [V(lambda e, v=v: e.memset(heads_of(v.ap, LE)[:, :, LD:LE], 1.0), v.free) for v in v_buf]
        banks = experts0.banks
        turn_bank, qkv_bank, state_bank, inter_bank, out_bank = banks[0:5]
        sum_banks = banks[5:8]
        l1_ready, l1z, l1zT, part, state_ready, l1_done, l1_stats = {}, {}, {}, {}, {}, {}, {}

        def l1_take(b):
            l1_ready[b] = collect(experts0, b, experts0.residual)
            l1_stats[b] = norm_stats(lambda j: x_sb[:, b * TPB + j, :], l1_ready[b])

        def l1_norm(b):
            zb = z[b % 2]
            l1z[b] = norm_apply_scalar(l1_stats[b], lambda j: zb.ap[:, j, :], lambda j: x_sb[:, b * TPB + j, :], zb.free)

        def l1_turn(b):
            zb, zt = z[b % 2], zT[b % 2]
            t, l1zT[b] = transposes(zt.ap, lambda j: zb.ap[:, j, :], l1z[b], zt.free, bank=turn_bank)
            zb.free = [t]

        def l1_project(t):
            b, c = divmod(t, TPB)
            zt, v = zT[b % 2], v_buf[t % 3]
            T(lambda e: e.matmul(qkv_bank.ap[:, 0:3 * D], ones_row, bqkv, start=True, stop=False),
              qkv_bank.free, loaded["bqkv"], ones_row_set)
            mm = T(lambda e: e.matmul(qkv_bank.ap[:, 0:3 * D], zt.ap[:, c * P:(c + 1) * P], wqkv, start=False, stop=True),
                   l1zT[b], loaded["wqkv"])
            zt.free = [mm]
            ex = S(lambda e: e.activation(exp_buf.ap, qkv_bank.ap[:, 0:2 * D], ACT.Exp), mm, exp_buf.free)
            pos = S(lambda e: e.activation(pos_buf.ap, qkv_bank.ap[:, 0:2 * D], ACT.Relu), mm, pos_buf.free)
            vc = S(lambda e: e.copy(heads_of(v.ap, LE)[:, :, 0:LD], heads_of(qkv_bank.ap[:, 2 * D:3 * D], LD)), mm, v.free)
            qkv_bank.free = [ex, pos, vc]
            part[t] = [ex, pos, vc]

        def l1_features(t):
            qk, v, kv = qk_buf[t % 3], v_buf[t % 3], kv_buf[t % 2]
            ex, pos, vc = part[t]
            f = V(lambda e: e.scalar_tensor_tensor(qk.ap, exp_buf.ap, 1.0, pos_buf.ap, ALU.min, ALU.add), ex, pos, qk.free)
            exp_buf.free = pos_buf.free = [f]
            kh, vh = heads_of(qk.ap[:, D:2 * D], LD), heads_of(v.ap, LE)
            o = G(lambda e: e.tensor_tensor(kv.ap.rearrange("p (h c d) -> p h c d", h=LH, c=LE),
                                            kh.unsqueeze(2).to_broadcast([P, LH, LE, LD]),
                                            vh.unsqueeze(3).to_broadcast([P, LH, LE, LD]), ALU.mult), f, vc, v_one, kv.free)
            part[t] = [f, vc, o]

        def l1_states(t):
            b, c = divmod(t, TPB)
            f, vc, o = part[t]
            qk, v, qT, users = qk_buf[t % 3], v_buf[t % 3], qT_buf[t % 2], []
            new = state_buf[t % len(state_buf)]
            if c > 0:
                m = T(lambda e: e.transpose(turn_bank.ap[:, 0:P], qk.ap[:, 0:D], ident), f, turn_bank.free)
                qt = S(lambda e: e.copy(qT.ap, turn_bank.ap[:, 0:P]), m, qT.free)
                turn_bank.free = [qt]
                part[t].append(qt)
                users.append(m)
            if c < TPB - 1:
                ms = T(lambda e: e.matmul(state_bank.ap[:, 0:LH * LE], qk.ap[:, D:2 * D], v.ap,
                                          start=True, stop=True), f, vc, v_one, state_bank.free)
                users.append(ms)
                m = V(lambda e: e.tensor_tensor(new.ap, state_bank.ap[:, 0:LH * LE], head_mask, ALU.mult), ms, new.free,
                      loaded["head_mask"])
                state_bank.free = [m]
                state_ready[t] = m
            qk.free = users
            v.free = [o] + users

        def l1_sums(t):
            f, vc, o = part[t][0:3]
            qk, kv = qk_buf[t % 3], kv_buf[t % 2]
            ps = []
            for g in range(LH // GRP):
                bank = sum_banks[(t * (LH // GRP) + g) % len(sum_banks)]
                mm = T(lambda e, g=g, bank=bank: e.matmul(bank.ap[:, 0:GW], upto, kv.ap[:, g * GW:(g + 1) * GW],
                                                          start=True, stop=True), o, bank.free, loaded["upto"])
                qh = heads_of(qk.ap[:, g * GRP * LD:(g + 1) * GRP * LD], LD)
                w = V(lambda e, g=g, bank=bank, qh=qh: e.tensor_tensor(
                    prod_buf.ap[:, g * GW:(g + 1) * GW].rearrange("p (h c d) -> p h c d", h=GRP, c=LE),
                    bank.ap[:, 0:GW].rearrange("p (h c d) -> p h c d", h=GRP, c=LE),
                    qh.unsqueeze(2).to_broadcast([P, GRP, LE, LD]), ALU.mult), mm, prod_buf.free)
                bank.free = [w]
                ps.append(w)
            kv.free = [mm]
            qk.free = qk.free + [w]
            part[t].append(ps)

        def l1_totals(t):
            b, c = divmod(t, TPB)
            qT, total = qT_buf[t % 2], sum_buf[t % 2]
            red = V(lambda e: e.tensor_reduce(total.ap, prod_buf.ap.rearrange("p (c d) -> p c d", d=LD), AX.X, ALU.add),
                    part[t][-1], total.free)
            prod_buf.free = [red]
            if c > 0:
                for i in range(t - c, t):
                    old = state_buf[i % len(state_buf)]
                    mi = T(lambda e, i=i, old=old: e.matmul(inter_bank.ap[:, 0:LH * LE], qT.ap, old.ap,
                                                            start=(i == t - c), stop=(i == t - 1)),
                           part[t][3], state_ready[i], inter_bank.free)
                    old.free = [mi]
                qT.free = [mi]
                red = V(lambda e: e.tensor_tensor(total.ap, total.ap, inter_bank.ap[:, 0:LH * LE], ALU.add), mi, red)
                inter_bank.free = [red]
            th = heads_of(total.ap, LE)
            n = V(lambda e: e.tensor_scalar(norm_buf.ap, th[:, :, LD], LEPS, None, ALU.add), red)
            r = V(lambda e: e.reciprocal(inv_buf.ap, norm_buf.ap), n)
            o = V(lambda e: e.tensor_tensor(heads_of(o_buf.ap, LD), th[:, :, 0:LD],
                                            inv_buf.ap.unsqueeze(2).to_broadcast([P, LH, LD]), ALU.mult), r, o_buf.free)
            total.free = [o]
            part[t] = o

        def l1_output(t):
            b = t // TPB
            mt = T(lambda e: e.transpose(out_bank.ap[:, 0:P], o_buf.ap, ident), part[t], out_bank.free)
            o_buf.free = [mt]
            w = S(lambda e: e.copy(oT_buf.ap, out_bank.ap[:, 0:P]), mt, oT_buf.free)
            T(lambda e: e.matmul(out_bank.ap[:, P:2 * P], ones_row, bout, start=True, stop=False),
              w, loaded["bout"], ones_row_set)
            mm = T(lambda e: e.matmul(out_bank.ap[:, P:2 * P], oT_buf.ap, wout, start=False, stop=True), w, loaded["wout"])
            oT_buf.free = [mm]
            xt = x_sb[:, t, :]
            x = V(lambda e: e.tensor_tensor(xt, xt, out_bank.ap[:, P:2 * P], ALU.add), mm, l1z[b])
            out_bank.free = [x]
            l1_done.setdefault(b, []).append(x)


        class Experts1(Experts):
            def steps(self, b):
                tiles = slice(b * TPB, (b + 1) * TPB)
                r0, r1 = self.rec[b % 2]

                def norms():
                    self.stats = norm_stats(lambda j: x_sb[:, b * TPB + j, :], l1_done[b])

                def apply():
                    rows = norm_apply_scalar(self.stats, lambda j: r0.ap[:, j, 0:D], lambda j: x_sb[:, b * TPB + j, :], r0.free)
                    self.rec_ok = [rows, S(lambda e: e.copy(r1.ap[:, :, 0:D], r0.ap[:, :, 0:D]), rows, r1.free)]
                    self.rec_ok += [G(lambda e, c=c, r=r: e.tensor_copy(r.ap[:, :, D + 1].bitcast(I32), token_id[:, c, tiles]),
                                      loaded["token_id"], r.free) for c, r in ((0, r0), (1, r1))]

                def choose():
                    t, w = transposes(z1T.ap, lambda j: r0.ap[:, j, 0:D], self.rec_ok[0], z1T.free, bank=out_bank)
                    bank = out_bank
                    mm = [T(lambda e, j=j: e.matmul(bank.ap[:, j * NE:(j + 1) * NE], z1T.ap[:, j * P:(j + 1) * P],
                                                    wg, start=True, stop=True), w, bank.free, loaded["wg"])
                          for j in range(TPB)]
                    z1T.free = [mm[-1]]
                    lg3 = bank.ap[:, 0:TPB * NE].rearrange("p (t n) -> p t n", t=TPB)
                    row = lambda m: m.unsqueeze(2).to_broadcast([P, TPB, NE])
                    m = V(lambda e: e.tensor_reduce(self.gate, lg3, AX.X, ALU.max), mm[-1], self.gate_ready)
                    d = V(lambda e: e.tensor_tensor(self.logits, lg3, row(self.gate), ALU.subtract), m, self.chain)
                    bank.free = [d]
                    x = S(lambda e: e.activation(self.logits, self.logits, ACT.Exp), d)
                    u = V(lambda e: e.tensor_reduce(self.gate, self.logits, AX.X, ALU.add), x, d)
                    i_ = V(lambda e: e.reciprocal(self.gate, self.gate), u)
                    self.logits_ready = V(lambda e: e.tensor_tensor(self.logits, self.logits, row(self.gate), ALU.mult), i_)
                    self.gate_ready = [self.logits_ready]
                    self.choose_top(b)
                    self.rec_ok += [V(lambda e, c=c, r=r: e.tensor_copy(r.ap[:, :, D], self.top[:, :, c]), self.top_ready, r.free)
                                    for c, r in ((0, r0), (1, r1))]

                def send():
                    self.send(b, out_bank, self.rec_ok)
                    self.chain += self.rec_ok[-2:]

                return [norms, apply, choose, send]

        experts1 = Experts1(1, 2, w1_mem1, w2_mem, b1_0, b2_mem1, [], ACT.Gelu_apprx_tanh,
                            sb("gate1", [P, TPB]), [], moe_work, ())
        experts1.residual = []
        load("w1_1", None, place=w1_mem1, after=[p.free for p in prob])
        load("w2_1", None, place=w2_mem, after=experts0.ended)
        spread("b1_1", NE * FF, place=b1_0, after=experts0.ended)
        spread("b2_1", NE * D, place=b2_mem1, after=[p.free for p in prob])
        experts1.weights_ready = [loaded[n] for n in ("w1_1", "w2_1", "b1_1", "b2_1")]

        later = []
        for step in (l1_take, l1_norm, l1_turn):
            step(0)
        ahead = {0: l1_take, 1: l1_norm, 2: l1_turn}
        l1_project(0)
        for t in range(NT + 2):
            if 1 <= t <= NT:
                l1_states(t - 1)
                l1_sums(t - 1)
            if t < NT:
                l1_features(t)
            if t + 1 < NT:
                l1_project(t + 1)
            if t >= 2:
                l1_output(t - 2)
            if 1 <= t <= NT:
                l1_totals(t - 1)
            if t >= 2 and (t - 2) % TPB == TPB - 1:
                later += experts1.steps((t - 2) // TPB)
            if t % TPB in ahead and t // TPB + 1 < BATCH:
                ahead[t % TPB](t // TPB + 1)
            if later:
                later.pop(0)()
        for step in later:
            step()

        experts1.work_free = [l1_done[b] for b in l1_done] + [part[t] for t in (NT - 2, NT - 1)]
        experts1.plan(out_bank)
        experts1.blocks(banks)

        out_rows = out.rearrange("b (t p) d -> p (b t) d", p=P)
        for b in range(BATCH):
            sl = slice(b * TPB, (b + 1) * TPB)
            w = collect(experts1, b, l1_done[b])
            q.dma("sync", f"out{b}", lambda e, sl=sl: e.dma_start(out_rows[:, sl, :], x_sb[:, sl, :]), w)
        q.emit(ctx.enter_context(nc.Block()))


def lay_out(i):
    r = {k: np.asarray(v) for k, v in i.items()}
    f = lambda name: r[name]
    z = lambda *s: np.zeros(s, np.float32)
    o = {"x": f("L0_attn_h_t").reshape(TOK, D)}
    o["ident"] = np.eye(P, dtype=np.float32)
    wdq, bdq = f("L0_attn_W_DQ"), f("L0_attn_b_DQ")
    o["wq"] = np.concatenate([wdq, wdq, wdq, z(D, P - 3 * DC)], 1)
    o["bq"] = np.concatenate([bdq, bdq, bdq, np.ones(2, np.float32), z(P - 3 * DC - 2)])[:, None]
    o["wk"] = np.concatenate([f("L0_attn_W_DKV"), f("L0_attn_W_KR"), z(D, 1)], 1)
    o["bk"] = np.concatenate([f("L0_attn_b_DKV"), f("L0_attn_b_KR"), np.ones(1, np.float32)])[:, None]
    o["bkv"] = f("L0_attn_b_DKV")[None]
    lo = z(P, 2)
    lo[2 * DC:3 * DC, 0] = -1.0
    lo[DC:2 * DC, 1] = -1.0
    lo[ROW_ONE + 1, 1] = -1.0
    o["lo_rows"] = lo
    per_head = lambda w: w.reshape(w.shape[0], HEADS, -1)
    uk, uq, uv = (per_head(f(f"L0_attn_W_{n}")) for n in ("UK", "UQ", "UV"))
    qr = per_head(f("L0_attn_W_QR"))
    buk, buq, buv, bqr = (f(f"L0_attn_b_{n}").reshape(HEADS, -1) for n in ("UK", "UQ", "UV", "QR"))
    o["mk"] = np.concatenate([uk.transpose(2, 1, 0), z(DK, HEADS, DR), buk.T[:, :, None]], 2)
    t = uq.transpose(2, 1, 0)
    o["mq"] = np.concatenate([t, t, t, buq.T[:, :, None], buq.T[:, :, None], z(DK, HEADS, P - ROW_MHI)], 2)
    rk = z(DR + 1, KSIDE)
    rk[0:DR, DC:DC + DR] = np.eye(DR)
    rk[DR, KSIDE - 1] = 1.0
    o["rk"] = rk
    t = qr.transpose(2, 1, 0)
    sel = z(1, HEADS, P)
    for h in range(HEADS):
        sel[0, h, ROW_MHI + h] = sel[0, h, ROW_MLO + h] = 1.0
    o["rq"] = np.concatenate([np.concatenate([t, t, t, bqr.T[:, :, None], bqr.T[:, :, None],
                                              z(DR, HEADS, P - ROW_MHI)], 2), sel], 0)
    o["wuv"] = uv.transpose(2, 1, 0)
    o["buv"] = buv.T
    o["wo"] = f("L0_attn_W_O").reshape(HEADS, DK, D).transpose(1, 0, 2)
    o["bo"] = f("L0_attn_b_O")[None]
    i = np.arange(P)
    o["upto"] = (i[:, None] <= i[None, :]).astype(np.float32)
    o["choice"] = np.tile(np.concatenate([np.arange(NE), np.arange(NE) * REGION]).astype(np.float32), (P, 1))
    o["token_id"] = (np.arange(2)[None, :, None] * TOK + np.arange(NT)[None, None, :] * P + i[:, None, None]).astype(np.int32)
    pad = z(P, REC)
    pad[:, D + 1:D + 2] = np.full((P, 1), SKIP, np.int32).view(np.float32)
    o["pad_rec"] = pad
    for n, k in ((0, 1), (1, 2)):
        o[f"block_no{n}"] = np.tile(np.arange(n_blocks(k), dtype=np.float32)[:, None], (1, NE))[None]
    o["centroids"] = f("L0_ffn_centroids").T
    o["ln_g"], o["ln_b"] = f("L0_ffn_ln_g").T, f("L0_ffn_ln_b").T
    o["w1_0"] = f("L0_ffn_w1").transpose(2, 0, 1).reshape(D, NE * FF)
    o["w2_0"] = f("L0_ffn_w2").transpose(2, 0, 1).reshape(FC, P, NE, D).transpose(1, 2, 0, 3).reshape(P, NE * FF)
    o["b1_0"], o["b2_0"] = f("L0_ffn_b1").reshape(1, -1), f("L0_ffn_b2").reshape(1, -1)
    o["wqkv"], o["bqkv"] = f("L1_attn_w_qkv").T, f("L1_attn_b_qkv")[None]
    o["wout"], o["bout"] = f("L1_attn_w_out").T, f("L1_attn_b_out")[None]
    o["head_mask"] = (i[:, None] // LD == np.arange(LH * LE)[None, :] // LE).astype(np.float32)
    o["wg"] = f("L1_ffn_Wg")
    o["w1_1"] = f("L1_ffn_W1").transpose(1, 0, 2).reshape(D, NE * FF)
    o["w2_1"] = f("L1_ffn_W2").reshape(NE, FC, P, D).transpose(2, 0, 1, 3).reshape(P, NE * FF)
    o["b1_1"], o["b2_1"] = f("L1_ffn_b1").reshape(1, -1), f("L1_ffn_b2").reshape(1, -1)
    return {k: np.ascontiguousarray(v) for k, v in o.items()}


def kernel(**inputs):
    import concourse.bacc as bacc
    from concourse.bass_utils import run_bass_kernel_spmd

    nc = bacc.Bacc("TRN2", target_bir_lowering=False, num_devices=1)
    arrays = lay_out(inputs)
    aps = {k: nc.dram_tensor(f"in_{k}", v.shape, mybir.dt.from_np(v.dtype), kind="ExternalInput").ap()
           for k, v in arrays.items()}
    out = nc.dram_tensor("out_0", (BATCH, SEQ, D), F32, kind="ExternalOutput").ap()
    build(nc, aps, out)
    r = run_bass_kernel_spmd(nc, [{f"in_{k}": v for k, v in arrays.items()}], core_ids=[0])
    return r.results[0]["out_0"]
```

```python
from contextlib import ExitStack
import math

import numpy as np
import concourse.bass as bass
from concourse import mybir

F32 = mybir.dt.float32
F32R = mybir.dt.float32r
BF16 = mybir.dt.bfloat16
I32 = mybir.dt.int32
U32 = mybir.dt.uint32
ALU = mybir.AluOpType
ACT = mybir.ActivationFunctionType
AX = mybir.AxisListType

P = 128
BATCH, SEQ, D = 4, 512, 128
TOK = BATCH * SEQ
NT = TOK // P
TPB = SEQ // P
HEADS, DK, DC, DR = 8, 128, 32, 32
SCORE_SCALE = 1.0 / math.sqrt(DK + DR)
EPS = 1e-5

ROW_ONE = 3 * DC
ROW_MHI = ROW_ONE + 2
ROW_MLO = ROW_MHI + HEADS
SCORE_K = ROW_MHI
SHIFT_K = ROW_MLO + HEADS
KSIDE = DC + DR + 1
QUAD = 4

LH, LD = 16, 8
LE = LD + 1
LEPS = 1e-6
GRP = 4
GW = GRP * LE * LD

NE, FF = 8, 512
FC = FF // P
REC = D + 2
HALVES = 2
HTOK = TOK // HALVES
BPH = BATCH // HALVES
REGION = HTOK + P
PAD_ROW = NE * REGION
SKIP = 1 << 20


def n_blocks(k):
    return (k * HTOK) // P + NE - 1


BLOCKS_BESIDE = (3, 2)
RECORDS_LAND = 24
TAIL = 2


def flat(x):
    if x is None:
        return []
    if isinstance(x, dict):
        return [x]
    return [t for y in x for t in flat(y)]


def pause():
    pass


class Queues:

    def __init__(self, nc, ctx):
        self.nc, self.ctx = nc, ctx
        self.items = {e: [] for e in ("sync", "scalar", "vector", "gpsimd", "tensor")}
        self.done = {e: ctx.enter_context(nc.semaphore(f"done_{e}")) for e in self.items if e != "sync"}
        self.slots = {}

    def put(self, engine, fn, after, token):
        after = flat(after)
        for t in after:
            t["needed"] = True
        self.items[engine].append((fn, after, token))
        return token

    def add(self, engine, fn, after=()):
        return self.put(engine, fn, after, {"dma": False, "needed": False, "sem": None, "value": None})

    def dma(self, engine, slot, fn, after=()):
        if slot not in self.slots:
            self.slots[slot] = [self.ctx.enter_context(self.nc.semaphore(f"dma_{slot}")), 0]
        self.slots[slot][1] += 16
        token = {"dma": True, "needed": True, "sem": self.slots[slot][0], "value": self.slots[slot][1]}
        return self.put(engine, fn, after, token)

    def emit(self, block):
        for engine, items in self.items.items():
            count = 0
            for _, _, t in items:
                if t["needed"] and not t["dma"]:
                    count += 1
                    t["sem"], t["value"] = self.done[engine], count

        def play(engine, items):
            def body(eng):
                seen = {}
                for fn, after, token in items:
                    need = {}
                    for t in after:
                        if t["value"] > seen.get(t["sem"].name, 0):
                            seen[t["sem"].name] = t["value"]
                            need[t["sem"].name] = (t["sem"], t["value"])
                    for sem, value in need.values():
                        eng.wait_ge(sem, value)
                    ins = fn(eng)
                    if token["needed"]:
                        ins.then_inc(token["sem"], 16 if token["dma"] else 1)
                if engine == "sync":
                    for sem, value in self.slots.values():
                        eng.wait_ge(sem, value)
            return body

        block.sync(play("sync", self.items["sync"]))
        block.scalar(play("scalar", self.items["scalar"]))
        block.vector(play("vector", self.items["vector"]))
        block.gpsimd(play("gpsimd", self.items["gpsimd"]))
        block.tensor(play("tensor", self.items["tensor"]))


class Buffer:

    def __init__(self, ap):
        self.ap, self.free = ap, []


def build(nc, a, out):
    ctx = ExitStack()
    with ctx:
        q = Queues(nc, ctx)

        def sb(name, shape, dt=F32):
            return ctx.enter_context(nc.sbuf_tensor(name, shape, dt))[:]

        def V(fn, *after):
            return q.add("vector", fn, after)

        def S(fn, *after):
            return q.add("scalar", fn, after)

        def G(fn, *after):
            return q.add("gpsimd", fn, after)

        def T(fn, *after):
            return q.add("tensor", fn, after)

        psum = ctx.enter_context(nc.psum_tensor("psum", [P, 8, 512], F32))[:]

        loaded = {}

        def load(name, shape, dt=F32, place=None, after=()):
            t = sb(name, shape, dt) if place is None else place
            loaded[name] = q.dma("sync", name, lambda e: e.dma_start(t, a[name]), after)
            return t

        def spread(name, n, place=None, after=()):
            t = sb(name, [P, n]) if place is None else place
            loaded[name] = q.dma("sync", name, lambda e: e.dma_start(t, a[name].to_broadcast([P, n])), after)
            return t

        early = sb("early", [P, 5 * 1024])
        probs_mem = sb("probs_mem", [P, HEADS * TPB * SEQ])

        def carve(region, sizes):
            at, pieces = 0, []
            for n in sizes:
                pieces.append(region[:, at:at + n])
                at += n
            assert at <= region.shape[1]
            return pieces

        x_sb = sb("x", [P, NT, D])
        x_rows = a["x"].rearrange("(t p) d -> p t d", p=P)
        x_in = []
        for b in range(BATCH):
            sl = slice(b * TPB, (b + 1) * TPB)
            x_in.append(q.dma("sync", f"x{b}", lambda e, sl=sl: e.dma_start(x_sb[:, sl, :], x_rows[:, sl, :])))
            if b == 0:
                ident = load("ident", [P, P])
                wq = load("wq", [P, P])
                bq = load("bq", [P, 1])
                wk = load("wk", [P, KSIDE])
                bk = load("bk", [KSIDE, 1])
                bkv = spread("bkv", DC)
                lo_rows = load("lo_rows", [P, 2])
                mk_m, mq_m, rq_m, buv_m, wo_m = carve(early, [HEADS * KSIDE] + 4 * [HEADS * P])
                heads = lambda m: m.rearrange("p (h c) -> p h c", h=HEADS)
                mk = load("mk", None, place=heads(mk_m))
                mq = load("mq", None, place=heads(mq_m))
                rk = load("rk", [DR + 1, KSIDE])
                rq = load("rq", None, place=heads(rq_m)[0:DR + 1])
        wuv = load("wuv", [P, HEADS, DC])
        buv = load("buv", [P, HEADS])
        wo = load("wo", None, place=heads(wo_m))
        bo = load("bo", [1, D])
        upto = load("upto", [P, P])
        before = sb("before", [P, P], BF16)
        ones_bf = sb("ones_bf", [P, P], BF16)
        choice = load("choice", [P, 2 * NE])
        token_id = load("token_id", [P, 2, HTOK // P], I32)
        pad_rec = load("pad_rec", [P, REC])
        block_no = load("block_no", [1, n_blocks(2), NE])
        wqkv, wout = load("wqkv", [D, 3 * D]), load("wout", [D, D])
        bias_full, lo_row2 = load("bias_full", [2, 4 * D]), load("lo_row2", [2, 1])
        head_mask = load("head_mask", [P, LH * LE])
        wg = load("wg", [D, NE])

        half = sb("half", [P, TPB])
        half_set = G(lambda e: e.memset(half, -0.5))
        ones_row = sb("ones_row", [1, P])
        ones_row_set = G(lambda e: e.memset(ones_row, 1.0))

        score_banks = [Buffer(psum[:, i, :]) for i in range(2)]
        second_misc = Buffer(psum[:, 2, :])
        shift_banks = [Buffer(psum[:, 3 + i, :]) for i in range(2)]
        num_bank, den_bank = Buffer(psum[:, 5, :]), Buffer(psum[:, 6, :])
        misc = Buffer(psum[:, 7, :])
        spares, spare_turn = [misc, second_misc], [0]

        def spare_bank():
            spare_turn[0] += 1
            return spares[spare_turn[0] % len(spares)]


        ln_stats = [sb(f"ln_stats{i}", [P, TPB, 6]) for i in range(3)]
        ln_mv = [Buffer(sb(f"ln_mv{i}", [P, TPB, 2])) for i in range(3)]
        ln_scale = [sb(f"ln_scale{i}", [P, TPB, 4]) for i in range(3)]
        ln_count = [0]

        def norm_stats(src, ready, twice=False):
            i = ln_count[0] % len(ln_mv)
            ln_count[0] += 1
            mv, stats, sc = ln_mv[i], ln_stats[i], ln_scale[i]
            st = [V(lambda e, j=j: e.bn_stats(stats[:, j, :], src(j)), ready, mv.free) for j in range(TPB)]
            ag = [V(lambda e, j=j: e.bn_aggr(mv.ap[:, j, :], stats[:, j, :]), st[j]) for j in range(TPB)]
            var, tmp = mv.ap[:, :, 1], sc[:, :, 2]
            t = V(lambda e: e.tensor_scalar(tmp, var, EPS, None, ALU.add), ag, mv.free)
            rs = [G(lambda e: e.tensor_tensor(sc[:, :, 0], tmp, half, ALU.pow), t, half_set)]
            if twice:
                t = G(lambda e: e.tensor_tensor(tmp, var, sc[:, :, 0], ALU.mult), rs)
                t = G(lambda e: e.tensor_tensor(tmp, tmp, sc[:, :, 0], ALU.mult), t)
                t = G(lambda e: e.tensor_scalar(tmp, tmp, EPS, None, ALU.add), t)
                t = G(lambda e: e.tensor_tensor(tmp, tmp, half, ALU.pow), t)
                rs.append(G(lambda e: e.tensor_tensor(sc[:, :, 1], tmp, sc[:, :, 0], ALU.mult), t))
            mv.free = []
            return mv, sc, rs

        def norm_apply_scalar(stats, dst, src, dst_free=()):
            pieces, w = norm_pieces(stats, dst, src, dst_free)
            for piece in pieces:
                piece()
            return w

        def norm_pieces(stats, dst, src, dst_free=()):
            mv, sc, rs = stats
            m, w = [], []

            def piece(j):
                if j == 0:
                    m.append(V(lambda e: e.scalar_tensor_tensor(sc[:, :, 3], mv.ap[:, :, 0], -1.0, sc[:, :, 0],
                                                                ALU.mult, ALU.mult), rs))
                w.append(S(lambda e: e.activation(dst(j), src(j), ACT.Identity, bias=sc[:, j, 3:4], scale=sc[:, j, 0:1]),
                           m, dst_free))
                mv.free.append(w[-1])

            return [lambda j=j: piece(j) for j in range(TPB)], w

        def norm_apply(stats, which, dst, src, dst_free=(), engine=V):
            mv, sc, rs = stats
            w = [engine(lambda e, j=j: e.tensor_scalar(dst(j), src(j), mv.ap[:, j, 0:1], sc[:, j, which:which + 1],
                                                       ALU.subtract, ALU.mult), rs, dst_free) for j in range(TPB)]
            mv.free += w
            return w

        m_sb = sb("m_absorbed", [KSIDE, HEADS, P])
        m_ready = []

        def absorb(h0):
            misc = spare_bank()
            mm = None
            for h in range(h0, h0 + 4):
                o = misc.ap[0:KSIDE, (h - h0) * P:(h - h0 + 1) * P]
                T(lambda e, h=h, o=o: e.matmul(o, mk[:, h, :], mq[:, h, :], start=True, stop=False),
                  misc.free, loaded["mk"], loaded["mq"])
                mm = T(lambda e, h=h, o=o: e.matmul(o, rk, rq[:, h, :], start=False, stop=True),
                       loaded["rk"], loaded["rq"])
            w = S(lambda e: e.copy(m_sb[:, h0:h0 + 4, :], misc.ap[0:KSIDE, :].rearrange("p (h c) -> p h c", h=4)), mm)
            misc.free = [w]
            m_ready.append(w)

        wvo = sb("wvo", [P, 2, D])
        bvo = sb("bvo", [P, D])
        buv_wide = heads(buv_m)

        def absorb_values():
            misc = spare_bank()
            wide = [G(lambda e, h=h: e.tensor_copy(buv_wide[:, h, :], buv[:, h:h + 1].to_broadcast([P, P])),
                      loaded["buv"]) for h in range(HEADS)]
            mm = None
            for h in range(HEADS):
                g, r = divmod(h, 4)
                mm = T(lambda e, h=h, g=g, r=r: e.matmul(misc.ap[r * DC:(r + 1) * DC, g * D:(g + 1) * D], wuv[:, h, :],
                                                         wo[:, h, :], start=True, stop=True),
                       misc.free, loaded["wuv"], loaded["wo"])
            for h in range(HEADS):
                T(lambda e, h=h: e.matmul(misc.ap[:, 2 * D:3 * D], buv_wide[:, h, :], wo[:, h, :],
                                          start=(h == 0), stop=False), wide)
            mm = T(lambda e: e.matmul(misc.ap[:, 2 * D:3 * D], ones_row, bo, start=False, stop=True),
                   ones_row_set, loaded["bo"])
            w1 = V(lambda e: e.tensor_copy(wvo, misc.ap[:, 0:2 * D].rearrange("p (g d) -> p g d", g=2)), mm)
            w2 = V(lambda e: e.tensor_copy(bvo, misc.ap[:, 2 * D:3 * D]), mm)
            misc.free = [w1, w2]
            return [w1, w2]

        z = [Buffer(sb(f"z{i}", [P, TPB, D])) for i in range(2)]
        zT = [Buffer(sb(f"zT{i}", [P, SEQ])) for i in range(2)]
        q_full = sb("q_full", [P, SEQ])
        q_hi = sb("q_hi", [P, SEQ], F32R)
        q_free = [[]]
        q_stack = [Buffer(sb(f"q_stack{i}", [P, SEQ], F32R)) for i in range(3)]
        k_side = [Buffer(sb(f"k_side{i}", [KSIDE, SEQ])) for i in range(2)]
        ckv = [Buffer(sb(f"ckv{i}", [P, TPB, DC])) for i in range(3)]
        ones_dc = sb("ones_dc", [P, DC])
        ones_dc_set = G(lambda e: e.memset(ones_dc, 1.0))
        u_hi = [Buffer(sb(f"u_hi{i}", [P, SEQ], F32R)) for i in range(2)]
        u_ring = [Buffer(sb(f"u_stack{i}", [P, SEQ], F32R)) for i in range(HEADS + 2)]
        u_stack = lambda b, h: u_ring[(b * HEADS + h) % len(u_ring)]
        q_ready, k_ready, c_ready, u_ready, zT_ready = {}, {}, {}, {}, {}
        z_ready = {}

        z_stats = {}

        def step_stats(b):
            z_stats[b] = norm_stats(lambda j: x_sb[:, b * TPB + j, :], x_in[b])

        def step_norm(b):
            zb = z[b % 2]
            z_ready[b] = norm_apply(z_stats[b], 0, lambda j: zb.ap[:, j, :], lambda j: x_sb[:, b * TPB + j, :], zb.free)

        def transposes(dst, src, ready, dst_free, bank=None):
            bank = bank or spare_bank()
            mm = [T(lambda e, j=j: e.transpose(bank.ap[:, j * P:(j + 1) * P], src(j), ident),
                    ready, bank.free, loaded["ident"]) for j in range(TPB)]
            w = S(lambda e: e.copy(dst, bank.ap), mm[-1], dst_free)
            bank.free = [w]
            return mm[-1], w

        def step_zT(b):
            zb, zt = z[b % 2], zT[b % 2]
            t, w = transposes(zt.ap, lambda j: zb.ap[:, j, :], z_ready[b], zt.free)
            zb.free = [t]
            zT_ready[b] = w

        def step_q(b):
            misc = spare_bank()
            zt, qs = zT[b % 2], q_stack[b % 3]
            mm = T(lambda e: e.matmul(misc.ap, wq, zt.ap, start=True, stop=True), zT_ready[b], misc.free, loaded["wq"])
            full = S(lambda e: e.activation(q_full, misc.ap, ACT.Identity, bias=bq), mm, loaded["bq"], q_free[0])
            misc.free = [full]
            hi = V(lambda e: e.tensor_copy(q_hi, q_full), full, q_free[0])
            w = V(lambda e: e.scalar_tensor_tensor(qs.ap, q_hi.bitcast(F32), lo_rows[:, 0:1], q_full, ALU.mult, ALU.add),
                  hi, loaded["lo_rows"], qs.free)
            q_free[0] = [w]
            q_ready[b] = w

        def step_k(b):
            misc = spare_bank()
            zt, ks = zT[b % 2], k_side[b % 2]
            mm = T(lambda e: e.matmul(misc.ap[0:KSIDE, :], wk, zt.ap, start=True, stop=True),
                   zT_ready[b], misc.free, loaded["wk"])
            w = S(lambda e: e.activation(ks.ap, misc.ap[0:KSIDE, :], ACT.Identity, bias=bk), mm, loaded["bk"], ks.free)
            misc.free = [w]
            k_ready[b] = w

        def step_ckv(b):
            misc = spare_bank()
            zt, c = zT[b % 2], ckv[b % 3]
            mm = [T(lambda e, j=j: e.matmul(misc.ap[:, j * DC:(j + 1) * DC], zt.ap[:, j * P:(j + 1) * P], wk[:, 0:DC],
                                            start=True, stop=True), zT_ready[b], misc.free) for j in range(TPB)]
            w = V(lambda e: e.tensor_tensor(c.ap, misc.ap[:, 0:TPB * DC].rearrange("p (t c) -> p t c", t=TPB),
                                            bkv.unsqueeze(1).to_broadcast([P, TPB, DC]), ALU.add),
                  mm[-1], loaded["bkv"], c.free)
            misc.free = [w]
            zt.free = [mm[-1]]
            c_ready[b] = w

        u_begun = {}

        def begin_u(b, h):
            ks, uh, bank = k_side[b % 2], u_hi[h % 2], spare_bank()
            mm = T(lambda e: e.matmul(bank.ap, m_sb[:, h, :], ks.ap, start=True, stop=True),
                   k_ready[b], m_ready[h // 4], bank.free)
            hi = S(lambda e: e.copy(uh.ap, bank.ap), mm, uh.free)
            bank.free = [hi]
            ks.free = [mm]
            u_begun[b, h] = [bank, hi]

        def end_u(b, h):
            us, uh, (bank, hi) = u_stack(b, h), u_hi[h % 2], u_begun[b, h]
            w = V(lambda e: e.scalar_tensor_tensor(us.ap, uh.ap.bitcast(F32), lo_rows[:, 1:2], bank.ap,
                                                   ALU.mult, ALU.add), hi, us.free)
            bank.free = [w]
            uh.free = [w]
            u_ready[b, h] = w

        def step_u(b, h):
            begin_u(b, h)
            end_u(b, h)

        neg_max = [Buffer(sb(f"neg_max{i}", [P, TPB, HEADS])) for i in range(2)]
        max_ready = {}

        score_turn = [0]

        def step_scores(b, h, tiles):
            qs, us, nm = q_stack[b % 3], u_stack(b, h), neg_max[b % 2]
            banks = score_banks + shift_banks if b == 0 else score_banks
            for j in tiles:
                bank = banks[score_turn[0] % len(banks)]
                score_turn[0] += 1
                mm = T(lambda e, j=j, bank=bank: e.matmul(bank.ap, qs.ap[0:SCORE_K, j * P:(j + 1) * P],
                                                          us.ap[0:SCORE_K, :], start=True, stop=True),
                       q_ready[b], u_ready[b, h], bank.free)
                w = V(lambda e, j=j, bank=bank: e.tensor_reduce(nm.ap[:, j, h:h + 1], bank.ap, AX.X, ALU.max, negate=True),
                      mm, nm.free)
                bank.free = [w]
                max_ready.setdefault(b, []).append(w)

        max_hi = sb("max_hi", [P, TPB, HEADS], F32R)
        max_tile = sb("max_tile", [P, TPB, P])
        mt_zero = G(lambda e: e.memset(max_tile, 0.0))
        mt_ones = G(lambda e: e.memset(max_tile[:, :, ROW_ONE:ROW_MHI], 1.0), mt_zero)
        mt_free = [[mt_ones]]
        shift_ready = {}

        split_ready = {}

        def step_split(b):
            nm = neg_max[b % 2]
            hi = V(lambda e: e.tensor_copy(max_hi, nm.ap), max_ready[b], mt_free[0])
            w1 = V(lambda e: e.tensor_copy(max_tile[:, :, ROW_MHI:ROW_MLO], max_hi.bitcast(F32)), hi, mt_free[0])
            w2 = V(lambda e: e.tensor_tensor(max_tile[:, :, ROW_MLO:SHIFT_K], nm.ap, max_hi.bitcast(F32), ALU.subtract), hi)
            nm.free = [w2]
            split_ready[b] = [w1, w2]

        def step_shift(b):
            misc = spare_bank()
            qs = q_stack[b % 3]
            mm = [T(lambda e, j=j: e.transpose(misc.ap[:, j * P:(j + 1) * P], max_tile[:, j, :], ident),
                    split_ready[b], misc.free) for j in range(TPB)]
            w = V(lambda e: e.tensor_copy(qs.ap[ROW_ONE:P, :], misc.ap[ROW_ONE:P, :]), mm[-1], max_ready[b])
            misc.free = [w]
            mt_free[0] = [split_ready[b], mm[-1]]
            shift_ready[b] = w

        prob = [Buffer(m.rearrange("p (t s) -> p t s", t=TPB)) for m in carve(probs_mem, HEADS * [TPB * SEQ])]
        oT = [Buffer(sb(f"oT{g}", [P, SEQ])) for g in range(2)]
        den_t, inv_col, inv_den = sb("den_t", [P, SEQ]), sb("inv_col", [P, SEQ // DC]), sb("inv_den", [P, SEQ])
        prob_ready, oT_ready, exp_turn = {}, {}, [0]

        def step_exp(b, h, tiles):
            qs, us, pr = q_stack[b % 3], u_stack(b, h), prob[h]
            banks = shift_banks if b < BATCH - 1 else shift_banks + score_banks + [second_misc]
            for j in tiles:
                bank = banks[exp_turn[0] % len(banks)]
                exp_turn[0] += 1
                mm = T(lambda e, j=j, bank=bank: e.matmul(bank.ap, us.ap[0:SHIFT_K, j * P:(j + 1) * P],
                                                          qs.ap[0:SHIFT_K, :], start=True, stop=True),
                       shift_ready[b], u_ready[b, h], bank.free)
                x = S(lambda e, j=j, bank=bank: e.activation(pr.ap[:, j, :], bank.ap, ACT.Exp, scale=SCORE_SCALE),
                      mm, pr.free)
                bank.free = [x]
                prob_ready.setdefault((b, h), []).append(x)
            us.free = [mm]
            qs.free = [mm]

        def step_values(b, g, j, part):
            c = ckv[b % 3]
            bank = (num_bank, den_bank)[part]
            for r in range(QUAD):
                pr = prob[g * QUAD + r]
                lhs = c.ap[:, j, :] if part == 0 else ones_dc
                mm = T(lambda e, r=r, pr=pr, lhs=lhs: e.matmul(bank.ap[r * DC:(r + 1) * DC, :], lhs, pr.ap[:, j, :],
                                                               start=(j == 0), stop=(j == TPB - 1)),
                       [prob_ready[b, g * QUAD + x][j] for x in range(QUAD)], c_ready[b], ones_dc_set, bank.free)
            if (j, part) == (TPB - 1, 1):
                for r in range(QUAD):
                    prob[g * QUAD + r].free = [mm]
                c.free = [mm]
                t = V(lambda e: e.transpose(den_t, den_bank.ap), mm)
                den_bank.free = [t]
                r = V(lambda e: e.reciprocal(inv_col, den_t.rearrange("p (b c) -> p b c", c=DC)[:, :, 0]), t)
                t = V(lambda e: e.transpose(inv_den.rearrange("p (b c) -> p b c", c=DC),
                                            inv_col.unsqueeze(2).to_broadcast([P, SEQ // DC, DC])), r)
                w = V(lambda e: e.tensor_tensor(oT[g].ap, num_bank.ap, inv_den, ALU.mult), t, oT[g].free)
                num_bank.free = [w]
                oT_ready[b, g] = w

        res_ready = {}
        xb_ready = {}

        def step_residual_bias(b, bias_ready):
            for j in range(TPB):
                t = b * TPB + j
                w = G(lambda e, t=t: e.tensor_tensor(x_sb[:, t, :], x_sb[:, t, :], bvo, ALU.add),
                      bias_ready, z_ready[b])
                xb_ready.setdefault(b, []).append(w)

        def step_out(b):
            misc = spare_bank()
            for j in range(TPB):
                for g in range(2):
                    mm = T(lambda e, j=j, g=g: e.matmul(misc.ap[:, j * P:(j + 1) * P], oT[g].ap[:, j * P:(j + 1) * P],
                                                        wvo[:, g, :], start=(g == 0), stop=(g == 1)),
                           oT_ready[b, 0], oT_ready[b, 1], misc.free, wvo_ready)
            oT[0].free = oT[1].free = [mm]
            xs = x_sb[:, b * TPB:(b + 1) * TPB, :]
            w = V(lambda e: e.tensor_tensor(xs, misc.ap.rearrange("p (t d) -> p t d", t=TPB), xs, ALU.add),
                  mm, xb_ready[b])
            misc.free = [w]
            res_ready[b] = w

        w1_mem, collect_mem = carve(early, [NE * FF, 2 * TPB * D])
        IN = 12
        b2_mem, rec_mem, block_mem, l1_mem = carve(probs_mem, [NE * D, IN * REC, 2 * P + 7 * FF + 6 * D, 6144])
        w2_mem = load("w2_0", [P, NE * FF])
        b1_cols = [load(f"b1_{n}", [P, NE * FC]) for n in range(2)]
        rec_in = [Buffer(m) for m in carve(rec_mem, IN * [REC])]
        in_use, fetches = IN * [False], [0]
        work = [Buffer(m) for m in carve(block_mem, 2 * [P] + 2 * [FF] + 3 * [FF] + 2 * [D] + 4 * [D] + 2 * [FF])]
        rec_out = [[Buffer(sb(f"rec{i}_{c}", [P, TPB, REC])) for c in range(2)] for i in range(2)]
        logits, top, gate = sb("logits", [P, TPB, NE]), sb("top", [P, TPB, NE]), sb("gate", [P, TPB])
        top_at = sb("top_at", [P, TPB, NE], U32)
        pick = [sb(f"pick{c}", [P, TPB, NE]) for c in range(2)]
        pick_bf = sb("pick_bf", [P, TPB, NE], BF16)
        seen = [sb(f"seen{i}", [P, NE], BF16) for i in range(2)]
        seen_f, rank, rank_k = sb("seen_f", [P, NE]), sb("rank", [P, TPB, NE]), sb("rank_k", [P, TPB, NE])
        row_f, row = sb("row_f", [P, TPB]), [[sb(f"row{i}_{c}", [P, TPB], I32) for c in range(2)] for i in range(2)]
        chain = [[]]
        wide = [sb(x, [1, n_blocks(2), NE]) for x in ("is_from", "is_upto", "val")]
        first_f = sb("first", [1, n_blocks(2)])
        blocks_f, upto_e, from_e, base = (sb(x, [1, NE]) for x in ("blocks_f", "upto_e", "from_e", "base"))
        count, blocks_i = sb("count", [1, NE], I32), sb("blocks_i", [1, NE], I32)

        class Half:

            def __init__(self, n, k, h):
                name = f"{n}_{h}"
                self.name = name
                self.records = nc.dram_tensor(f"records{name}", [PAD_ROW + P, REC], F32, kind="Internal").ap()
                self.outs = nc.dram_tensor(f"outs{name}", [k * HTOK, D], F32, kind="Internal").ap()
                self.pad = q.dma("sync", f"pad{name}", lambda e: e.dma_start(self.records[PAD_ROW:PAD_ROW + P, :], pad_rec),
                                 loaded["pad_rec"])
                self.table = sb(f"table{name}", [1, 2, n_blocks(k)], I32)
                self.fill = sb(f"fill{name}", [1, NE], I32)
                self.scattered, self.sent, self.ended, self.residual = [], [], [], {}

        class Experts:
            def __init__(self, n, k, func):
                self.n, self.k, self.nb, self.func = n, k, n_blocks(k), func
                self.halves = [Half(n, k, h) for h in range(HALVES)]
                self.weights_ready = []

            def choose_top(self, logits_ready):
                mx = [V(lambda e, j=j: e.max(top[:, j, :], logits[:, j, :]), logits_ready, chain[0]) for j in range(TPB)]
                at = [V(lambda e, j=j: e.max_index(top_at[:, j, :], top[:, j, :], logits[:, j, :]), mx[j])
                      for j in range(TPB)]
                self.pick_ready = [V(lambda e, c=c: e.tensor_tensor(
                    pick[c], choice[:, 0:NE].unsqueeze(1).to_broadcast([P, TPB, NE]),
                    top_at[:, :, c:c + 1].to_broadcast([P, TPB, NE]), ALU.is_equal),
                    at, loaded["choice"]) for c in range(self.k)]
                return mx

            def pick(self, b):
                if self.k == 1:
                    bf = V(lambda e: e.tensor_copy(pick_bf, pick[0]), self.pick_ready, chain[0])
                else:
                    bf = V(lambda e: e.tensor_tensor(pick_bf, pick[0], pick[1], ALU.add), self.pick_ready, chain[0])
                begin = b % BPH == 0
                old, new = seen[b % 2], seen[(b + 1) % 2]
                s1 = V(lambda e: e.tensor_reduce(seen_f, pick_bf.rearrange("p t n -> p n t"), AX.X, ALU.add), bf)
                self.picked = [bf, s1, [] if begin else self.seen_set]
                if begin:
                    self.seen_set = [V(lambda e: e.tensor_copy(new, seen_f), s1, chain[0])]
                else:
                    self.seen_set = [V(lambda e: e.tensor_tensor(new, old, seen_f, ALU.add), s1, self.seen_set, chain[0])]

            def locate(self, b, bank):
                begin, old = b % BPH == 0, seen[b % 2]
                bf, s1, old_set = self.picked
                for j in range(TPB):
                    o = bank.ap[:, j * NE:(j + 1) * NE]
                    if not begin:
                        T(lambda e, o=o: e.matmul(o, ones_bf, old, start=True, stop=False),
                          bank.free, old_set, ones_bf_set)
                    for i in range(j):
                        T(lambda e, o=o, i=i: e.matmul(o, ones_bf, pick_bf[:, i, :], start=(begin and i == 0), stop=False),
                          bf, bank.free, ones_bf_set)
                    mm = T(lambda e, o=o, j=j: e.matmul(o, before, pick_bf[:, j, :], start=(begin and j == 0), stop=True),
                           bf, bank.free, before_set)
                r = V(lambda e: e.tensor_tensor(rank, bank.ap[:, 0:TPB * NE].rearrange("p (t n) -> p t n", t=TPB),
                                                choice[:, NE:2 * NE].unsqueeze(1).to_broadcast([P, TPB, NE]), ALU.add), mm)
                bank.free = [r]
                done = [mm, s1]
                self.row_ready = []
                for c in range(self.k):
                    m = V(lambda e, c=c: e.tensor_tensor(rank_k, rank, pick[c], ALU.mult), r, done)
                    f = V(lambda e: e.tensor_reduce(row_f, rank_k, AX.X, ALU.add), m)
                    w = V(lambda e, c=c: e.tensor_copy(row[b % 2][c], row_f), f, rec_out[b % 2][c].free)
                    done = [mm, s1, w]
                    self.row_ready.append(w)
                    rec_out[b % 2][c].free = []
                chain[0] = done

            def scatter(self, b, tiles, rec_ready, row_ready):
                half = self.halves[b // BPH]
                for j in tiles:
                    for c in range(self.k):
                        rec, at = rec_out[b % 2][c], row[b % 2][c]
                        d = q.dma("gpsimd", f"scatter{b % 2}{c}{j}", lambda e, j=j, rec=rec, at=at: e.indirect_dma_start(
                            half.records, bass.IndirectOffsetOnAxis(at[:, j:j + 1], 0), rec.ap[:, j, :], None),
                            [row_ready[c], rec_ready])
                        rec.free.append(d)
                        half.scattered.append(d)

            def plan(self, h, bank):
                half, nb = self.halves[h], self.nb
                (is_from, is_upto, val), number, first = (m[:, 0:nb] for m in wide), block_no[:, 0:nb], first_f[:, 0:nb]
                fill, table = half.fill, half.table
                spread_e = lambda x: x.unsqueeze(1).to_broadcast([1, nb, NE])
                mm = T(lambda e: e.matmul(bank.ap[:, 0:NE], ones_bf, seen[0], start=True, stop=True),
                       self.seen_set, bank.free)
                c1 = V(lambda e: e.tensor_scalar(count, bank.ap[0:1, 0:NE], float(P - 1), None, ALU.add), mm)
                c2 = V(lambda e: e.tensor_tensor(fill, bank.ap[0:1, 0:NE], choice[0:1, NE:2 * NE], ALU.add), mm)
                bank.free = [c1, c2]
                chain[0] = chain[0] + [mm]
                c3 = V(lambda e: e.tensor_scalar(blocks_i, count, P.bit_length() - 1, None, ALU.logical_shift_right), c1)
                c4 = V(lambda e: e.tensor_copy(blocks_f, blocks_i), c3)
                c5 = V(lambda e: e.tensor_tensor_scan(upto_e, ones_row[:, 0:NE], blocks_f, 0.0, ALU.mult, ALU.add),
                       c4, ones_row_set)
                c6 = V(lambda e: e.tensor_tensor(from_e, upto_e, blocks_f, ALU.subtract), c5)
                c7 = V(lambda e: e.scalar_tensor_tensor(base, from_e, -float(P), choice[0:1, NE:2 * NE], ALU.mult, ALU.add), c6)
                c8 = V(lambda e: e.tensor_tensor(is_upto, spread_e(upto_e), number, ALU.is_le), c5, loaded["block_no"])
                c9 = V(lambda e: e.tensor_tensor(is_from, spread_e(from_e), number, ALU.is_le), c6)
                ca = V(lambda e: e.tensor_tensor(is_from, is_from, is_upto, ALU.subtract), c8, c9)
                cb = V(lambda e: e.scalar_tensor_tensor(val, number, float(P), spread_e(base), ALU.mult, ALU.add), c7)
                cc = V(lambda e: e.scalar_tensor_tensor(val, val, -float(PAD_ROW), is_from, ALU.add, ALU.mult), ca, cb)
                cd = V(lambda e: e.tensor_reduce(first, val, AX.X, ALU.add), cc)
                ce = V(lambda e: e.tensor_scalar(table[:, 0, :], first, float(PAD_ROW), None, ALU.add), cd)
                cf = V(lambda e: e.tensor_tensor(val, is_from, spread_e(choice[0:1, 0:NE]), ALU.mult), cd)
                cg = V(lambda e: e.tensor_reduce(first, val, AX.X, ALU.add), cf, ce)
                ch = V(lambda e: e.tensor_copy(table[:, 1, :], first), cg)
                half.table_ready = [ce, ch]

                def pad(e, i):
                    at = e.value_load(fill[0:1, i:i + 1], min_val=0, max_val=PAD_ROW)
                    return e.dma_start(half.records[bass.ds(at, P), :], pad_rec)

                half.padded = [q.dma("scalar" if i % 4 == 1 else "sync", f"fill{i}", lambda e, i=i: pad(e, i), [c2])
                               for i in range(NE)]

            def blocks(self, h, banks):
                half, k, nb, table = self.halves[h], self.k, self.nb, self.halves[h].table
                xT, h_sb, h_act, y_sb, out_sb, w1_now = work[0:2], work[2:4], work[4:7], work[7:9], work[9:13], work[13:15]
                x_bank, y_bank, h_banks = banks[0], banks[1], banks[2:4]
                w1, w2, b1, b2 = w1_mem, w2_mem, b1_cols[self.n], b2_mem
                got, xt, h_ok, slot_of = {}, {}, {}, {}

                def fetch():
                    while len(got) < nb and not in_use[fetches[0] % IN]:
                        i, slot = len(got), fetches[0] % IN
                        fetches[0] += 1
                        r = slot_of[i] = rec_in[slot]
                        in_use[slot] = True

                        def go(e, i=i, r=r):
                            at = e.value_load(table[0:1, 0, i:i + 1], min_val=0, max_val=PAD_ROW)
                            return e.dma_start(r.ap, half.records[bass.ds(at, P), :])

                        got[i] = q.dma("sync", f"fetch{slot}", go,
                                       [half.table_ready, half.padded, half.scattered, half.pad, r.free])

                def turn(i):
                    r, x = slot_of[i], xT[i % 2]
                    mm = T(lambda e: e.transpose(x_bank.ap[:, 0:P], r.ap[:, 0:D], ident), got[i], x_bank.free)
                    w = S(lambda e: e.copy(x.ap, x_bank.ap[:, 0:P]), mm, x.free)
                    x_bank.free = [w]
                    xt[i] = [w, mm]

                expert_tensor, expert_vector = {}, {}

                def look(i):
                    def entry(e, expert):
                        expert[i] = e.snap(e.value_load(table[0:1, 1, i:i + 1], min_val=0, max_val=NE - 1))

                    T(lambda e: entry(e, expert_tensor), half.table_ready)
                    V(lambda e: entry(e, expert_vector), half.table_ready)

                def bring(i):
                    wn = w1_now[i % 2]
                    wn.ready = V(lambda e: e.tensor_copy(wn.ap, w1[:, bass.ds(expert_vector[i] * FF, FF)]),
                                 wn.free, self.weights_ready)

                def first(i):
                    x, hs, ha, bank, wn = xT[i % 2], h_sb[i % 2], h_act[i % 3], h_banks[i % 2], w1_now[i % 2]
                    by_chunk = lambda m: m.rearrange("p (c t) -> p c t", c=FC)
                    for c in range(FC):
                        mm = T(lambda e, c=c: e.matmul(bank.ap[:, c * P:(c + 1) * P], wn.ap[:, c * P:(c + 1) * P],
                                                       x.ap, start=True, stop=True), xt[i], wn.ready, bank.free)
                    w = V(lambda e: e.tensor_tensor(
                        by_chunk(hs.ap), by_chunk(bank.ap),
                        b1[:, bass.ds(expert_vector[i] * FC, FC)].unsqueeze(2).to_broadcast([P, FC, P]), ALU.add),
                        mm, hs.free, self.weights_ready)
                    x.free = wn.free = [mm]
                    bank.free = [w]
                    h_ok[i] = S(lambda e: e.activation(ha.ap, hs.ap, self.func), w, ha.free)
                    hs.free = [h_ok[i]]

                def second(i):
                    ha, y, o, r = h_act[i % 3], y_sb[i % 2], out_sb[i % 4], slot_of[i]
                    for c in range(FC):
                        mm = T(lambda e, c=c: e.matmul(y_bank.ap[:, 0:D], ha.ap[:, c * P:(c + 1) * P],
                                                       w2[:, bass.ds(expert_tensor[i] * FF + c * P, D)],
                                                       start=(c == 0), stop=(c == FC - 1)), h_ok[i], y_bank.free)
                    w = V(lambda e: e.tensor_tensor(y.ap, y_bank.ap[:, 0:D], b2[:, bass.ds(expert_vector[i] * D, D)], ALU.add),
                          mm, y.free)
                    ha.free = [mm]
                    y_bank.free = [w]
                    g = S(lambda e: e.activation(o.ap, y.ap, ACT.Copy, scale=r.ap[:, D:D + 1]), w, o.free)
                    y.free = [g]
                    d = q.dma("gpsimd", f"send{i % 4}", lambda e: e.indirect_dma_start(
                        half.outs, bass.IndirectOffsetOnAxis(r.ap[:, D + 1:D + 2].bitcast(I32), 0), o.ap, None,
                        bounds_check=k * HTOK - 1, oob_is_err=False), g)
                    o.free = [d]
                    r.free = [d]
                    in_use[rec_in.index(r)] = False
                    half.sent.append(d)
                    half.ended = [mm, w, g]

                def turn_first():
                    fetch()
                    look(0)
                    look(1)
                    bring(0)
                    turn(0)

                def enter(i):
                    if i + 2 < nb:
                        look(i + 2)
                    if i + 1 < nb:
                        bring(i + 1)
                        turn(i + 1)
                    if i < nb:
                        first(i)

                def leave(i):
                    if i >= 2:
                        second(i - 2)
                    fetch()

                steps = [fetch, turn_first]
                for i in range(nb + 2):
                    steps.append(lambda i=i: enter(i))
                    if i >= 2:
                        steps.append(lambda i=i: leave(i))
                return steps

        ln_g, ln_b = load("ln_g", [P, NE]), load("ln_b", [P, NE])
        centroids = load("centroids", [P, NE])
        z1 = [Buffer(sb(f"ffn_z{i}", [P, TPB, D])) for i in range(2)]
        z1T = Buffer(sb("ffn_zT", [P, SEQ]))

        class Experts0(Experts):
            def steps(self, b, bank_of):
                tiles = slice(b * TPB, (b + 1) * TPB)
                zb, rec, half = z1[b % 2], rec_out[b % 2][0], self.halves[b // BPH]
                at = {}

                def norms():
                    at["stats"] = norm_stats(lambda j: x_sb[:, b * TPB + j, :], res_ready[b], twice=True)

                def apply():
                    src = lambda j: x_sb[:, b * TPB + j, :]
                    at["z"] = norm_apply_scalar(at["stats"], lambda j: zb.ap[:, j, :], src, zb.free)
                    at["rec"] = norm_apply(at["stats"], 1, lambda j: rec.ap[:, j, 0:D], src, rec.free)
                    at["rec"].append(V(lambda e: e.tensor_copy(rec.ap[:, :, D + 1].bitcast(I32), token_id[:, 0, at_half(b)]),
                                       loaded["token_id"], rec.free))

                def turn():
                    at["turned"] = transposes(z1T.ap, lambda j: zb.ap[:, j, :], at["z"], z1T.free, bank=bank_of())[1]

                def choose():
                    w, bank = at["turned"], bank_of()
                    mm = [T(lambda e, j=j: e.matmul(bank.ap[:, j * NE:(j + 1) * NE], z1T.ap[:, j * P:(j + 1) * P],
                                                    centroids, start=True, stop=True), w, bank.free, loaded["centroids"])
                          for j in range(TPB)]
                    z1T.free = [mm[-1]]
                    lg = V(lambda e: e.tensor_copy(logits, bank.ap[:, 0:TPB * NE].rearrange("p (t n) -> p t n", t=TPB)),
                           mm[-1], chain[0])
                    bank.free = [lg]
                    tops = self.choose_top(lg)
                    at["exp"] = S(lambda e: e.activation(gate, top[:, :, 0], ACT.Exp, scale=-1.0), tops, gate_free[0])

                def weigh():
                    ex = at["exp"]
                    p1 = V(lambda e: e.tensor_scalar(gate, gate, 1.0, None, ALU.add), ex)
                    gate_free[0] = [V(lambda e: e.reciprocal(rec.ap[:, :, D], gate), p1, rec.free)]
                    at["rec"] += gate_free[0]

                def send():
                    self.pick(b)
                    self.locate(b, bank_of())
                    chain[0] = chain[0] + gate_free[0]
                    self.scatter(b, range(TPB), at["rec"], self.row_ready)
                    xs = x_sb[:, tiles, :]
                    w = G(lambda e: e.tensor_tensor(xs, xs, zb.ap, ALU.add), at["rec"], at["z"])
                    zb.free = [w]
                    half.residual[b] = w

                return [norms, pause, apply, turn, choose, weigh, send]

            def setup(self, x):
                misc = spare_bank()
                w, b1 = w1_mem[:, x * FF:(x + 1) * FF], b1_cols[0][:, x * FC:(x + 1) * FC]
                for c in range(FC):
                    mm = T(lambda e, c=c: e.matmul(misc.ap[:, c:c + 1], w[:, c * P:(c + 1) * P], ln_b[:, x:x + 1],
                                                   start=True, stop=True), misc.free, loaded["w1_0"], loaded["ln_b"])
                v = V(lambda e: e.tensor_tensor(b1, misc.ap[:, 0:FC], b1, ALU.add), mm, loaded["b1_0"])
                misc.free = [v]
                g = G(lambda e: e.tensor_scalar(w, w, ln_g[:, x:x + 1], None, ALU.mult), mm, loaded["ln_g"])
                self.weights_ready += [v, g]

        at_half = lambda b: slice(b % BPH * TPB, (b % BPH + 1) * TPB)
        gate_free = [[]]
        experts0 = Experts0(0, 1, ACT.Relu)

        step_stats(0)
        step_norm(0)
        step_zT(0)
        step_k(0)
        absorb(0)
        step_q(0)
        absorb(4)
        step_u(0, 0)
        before_set = V(lambda e: e.tensor_tensor(before, upto, ident, ALU.subtract), loaded["upto"], loaded["ident"])
        ones_bf_set = V(lambda e: e.memset(ones_bf, 1.0))
        bias_hi, bias_rows, ones_2 = sb("bias_hi", [2, 4 * D], F32R), sb("bias_rows", [2, 4 * D], F32R), sb("ones_2", [2, P], F32R)
        w = V(lambda e: e.tensor_copy(bias_hi, bias_full), loaded["bias_full"])
        bias_ready = [V(lambda e: e.scalar_tensor_tensor(bias_rows, bias_hi.bitcast(F32), lo_row2, bias_full,
                                                         ALU.mult, ALU.add), w, loaded["lo_row2"]),
                      V(lambda e: e.tensor_copy(ones_2, ones_dc[0:2, 0:1].to_broadcast([2, P])), ones_dc_set)]
        ahead = {0: [lambda: step_stats(1)], 1: [lambda: step_norm(1)], 3: [lambda: step_zT(1)], 4: [lambda: step_k(1)],
                 5: [lambda: step_q(1)], 6: [lambda: step_ckv(1)]}
        for h in range(HEADS):
            if h + 1 < HEADS:
                begin_u(0, h + 1)
            step_scores(0, h, range(TPB))
            if h + 1 < HEADS:
                end_u(0, h + 1)
            if h == 0:
                step_ckv(0)
            if h == 2:
                wvo_ready = absorb_values()
                load("w1_0", None, place=w1_mem, after=[wvo_ready, m_ready])
            for step in ahead.get(h, []):
                step()
        step_split(0)
        step_u(1, 0)
        step_shift(0)

        def group_steps(b, g):
            return [(b, g, j, part) for j in range(TPB) for part in range(2)]

        values = []
        later = []

        def next_of(steps, n=1):
            for _ in range(min(n, len(steps))):
                steps.pop(0)()

        def next_values(n=1):
            for _ in range(min(n, len(values))):
                step_values(*values.pop(0))

        def after_attention(b):
            steps = [pause, pause, lambda: step_out(b)] + experts0.steps(b, spare_bank)
            if b == BATCH - 1:
                steps.append(lambda: experts0.plan(b // BPH, spare_bank()))
            return steps

        for b in range(BATCH - 1):
            step_residual_bias(b, wvo_ready)
            two_ahead = b + 2 < BATCH
            scores = [(b + 1, h, (j,)) for h in range(HEADS) for j in range(TPB)]
            for h in range(HEADS):
                if h + 1 < HEADS:
                    begin_u(b + 1, h + 1)
                for j in range(TPB):
                    step_exp(b, h, (j,))
                    for _ in range(1 if h < 6 else 2):
                        if scores and scores[0][0:2] in u_ready:
                            step_scores(*scores.pop(0))
                    if j % 2 == 0:
                        next_values()
                    if j == 1 and h + 1 < HEADS:
                        end_u(b + 1, h + 1)
                    if j % 2 == 1:
                        next_of(later)
                if two_ahead and h in (1, 2, 4, 5, 6, 7):
                    {1: step_stats, 2: step_norm, 4: step_zT, 5: step_k, 6: step_q, 7: step_ckv}[h](b + 2)
                if b > 0 and h % 2 == 1:
                    experts0.setup((b - 1) * TPB + h // 2)
                if b > 0 and h == QUAD - 1:
                    later += after_attention(b - 1)
                if h == QUAD - 1:
                    values += group_steps(b, 0)
            values += group_steps(b, 1)
            step_split(b + 1)
            if two_ahead:
                step_u(b + 2, 0)
            next_values(1)
            step_shift(b + 1)
            next_values(2)
        b = BATCH - 1
        step_residual_bias(b, wvo_ready)
        later.append(lambda: experts0.plan(0, spare_bank()))
        for g in range(HEADS // QUAD):
            for j in range(TPB):
                for r in range(QUAD):
                    step_exp(b, g * QUAD + r, (j,))
                    if r % 2 == 1:
                        next_values()
                        next_of(later)
                if (g, j) == (0, TPB - 1):
                    later += after_attention(b - 1)
                values += [(b, g, j, part) for part in range(2)]
        for v in values:
            step_values(*v)
        spread("b2_0", NE * D, place=b2_mem, after=prob[0].free)
        experts0.weights_ready += [loaded["w2_0"], loaded["b2_0"]]
        for m in rec_in:
            m.free = [prob[0].free, prob[1].free]
        for m in work:
            m.free = [p.free for p in prob]
        block_banks = score_banks + [second_misc, shift_banks[0]]
        spares[1] = shift_banks[1]
        as_rows = lambda m: m.rearrange("p (t d) -> p t d", t=TPB)
        collect_bufs = [Buffer(as_rows(m)) for m in carve(collect_mem, 2 * [TPB * D])]
        for m in collect_bufs:
            m.free = wvo_ready
        collect_turn = [0]

        def interleave(a, b, per):
            for step in a:
                step()
                for _ in range(min(per, len(b))):
                    b.pop(0)()

        def drain(steps):
            while steps:
                steps.pop(0)()

        collected = {}

        def collect(ex, b):
            half = ex.halves[b // BPH]
            for c in range(ex.k):
                i = collect_turn[0] % len(collect_bufs)
                collect_turn[0] += 1
                y = collect_bufs[i]
                at = c * HTOK + (b % BPH) * SEQ
                d = q.dma("sync", f"collect{i}", lambda e, y=y, at=at: e.dma_start(
                    y.ap, half.outs[at:at + SEQ, :].rearrange("(t p) d -> p t d", p=P)), [half.sent, y.free])
                collected.setdefault((ex.n, b), []).append((y, d))

        def add_collected(ex, b, ready):
            xs = x_sb[:, b * TPB:(b + 1) * TPB, :]
            for y, d in collected[ex.n, b]:
                ready = [V(lambda e, y=y: e.tensor_tensor(xs, xs, y.ap, ALU.add), d, ready)]
                y.free = ready
            return ready

        blocks = experts0.blocks(0, block_banks)
        tail = later + after_attention(BATCH - 1)
        interleave(tail, blocks, TAIL)
        next_blocks = experts0.blocks(1, block_banks)
        next_of(next_blocks)
        drain(blocks)
        freed = [p.free for p in prob] + [oT_ready[BATCH - 1, 0], oT_ready[BATCH - 1, 1], mt_free[0], q_free[0]]

        def reuse(m):
            x = Buffer(m)
            x.free = list(freed)
            return x

        KVW = LH * LE * LD
        e_ = carve(l1_mem, [KVW] * 3 + [2 * D] * 5 + [D] * 2 + 3 * [LH * LE] + 2 * [P] + 2 * [LH * LE])
        kv_buf, prod_buf = [reuse(m) for m in e_[0:2]], [reuse(m) for m in carve(e_[2], 2 * [KVW // 2])]
        exp_buf, pos_buf, qk_buf = reuse(e_[3]), reuse(e_[4]), [reuse(m) for m in e_[5:8]]
        o_buf, oT_buf = reuse(e_[8]), reuse(e_[9])
        v_buf, qT_buf, sum_buf = ([reuse(m) for m in e_[i:j]] for i, j in ((10, 13), (13, 15), (15, 17)))
        state_buf = [reuse(m) for region in (q_full, den_t) for m in carve(region, 3 * [LH * LE])]
        norm_buf, inv_buf = (reuse(m) for m in carve(inv_den, 2 * [LH]))
        heads_of = lambda m, n: m.rearrange("p (h c) -> p h c", c=n)
        v_one = [V(lambda e, v=v: e.memset(heads_of(v.ap, LE)[:, :, LD:LE], 1.0), v.free) for v in v_buf]
        qkv_bank, state_bank, sum_banks = shift_banks[1], num_bank, [den_bank, misc]
        turn_bank = qkv_bank

        def alone():
            return not blocks or wait > 0

        def shared_or(own):
            return own if alone() else state_bank
        l1_ready, l1z, l1zT, part, products, reduced, state_ready, l1_done, l1_stats = {}, {}, {}, {}, {}, {}, {}, {}, {}

        def l1_take(b):
            l1_ready[b] = add_collected(experts0, b, experts0.halves[b // BPH].residual[b])
            l1_stats[b] = norm_stats(lambda j: x_sb[:, b * TPB + j, :], l1_ready[b])

        l1_pieces = {}

        def l1_norm(b, j):
            zb = z[b % 2]
            if j == 0:
                l1_pieces[b], l1z[b] = norm_pieces(l1_stats[b], lambda j: zb.ap[:, j, :], lambda j: x_sb[:, b * TPB + j, :],
                                                   list(zb.free))
            l1_pieces[b][j]()

        def l1_turn(b):
            zb, zt = z[b % 2], zT[b % 2]
            t, l1zT[b] = transposes(zt.ap, lambda j: zb.ap[:, j, :], l1z[b], zt.free, bank=turn_bank)
            zb.free = [t]

        def l1_project(t):
            b, c = divmod(t, TPB)
            zt, v = zT[b % 2], v_buf[t % 3]
            T(lambda e: e.matmul(qkv_bank.ap[:, 0:3 * D], ones_2, bias_rows[:, 0:3 * D], start=True, stop=False),
              qkv_bank.free, bias_ready)
            mm = T(lambda e: e.matmul(qkv_bank.ap[:, 0:3 * D], zt.ap[:, c * P:(c + 1) * P], wqkv, start=False, stop=True),
                   l1zT[b], loaded["wqkv"])
            zt.free = [mm]
            ex = S(lambda e: e.activation(exp_buf.ap, qkv_bank.ap[:, 0:2 * D], ACT.Exp), mm, exp_buf.free)
            pos = S(lambda e: e.activation(pos_buf.ap, qkv_bank.ap[:, 0:2 * D], ACT.Relu), mm, pos_buf.free)
            vc = S(lambda e: e.copy(heads_of(v.ap, LE)[:, :, 0:LD], heads_of(qkv_bank.ap[:, 2 * D:3 * D], LD)), mm, v.free)
            qkv_bank.free = [ex, pos, vc]
            part[t] = [ex, pos, vc]

        def l1_features(t):
            qk, v, kv = qk_buf[t % 3], v_buf[t % 3], kv_buf[t % 2]
            ex, pos, vc = part[t]
            f = V(lambda e: e.scalar_tensor_tensor(qk.ap, exp_buf.ap, 1.0, pos_buf.ap, ALU.min, ALU.add), ex, pos, qk.free)
            exp_buf.free = pos_buf.free = [f]
            kh, vh = heads_of(qk.ap[:, D:2 * D], LD), heads_of(v.ap, LE)
            o = G(lambda e: e.tensor_tensor(kv.ap.rearrange("p (h c d) -> p h c d", h=LH, c=LE),
                                            kh.unsqueeze(2).to_broadcast([P, LH, LE, LD]),
                                            vh.unsqueeze(3).to_broadcast([P, LH, LE, LD]), ALU.mult), f, vc, v_one, kv.free)
            part[t] = [f, vc, o]

        def l1_states(t):
            b, c = divmod(t, TPB)
            f, vc, o = part[t]
            qk, v, qT, users = qk_buf[t % 3], v_buf[t % 3], qT_buf[t % 2], []
            new = state_buf[t % len(state_buf)]
            if c > 0:
                m = T(lambda e: e.transpose(state_bank.ap[:, 0:P], qk.ap[:, 0:D], ident), f, state_bank.free)
                qt = S(lambda e: e.copy(qT.ap, state_bank.ap[:, 0:P]), m, qT.free)
                state_bank.free = [qt]
                part[t].append(qt)
                users.append(m)
            if c < TPB - 1:
                ms = T(lambda e: e.matmul(state_bank.ap[:, 0:LH * LE], qk.ap[:, D:2 * D], v.ap,
                                          start=True, stop=True), f, vc, v_one, state_bank.free)
                users.append(ms)
                m = V(lambda e: e.tensor_tensor(new.ap, state_bank.ap[:, 0:LH * LE], head_mask, ALU.mult), ms, new.free,
                      loaded["head_mask"])
                state_bank.free = [m]
                state_ready[t] = m
            qk.free = users
            v.free = [o] + users

        def l1_sums(t, g):
            f, vc, o = part[t][0:3]
            qk, kv = qk_buf[t % 3], kv_buf[t % 2]
            banks = sum_banks + (block_banks[2:4] if alone() else [])
            bank = banks[(t * (LH // GRP) + g) % len(banks)]
            mm = T(lambda e: e.matmul(bank.ap[:, 0:GW], upto, kv.ap[:, g * GW:(g + 1) * GW], start=True, stop=True),
                   o, bank.free, loaded["upto"])
            qh = heads_of(qk.ap[:, g * GRP * LD:(g + 1) * GRP * LD], LD)
            pair, at = prod_buf[g // 2], g % 2 * GW
            w = V(lambda e: e.tensor_tensor(
                pair.ap[:, at:at + GW].rearrange("p (h c d) -> p h c d", h=GRP, c=LE),
                bank.ap[:, 0:GW].rearrange("p (h c d) -> p h c d", h=GRP, c=LE),
                qh.unsqueeze(2).to_broadcast([P, GRP, LE, LD]), ALU.mult), mm, pair.free)
            bank.free = [w]
            products.setdefault(t, []).append(w)
            if g == LH // GRP - 1:
                kv.free = [mm]
                qk.free = qk.free + [w]

        def l1_reduce(t, i):
            pair, total = prod_buf[i], sum_buf[t % 2]
            n = LH * LE // 2
            red = V(lambda e: e.tensor_reduce(total.ap[:, i * n:(i + 1) * n], pair.ap.rearrange("p (c d) -> p c d", d=LD),
                                              AX.X, ALU.add), products[t][-2:], total.free)
            pair.free = [red]
            reduced.setdefault(t, []).append(red)

        def l1_totals(t):
            b, c = divmod(t, TPB)
            inter_bank = shared_or(block_banks[0])
            qT, total = qT_buf[t % 2], sum_buf[t % 2]
            red = reduced[t]
            if c > 0:
                for i in range(t - c, t):
                    old = state_buf[i % len(state_buf)]
                    mi = T(lambda e, i=i, old=old: e.matmul(inter_bank.ap[:, 0:LH * LE], qT.ap, old.ap,
                                                            start=(i == t - c), stop=(i == t - 1)),
                           part[t][3], state_ready[i], inter_bank.free)
                    old.free = [mi]
                qT.free = [mi]
                red = V(lambda e: e.tensor_tensor(total.ap, total.ap, inter_bank.ap[:, 0:LH * LE], ALU.add), mi, red)
                inter_bank.free = [red]
            th = heads_of(total.ap, LE)
            n = V(lambda e: e.tensor_scalar(norm_buf.ap, th[:, :, LD], LEPS, None, ALU.add), red)
            r = V(lambda e: e.reciprocal(inv_buf.ap, norm_buf.ap), n)
            o = V(lambda e: e.tensor_tensor(heads_of(o_buf.ap, LD), th[:, :, 0:LD],
                                            inv_buf.ap.unsqueeze(2).to_broadcast([P, LH, LD]), ALU.mult), r, o_buf.free)
            total.free = [o]
            part[t] = o

        def l1_turn_output(t):
            out_bank = shared_or(block_banks[1])
            mt = T(lambda e: e.transpose(out_bank.ap[:, 0:P], o_buf.ap, ident), part[t], out_bank.free)
            o_buf.free = [mt]
            part[t] = S(lambda e: e.copy(oT_buf.ap, out_bank.ap[:, 0:P]), mt, oT_buf.free)
            out_bank.free = [part[t]]

        def l1_output(t):
            out_bank = shared_or(block_banks[1])
            T(lambda e: e.matmul(out_bank.ap[:, P:2 * P], ones_2, bias_rows[:, 3 * D:4 * D], start=True, stop=False),
              out_bank.free, bias_ready)
            mm = T(lambda e: e.matmul(out_bank.ap[:, P:2 * P], oT_buf.ap, wout, start=False, stop=True), part[t], loaded["wout"])
            oT_buf.free = [mm]
            xt = x_sb[:, t, :]
            x = V(lambda e: e.tensor_tensor(xt, xt, out_bank.ap[:, P:2 * P], ALU.add), mm, l1z[t // TPB])
            out_bank.free = [x]
            l1_done.setdefault(t // TPB, []).append(x)

        class Experts1(Experts):
            def steps(self, b, bank_of):
                r0, r1 = rec_out[b % 2]
                at = {}

                def norms():
                    at["stats"] = norm_stats(lambda j: x_sb[:, b * TPB + j, :], l1_done[b])

                def apply(j):
                    if j == 0:
                        at["pieces"], at["rows"] = norm_pieces(at["stats"], lambda j: r0.ap[:, j, 0:D],
                                                               lambda j: x_sb[:, b * TPB + j, :], list(r0.free))
                    at["pieces"][j]()

                def second_record():
                    at["rec"] = [at["rows"], S(lambda e: e.copy(r1.ap[:, :, 0:D], r0.ap[:, :, 0:D]), at["rows"], r1.free)]
                    at["rec"] += [V(lambda e, c=c, r=r: e.tensor_copy(r.ap[:, :, D + 1].bitcast(I32), token_id[:, c, at_half(b)]),
                                    loaded["token_id"], r.free) for c, r in ((0, r0), (1, r1))]

                row_of = lambda m: m.unsqueeze(2).to_broadcast([P, TPB, NE])

                def turn():
                    at["turned"] = transposes(z1T.ap, lambda j: r0.ap[:, j, 0:D], at["rows"], z1T.free, bank=bank_of())[1]

                def choose():
                    w, bank = at["turned"], bank_of()
                    mm = [T(lambda e, j=j: e.matmul(bank.ap[:, j * NE:(j + 1) * NE], z1T.ap[:, j * P:(j + 1) * P],
                                                    wg, start=True, stop=True), w, bank.free, loaded["wg"])
                          for j in range(TPB)]
                    z1T.free = [mm[-1]]
                    lg3 = bank.ap[:, 0:TPB * NE].rearrange("p (t n) -> p t n", t=TPB)
                    m = V(lambda e: e.tensor_reduce(gate, lg3, AX.X, ALU.max), mm[-1], gate_free[0])
                    d = V(lambda e: e.tensor_tensor(logits, lg3, row_of(gate), ALU.subtract), m, chain[0])
                    bank.free = [d]
                    at["exp"] = [S(lambda e: e.activation(logits, logits, ACT.Exp), d), d]

                def top_two():
                    u = V(lambda e: e.tensor_reduce(gate, logits, AX.X, ALU.add), at["exp"])
                    i_ = V(lambda e: e.reciprocal(gate, gate), u)
                    p_ = V(lambda e: e.tensor_tensor(logits, logits, row_of(gate), ALU.mult), i_)
                    gate_free[0] = [p_]
                    tops = self.choose_top(p_)
                    w = [V(lambda e, c=c, r=r: e.tensor_copy(r.ap[:, :, D], top[:, :, c]), tops, r.free)
                         for c, r in ((0, r0), (1, r1))]
                    at["rec"] += w
                    at["top_users"] = w

                def pick():
                    self.pick(b)

                def locate():
                    self.locate(b, bank_of())
                    chain[0] = chain[0] + at["top_users"]
                    at["rows_at"] = self.row_ready

                send = [lambda j=j: self.scatter(b, (j,), at["rec"], at["rows_at"]) for j in range(TPB)]
                normed = [lambda j=j: apply(j) for j in range(TPB)]
                return [norms, pause, *normed, turn, second_record, choose, pause, top_two, pick, locate] + send

        experts1 = Experts1(1, 2, ACT.Gelu_apprx_tanh)

        later = []

        def l1_steps(t):
            now, sums, leaves = t < NT, 1 <= t <= NT, t >= 2
            steps = [(now, lambda: l1_features(t)), (sums, lambda: l1_states(t - 1)),
                     (sums, lambda: l1_sums(t - 1, 0)), (sums, lambda: l1_sums(t - 1, 1)),
                     (leaves, lambda: l1_turn_output(t - 2)),
                     (sums, lambda: l1_reduce(t - 1, 0)),
                     (sums, lambda: l1_sums(t - 1, 2)), (sums, lambda: l1_sums(t - 1, 3)),
                     (t + 1 < NT, lambda: l1_project(t + 1)),
                     (leaves, lambda: l1_output(t - 2)),
                     (sums, lambda: l1_reduce(t - 1, 1)), (sums, lambda: l1_totals(t - 1))]
            steps = [step for there, step in steps if there]
            return steps

        LAST = 11
        prepare = {}
        for b, when in ((1, ((0, LAST), (1, 1), (1, 3), (1, 5), (1, 7), (2, 2))),
                        (2, ((6, 4), (6, 6), (6, 8), (6, 10), (7, 0), (7, 4))),
                        (3, ((8, LAST), (9, 2), (9, 5), (9, 8), (9, LAST), (10, 4)))):
            norm = [lambda b=b, j=j: l1_norm(b, j) for j in range(TPB)]
            for at, step in zip(when, [lambda b=b: l1_take(b)] + norm + [lambda b=b: l1_turn(b)]):
                prepare[at] = step

        def take_weights():
            ended = experts0.halves[1].ended
            for name, place in (("w1_1", w1_mem), ("w2_1", w2_mem)):
                load(name, None, place=place, after=ended)
            spread("b2_1", NE * D, place=b2_mem, after=ended)
            experts1.weights_ready = [loaded[n] for n in ("w1_1", "w2_1", "b1_1", "b2_1")]

        blocks = next_blocks
        collect(experts0, 0)
        collect(experts0, 1)
        wait = 0
        next_of(blocks, 8)
        interleave([lambda: l1_take(0), lambda: [l1_norm(0, j) for j in range(TPB)], lambda: l1_turn(0), lambda: l1_project(0)], blocks, 3)
        layer1_begun = False
        for t in range(NT + 2):
            if t == 6:
                drain(blocks)
                collect(experts0, 2)
                collect(experts0, 3)
                take_weights()
            steps = l1_steps(t)
            for n, step in enumerate(steps):
                step()
                n = LAST if n == len(steps) - 1 else n
                if (t, n) in prepare:
                    prepare[t, n]()
                if wait:
                    wait -= 1
                elif n % 4 < BLOCKS_BESIDE[layer1_begun]:
                    next_of(blocks)
                if n % 2 == 1:
                    next_of(later)
                    if t > BPH * TPB + 1 and not later and not layer1_begun:
                        layer1_begun, wait = True, RECORDS_LAND
                        blocks = experts1.blocks(0, block_banks)
                        next_of(blocks)
            if t >= 2 and (t - 2) % TPB == TPB - 1:
                b = (t - 2) // TPB
                later.extend(experts1.steps(b, lambda: qkv_bank))
                if b % BPH == BPH - 1:
                    later.append(lambda h=b // BPH: experts1.plan(h, qkv_bank))
        interleave(later, blocks, 1)
        drain(blocks)

        out_rows = out.rearrange("b (t p) d -> p (b t) d", p=P)

        def leave(b):
            sl = slice(b * TPB, (b + 1) * TPB)
            w = add_collected(experts1, b, l1_done[b])
            q.dma("sync", f"out{b}", lambda e: e.dma_start(out_rows[:, sl, :], x_sb[:, sl, :]), w)

        blocks = experts1.blocks(1, block_banks)
        next_of(blocks)
        for b in range(BPH):
            collect(experts1, b)
            next_of(blocks, 26)
            leave(b)
        drain(blocks)
        collect_bufs += [Buffer(as_rows(m)) for m in carve(w2_mem, 2 * [TPB * D])]
        for m in collect_bufs[2:]:
            m.free = experts1.halves[1].ended
        for b in range(BPH, BATCH):
            collect(experts1, b)
        for b in range(BPH, BATCH):
            leave(b)
        q.emit(ctx.enter_context(nc.Block()))


def lay_out(i):
    r = {k: np.asarray(v) for k, v in i.items()}
    f = lambda name: r[name]
    z = lambda *s: np.zeros(s, np.float32)
    o = {"x": f("L0_attn_h_t").reshape(TOK, D)}
    o["ident"] = np.eye(P, dtype=np.float32)
    wdq, bdq = f("L0_attn_W_DQ"), f("L0_attn_b_DQ")
    o["wq"] = np.concatenate([wdq, wdq, wdq, z(D, P - 3 * DC)], 1)
    o["bq"] = np.concatenate([bdq, bdq, bdq, np.ones(2, np.float32), z(P - 3 * DC - 2)])[:, None]
    o["wk"] = np.concatenate([f("L0_attn_W_DKV"), f("L0_attn_W_KR"), z(D, 1)], 1)
    o["bk"] = np.concatenate([f("L0_attn_b_DKV"), f("L0_attn_b_KR"), np.ones(1, np.float32)])[:, None]
    o["bkv"] = f("L0_attn_b_DKV")[None]
    lo = z(P, 2)
    lo[2 * DC:3 * DC, 0] = -1.0
    lo[DC:2 * DC, 1] = -1.0
    lo[ROW_ONE + 1, 1] = -1.0
    o["lo_rows"] = lo
    per_head = lambda w: w.reshape(w.shape[0], HEADS, -1)
    uk, uq, uv = (per_head(f(f"L0_attn_W_{n}")) for n in ("UK", "UQ", "UV"))
    qr = per_head(f("L0_attn_W_QR"))
    buk, buq, buv, bqr = (f(f"L0_attn_b_{n}").reshape(HEADS, -1) for n in ("UK", "UQ", "UV", "QR"))
    o["mk"] = np.concatenate([uk.transpose(2, 1, 0), z(DK, HEADS, DR), buk.T[:, :, None]], 2)
    t = uq.transpose(2, 1, 0)
    o["mq"] = np.concatenate([t, t, t, buq.T[:, :, None], buq.T[:, :, None], z(DK, HEADS, P - ROW_MHI)], 2)
    rk = z(DR + 1, KSIDE)
    rk[0:DR, DC:DC + DR] = np.eye(DR)
    rk[DR, KSIDE - 1] = 1.0
    o["rk"] = rk
    t = qr.transpose(2, 1, 0)
    sel = z(1, HEADS, P)
    for h in range(HEADS):
        sel[0, h, ROW_MHI + h] = sel[0, h, ROW_MLO + h] = 1.0
    o["rq"] = np.concatenate([np.concatenate([t, t, t, bqr.T[:, :, None], bqr.T[:, :, None],
                                              z(DR, HEADS, P - ROW_MHI)], 2), sel], 0)
    o["wuv"] = uv.transpose(2, 1, 0)
    o["buv"] = buv.T
    o["wo"] = f("L0_attn_W_O").reshape(HEADS, DK, D).transpose(1, 0, 2)
    o["bo"] = f("L0_attn_b_O")[None]
    i = np.arange(P)
    o["upto"] = (i[:, None] <= i[None, :]).astype(np.float32)
    o["choice"] = np.tile(np.concatenate([np.arange(NE), np.arange(NE) * REGION]).astype(np.float32), (P, 1))
    o["token_id"] = (np.arange(2)[None, :, None] * HTOK + np.arange(HTOK // P)[None, None, :] * P + i[:, None, None]).astype(np.int32)
    pad = z(P, REC)
    pad[:, D + 1:D + 2] = np.full((P, 1), SKIP, np.int32).view(np.float32)
    o["pad_rec"] = pad
    o["block_no"] = np.tile(np.arange(n_blocks(2), dtype=np.float32)[:, None], (1, NE))[None]
    o["centroids"] = f("L0_ffn_centroids").T
    o["ln_g"], o["ln_b"] = f("L0_ffn_ln_g").T, f("L0_ffn_ln_b").T
    o["w1_0"] = f("L0_ffn_w1").transpose(2, 0, 1).reshape(D, NE * FF)
    o["w2_0"] = f("L0_ffn_w2").transpose(2, 0, 1).reshape(FC, P, NE, D).transpose(1, 2, 0, 3).reshape(P, NE * FF)
    columns = lambda b: b.reshape(NE, FC, P).transpose(2, 0, 1).reshape(P, NE * FC)
    o["b1_0"], o["b2_0"] = columns(f("L0_ffn_b1")), f("L0_ffn_b2").reshape(1, -1)
    o["wqkv"], o["wout"] = f("L1_attn_w_qkv").T, f("L1_attn_w_out").T
    o["bias_full"] = np.tile(np.concatenate([f("L1_attn_b_qkv"), f("L1_attn_b_out")]), (2, 1))
    o["lo_row2"] = np.array([[0.0], [-1.0]], np.float32)
    o["head_mask"] = (i[:, None] // LD == np.arange(LH * LE)[None, :] // LE).astype(np.float32)
    o["wg"] = f("L1_ffn_Wg")
    o["w1_1"] = f("L1_ffn_W1").transpose(1, 0, 2).reshape(D, NE * FF)
    o["w2_1"] = f("L1_ffn_W2").reshape(NE, FC, P, D).transpose(2, 0, 1, 3).reshape(P, NE * FF)
    o["b1_1"], o["b2_1"] = columns(f("L1_ffn_b1")), f("L1_ffn_b2").reshape(1, -1)
    return {k: np.ascontiguousarray(v) for k, v in o.items()}


def kernel(**inputs):
    import concourse.bacc as bacc
    from concourse.bass_utils import run_bass_kernel_spmd

    nc = bacc.Bacc("TRN2", target_bir_lowering=False, num_devices=1)
    arrays = lay_out(inputs)
    aps = {k: nc.dram_tensor(f"in_{k}", v.shape, mybir.dt.from_np(v.dtype), kind="ExternalInput").ap()
           for k, v in arrays.items()}
    out = nc.dram_tensor("out_0", (BATCH, SEQ, D), F32, kind="ExternalOutput").ap()
    build(nc, aps, out)
    r = run_bass_kernel_spmd(nc, [{f"in_{k}": v for k, v in arrays.items()}], core_ids=[0])
    return r.results[0]["out_0"]
```
